# Optimizing a Trainium2 kernel written in Bass

```python
import numpy as np
import jax
import jax.numpy as jnp

def _softmax(x, axis=-1):
    return jax.nn.softmax(x, axis=axis)

def _gelu(x):
    return jax.nn.gelu(x, approximate=True)

def _silu(x):
    return jax.nn.silu(x)

def _sigmoid(x):
    return jax.nn.sigmoid(x)

def _layernorm(x, axis=-1, eps=1e-05):
    m = jnp.mean(x, axis=axis, keepdims=True)
    v = jnp.var(x, axis=axis, keepdims=True)
    return (x - m) / jnp.sqrt(v + eps)

def _scatter_add(tgt, idx, src, axis=0):
    return tgt.at[idx].add(src)

def _segment_sum(src, seg, n):
    return jax.ops.segment_sum(src, seg, n)
kernel_name = 'mk_seq_preln_d1_jaxref_r8_515cb0'

def setup_inputs(seed: int=0):
    np.random.seed(seed)
    _w = jnp.asarray

    def _L0_attn_setup():
        import jax, jax.numpy as jnp
        import numpy as np
        N_EMBD = 256
        N_QHEAD = 16
        N_KVHEAD = 4
        GROUP = N_QHEAD // N_KVHEAD
        HEAD_D = N_EMBD // N_QHEAD
        KV_DIM = N_EMBD // GROUP
        B, T = (2, 256)
        ROPE_BASE = 10000.0

        def _apply_rope(u):
            d = u.shape[-1]
            t = u.shape[2]
            i = jnp.arange(1, d // 2 + 1, dtype=jnp.float32)
            thetas = ROPE_BASE ** (-2.0 * (i - 1.0) / d)
            ang = jnp.arange(1, t + 1, dtype=jnp.float32)[:, None] * thetas
            cos = jnp.concatenate([jnp.cos(ang), jnp.cos(ang)], axis=1)
            sin = jnp.concatenate([jnp.sin(ang), jnp.sin(ang)], axis=1)
            left, right = (u[..., :d // 2], u[..., d // 2:])
            rot = jnp.concatenate([-right, left], axis=-1)
            return u * cos + rot * sin
        key = jax.random.key(seed)
        ks = jax.random.split(key, 9)
        s_in = 1.0 / np.sqrt(N_EMBD)
        return {'x': jax.random.normal(ks[0], (B, T, N_EMBD), dtype=jnp.float32), 'Wq': jax.random.uniform(ks[1], (N_EMBD, N_EMBD), jnp.float32, -s_in, s_in), 'bq': jax.random.uniform(ks[2], (N_EMBD,), jnp.float32, -s_in, s_in), 'Wk': jax.random.uniform(ks[3], (KV_DIM, N_EMBD), jnp.float32, -s_in, s_in), 'bk': jax.random.uniform(ks[4], (KV_DIM,), jnp.float32, -s_in, s_in), 'Wv': jax.random.uniform(ks[5], (KV_DIM, N_EMBD), jnp.float32, -s_in, s_in), 'bv': jax.random.uniform(ks[6], (KV_DIM,), jnp.float32, -s_in, s_in), 'Wo': jax.random.uniform(ks[7], (N_EMBD, N_EMBD), jnp.float32, -s_in, s_in), 'bo': jax.random.uniform(ks[8], (N_EMBD,), jnp.float32, -s_in, s_in)}
    _L0_attn_in = _L0_attn_setup()

    def _L0_ffn_setup():
        import jax, jax.numpy as jnp
        import numpy as np
        H = 256
        E = 64
        I = 64
        SI = 64
        TOP_K = 8
        B, T = (2, 64)
        key = jax.random.key(seed)
        ks = jax.random.split(key, 8)
        s = 0.02
        return {'h': jax.random.normal(ks[0], (B, T, H), jnp.float32), 'gate_w': jax.random.normal(ks[1], (E, H), jnp.float32) * s, 'gu_w': jax.random.normal(ks[2], (E, 2 * I, H), jnp.float32) * s, 'dp_w': jax.random.normal(ks[3], (E, H, I), jnp.float32) * s, 'sh_gate_w': jax.random.normal(ks[4], (SI, H), jnp.float32) * s, 'sh_up_w': jax.random.normal(ks[5], (SI, H), jnp.float32) * s, 'sh_down_w': jax.random.normal(ks[6], (H, SI), jnp.float32) * s, 'sh_gate1_w': jax.random.normal(ks[7], (1, H), jnp.float32) * s}
    _L0_ffn_in = _L0_ffn_setup()
    _d = {'L0_attn_x': _L0_attn_in['x'], 'L0_attn_Wq': _L0_attn_in['Wq'], 'L0_attn_bq': _L0_attn_in['bq'], 'L0_attn_Wk': _L0_attn_in['Wk'], 'L0_attn_bk': _L0_attn_in['bk'], 'L0_attn_Wv': _L0_attn_in['Wv'], 'L0_attn_bv': _L0_attn_in['bv'], 'L0_attn_Wo': _L0_attn_in['Wo'], 'L0_attn_bo': _L0_attn_in['bo'], 'L0_ffn_gate_w': _L0_ffn_in['gate_w'], 'L0_ffn_gu_w': _L0_ffn_in['gu_w'], 'L0_ffn_dp_w': _L0_ffn_in['dp_w'], 'L0_ffn_sh_gate_w': _L0_ffn_in['sh_gate_w'], 'L0_ffn_sh_up_w': _L0_ffn_in['sh_up_w'], 'L0_ffn_sh_down_w': _L0_ffn_in['sh_down_w'], 'L0_ffn_sh_gate1_w': _L0_ffn_in['sh_gate1_w']}
    _x0 = _d['L0_attn_x']
    _d['L0_attn_x'] = jax.random.normal(jax.random.fold_in(jax.random.key(seed), 1), (8, 512, 256), dtype=_x0.dtype)
    del _x0
    return _d

def reference(L0_attn_x, L0_attn_Wq, L0_attn_bq, L0_attn_Wk, L0_attn_bk, L0_attn_Wv, L0_attn_bv, L0_attn_Wo, L0_attn_bo, L0_ffn_gate_w, L0_ffn_gu_w, L0_ffn_dp_w, L0_ffn_sh_gate_w, L0_ffn_sh_up_w, L0_ffn_sh_down_w, L0_ffn_sh_gate1_w):

    def _L0_attn_ref(x, Wq, bq, Wk, bk, Wv, bv, Wo, bo):
        import jax, jax.numpy as jnp
        import numpy as np
        N_EMBD = 256
        N_QHEAD = 16
        N_KVHEAD = 4
        GROUP = N_QHEAD // N_KVHEAD
        HEAD_D = N_EMBD // N_QHEAD
        KV_DIM = N_EMBD // GROUP
        B, T = (2, 256)
        ROPE_BASE = 10000.0

        def _apply_rope(u):
            d = u.shape[-1]
            t = u.shape[2]
            i = jnp.arange(1, d // 2 + 1, dtype=jnp.float32)
            thetas = ROPE_BASE ** (-2.0 * (i - 1.0) / d)
            ang = jnp.arange(1, t + 1, dtype=jnp.float32)[:, None] * thetas
            cos = jnp.concatenate([jnp.cos(ang), jnp.cos(ang)], axis=1)
            sin = jnp.concatenate([jnp.sin(ang), jnp.sin(ang)], axis=1)
            left, right = (u[..., :d // 2], u[..., d // 2:])
            rot = jnp.concatenate([-right, left], axis=-1)
            return u * cos + rot * sin
        b, t, _ = x.shape
        q = x @ Wq.T + bq
        k = x @ Wk.T + bk
        v = x @ Wv.T + bv
        q = q.reshape(b, t, N_QHEAD, HEAD_D).transpose(0, 2, 1, 3)
        k = k.reshape(b, t, N_KVHEAD, HEAD_D).transpose(0, 2, 1, 3)
        v = v.reshape(b, t, N_KVHEAD, HEAD_D).transpose(0, 2, 1, 3)
        q = _apply_rope(q)
        k = _apply_rope(k)
        scale = jnp.sqrt(jnp.asarray(HEAD_D, q.dtype))
        q = q.reshape(b, N_KVHEAD, GROUP, t, HEAD_D)
        att = jnp.einsum('bhgqd,bhkd->bhgqk', q, k) / scale
        causal = jnp.tril(jnp.ones((t, t), dtype=bool))
        att = jnp.where(causal, att, jnp.asarray(-jnp.inf, att.dtype))
        att = jax.nn.softmax(att, axis=-1)
        y = jnp.einsum('bhgqk,bhkd->bhgqd', att, v)
        y = y.transpose(0, 3, 1, 2, 4).reshape(b, t, N_EMBD)
        return y @ Wo.T + bo

    def _L0_ffn_ref(h, gate_w, gu_w, dp_w, sh_gate_w, sh_up_w, sh_down_w, sh_gate1_w):
        import jax, jax.numpy as jnp
        import numpy as np
        H = 256
        E = 64
        I = 64
        SI = 64
        TOP_K = 8
        B, T = (2, 64)
        Bb, Tt, Hh = h.shape
        x = h.reshape(Bb * Tt, Hh)
        N = x.shape[0]
        logits = x @ gate_w.T
        topv, topi = jax.lax.top_k(logits, TOP_K)
        rw = jax.nn.softmax(topv.astype(jnp.float32), axis=-1).astype(x.dtype)
        W = jnp.zeros((N, E), x.dtype).at[jnp.arange(N)[:, None], topi].set(rw)
        gu = jnp.einsum('nh,eih->nei', x, gu_w)
        gate, up = (gu[..., :I], gu[..., I:])
        inter = jax.nn.silu(gate) * up
        inter_w = inter * W[:, :, None]
        out = jnp.einsum('nei,ehi->nh', inter_w, dp_w)
        sh_inter = jax.nn.silu(x @ sh_gate_w.T) * (x @ sh_up_w.T)
        sh_out = sh_inter @ sh_down_w.T
        sh_g = jax.nn.sigmoid(x @ sh_gate1_w.T)
        out = out + sh_g * sh_out
        return out.reshape(Bb, Tt, Hh)
    x = L0_attn_x
    x = x + _L0_attn_ref(_layernorm(x, axis=-1), L0_attn_Wq, L0_attn_bq, L0_attn_Wk, L0_attn_bk, L0_attn_Wv, L0_attn_bv, L0_attn_Wo, L0_attn_bo)
    x = x + _L0_ffn_ref(_layernorm(x, axis=-1), L0_ffn_gate_w, L0_ffn_gu_w, L0_ffn_dp_w, L0_ffn_sh_gate_w, L0_ffn_sh_up_w, L0_ffn_sh_down_w, L0_ffn_sh_gate1_w)
    return x

_drawn_inputs = setup_inputs


def setup_inputs(seed=0):
    import zlib

    import numpy as np

    out = dict(_drawn_inputs(seed))
    spreads = {}
    factors = {'L0_attn_Wq': 4.438,
     'L0_attn_bq': 8.0,
     'L0_attn_Wk': 4.388,
     'L0_attn_bk': 8.0,
     'L0_ffn_gate_w': 8.0,
     'L0_ffn_gu_w': 8.0,
     'L0_ffn_dp_w': 8.0,
     'L0_ffn_sh_gate_w': 8.0,
     'L0_ffn_sh_up_w': 8.0,
     'L0_ffn_sh_down_w': 8.0,
     'L0_ffn_sh_gate1_w': 8.0}
    for name, (base, spread) in spreads.items():
        noise = np.random.default_rng([zlib.crc32(name.encode()), seed]).standard_normal(out[name].shape)
        drawn = base * np.exp(spread * noise) if base else spread * noise
        out[name] = jnp.asarray(drawn.astype(out[name].dtype))
    for name, factor in factors.items():
        out[name] = (out[name] * factor).astype(out[name].dtype)
    return out
```

```python
from contextlib import ExitStack

import numpy as np

import concourse.bass as bass
from concourse import mybir

F32 = mybir.dt.float32
F32R = mybir.dt.float32r
BF16 = mybir.dt.bfloat16
I32 = mybir.dt.int32
U32 = mybir.dt.uint32
ALU = mybir.AluOpType
ACT = mybir.ActivationFunctionType
AX = mybir.AxisListType

P = 128
BATCH, SEQ, D = 8, 512, 256
HEADS, KV_HEADS, HEAD_D = 16, 4, 16
KV_D = KV_HEADS * HEAD_D
QK_D = D + KV_D
QKV_D = D + 2 * KV_D
PAIRS_OF_HEADS = HEADS // 2
TILES = SEQ // P
TOKENS = BATCH * SEQ
ALL_TILES = TOKENS // P
KC = D // P
EXPERTS, INNER, TOP = 64, 64, 8
GU = 2 * INNER
SHARED = 2 * INNER + 1
ROUTED = TOKENS * TOP
BLOCKS = ROUTED // P + EXPERTS
ROW = D + 3 * TOP
C_IDX, C_RW, C_DST = D, D + TOP, D + 2 * TOP
EPS = 1e-5
MASKED = -1e30
SKIP = 65536.0

C_IDENT, C_MASK1, C_MASK2, C_TRI, C_PIDX = 0, P, 2 * P, 3 * P, 4 * P
C_COS = 5 * P
C_SIN = C_COS + TILES * 8
C_NSIN = C_SIN + TILES * 8
C_BQKV = C_NSIN + TILES * 8
C_BO = C_BQKV + QKV_D
C_BLK = C_BO + D
C_DSTC = C_BLK + BLOCKS
C_END = C_DSTC + ALL_TILES * TOP


def held(value):
    return max(value, 0) if isinstance(value, int) else value


def build(nc, x, const, wqkv, wo, wroute, wgu, wdp, wshd, out):
    rows_d = nc.dram_tensor("rows_d", (BLOCKS * P, ROW), F32, kind="Internal").ap()
    res_d = nc.dram_tensor("res_d", (ROUTED, D), F32, kind="Internal").ap()
    x2_d = nc.dram_tensor("x2_d", (TOKENS, D + SHARED), F32, kind="Internal").ap()
    x_v = x.rearrange("b (t p) h -> (b t) p h", p=P)
    x2_v = x2_d.rearrange("(t p) h -> t p h", p=P)

    with ExitStack() as top:
        sem = lambda n: top.enter_context(nc.semaphore(n))
        ksb = lambda n, s, d: top.enter_context(nc.sbuf_tensor(n, s, d))
        cst = ksb("cst", [P, C_END], F32)
        shd_w = ksb("shd_w", [INNER, D], F32)
        taken = ksb("taken", [EXPERTS, BLOCKS], F32)
        ident = cst[:, C_IDENT:C_IDENT + P]
        met_pe, met_dve, met_pool = sem("waits_met_pe"), sem("waits_met_dve"), sem("waits_met_pool")

        with ExitStack() as ctx:
            sb = lambda n, s, d: ctx.enter_context(nc.sbuf_tensor(n, s, d))
            ps = lambda n, s: ctx.enter_context(nc.psum_tensor(n, s, F32))
            two = lambda n, s, d: [sb(f"{n}{k}", s, d) for k in range(2)]
            wqkv_s = sb("wqkv_s", [P, KC, QKV_D], F32)
            wo_s = sb("wo_s", [P, KC, D], F32)
            wroute_s = sb("wroute_s", [P, KC, EXPERTS + SHARED], F32)
            ident_r = sb("ident_r", [P, P], F32R)
            ident_b = sb("ident_b", [P, P], BF16)
            mask1 = sb("mask1", [P, P], BF16)
            mask2 = sb("mask2", [P, P], BF16)
            tri_b = sb("tri_b", [P, P], BF16)
            ones_b = sb("ones_b", [P, P], BF16)
            ones_f = sb("ones_f", [P, P], F32)
            minus_half = sb("minus_half", [P, 1], F32)
            blank = sb("blank", [P, ROW], F32)
            xin = sb("xin", [P, TILES, D], F32)
            xr = two("xr", [P, D], F32)
            stat = two("stat", [P, 6], F32)
            mv = two("mv", [P, 2], F32)
            rstd = two("rstd", [P, 1], F32)
            xn = two("xn", [P, D], F32)
            xnT = two("xnT", [P, KC, P], F32)
            qkv = two("qkv", [P, QKV_D], F32)
            rot = two("rot", [P, QK_D // 16, 2, 8], F32)
            rope = two("rope", [P, QK_D // 16, 2, 8], F32)
            qs = two("qs", [P, PAIRS_OF_HEADS, 4, 32], F32R)
            ks = sb("ks", [P, KV_HEADS, 2, 4, 32], F32R)
            qT = two("qT", [P, PAIRS_OF_HEADS, SEQ], F32R)
            kT = two("kT", [P, 2 * KV_HEADS, SEQ], F32R)
            v1 = two("v1", [P, TILES, KV_HEADS, 32], F32)
            nmax = two("nmax", [P, TILES, 2], F32)
            mt = two("mt", [P, TILES, P], F32R)
            pexp = [sb(f"pexp{k}", [P, 5, SEQ], F32) for k in range(4)]
            oT = two("oT", [P, KV_HEADS, SEQ], F32)
            rden = two("rden", [P, HEADS], F32)
            yb = two("yb", [P, D], F32)
            yT = two("yT", [P, KC, P], F32)
            xb = two("xb", [P, D], F32)
            x2 = two("x2", [P, D + SHARED], F32)
            stat2 = two("stat2", [P, 6], F32)
            mv2 = two("mv2", [P, 2], F32)
            rstd2 = two("rstd2", [P, 1], F32)
            x2T = two("x2T", [P, KC, P], F32)
            pay = two("pay", [P, TILES, ROW], F32)
            logit = two("logit", [P, TILES, EXPERTS], F32)
            chosen = sb("chosen", [P, TILES, EXPERTS], BF16)
            topv = sb("topv", [P, TILES, TOP], F32)
            topi = sb("topi", [P, TILES, TOP], U32)
            etop = sb("etop", [P, TILES, TOP], F32)
            esum = sb("esum", [P, TILES, 1], F32)
            erec = sb("erec", [P, TILES, 1], F32)
            col = sb("col", [EXPERTS, 16], F32)
            diag = sb("diag", [EXPERTS, 3, EXPERTS], F32)
            thd = sb("thd", [P, 2, EXPERTS], F32)
            place = sb("place", [P, TILES, EXPERTS], F32)
            slot_f = sb("slot_f", [P, TILES, TOP], F32)
            slot_i = two("slot_i", [P, TILES, TOP], I32)

            ps1 = ps("ps1", [P, 2, SEQ])
            ps2 = ps("ps2", [P, 2, SEQ])
            psv = ps("psv", [P, SEQ])
            psp = ps("psp", [P, 2, SEQ])
            psq = ps("psq", [P, SEQ])

            (s_const, s_memset, s_conv, s_blank, s_stat, s_ln1, s_rstd1, s_xn, s_xnT_ps, s_xnT, s_qkv_ps, s_qkv,
             s_rot, s_cosd, s_rope, s_v, s_hi, s_lo, s_split_ps, s_split, s_s1, s_red, s_msplit, s_m_ps,
             s_m, s_s2, s_exp, s_pv, s_oT, s_o_ps, s_rden, s_y, s_yT_ps, s_yT, s_att_ps, s_xb, s_x2, s_stat2,
             s_ln2, s_rstd2, s_x2n, s_x2T_ps, s_x2T, s_pre_ps, s_pre, s_top, s_left, s_chosen, s_shift, s_etop,
             s_esum, s_erec, s_rw, s_cnt_ps, s_cnt, s_new, s_base_ps, s_base, s_diag, s_rank_ps, s_thd, s_pl,
             s_slot, s_sloti, s_tk, s_pool, s_mhi, s_var1, s_var2) = [sem(n) for n in (
                 "const_in memsets consts_converted blank_rows stats1 moments1 rstd1_ready xn_ready xnT_psum xnT_ready "
                 "qkv_psum qkv_ready rot_ready cos_done rope_ready v_ready hi_ready lo_ready split_psum split_ready "
                 "scores1_psum max_read max_split maxT_psum maxT_ready scores2_psum exp_done pv_psum oT_ready "
                 "o_psum den_ready y_ready yT_psum yT_ready att_psum xb_ready x2_ready stats2 moments2 rstd2_ready "
                 "x2n_ready x2nT_psum x2nT_ready preact_psum preact_ready top_ready left_ready chosen_ready "
                 "top_shifted top_exp exp_sum exp_recip weights_ready count_psum count_ready new_ready base_psum "
                 "base_ready diag_ready rank_psum rows_read place_chain slots_ready slot_ints taken_step "
                 "pool_chain max_hi var1_ready var2_ready").split()]
            s_x = [sem(f"x_in{k}") for k in range(TILES)]
            s_xr = [sem(f"x_again{k}") for k in range(2)]
            s_x2out = [sem(f"x2_out{k}") for k in range(2)]
            s_scat = [sem(f"scattered{k}") for k in range(2)]

            BLANKS = 8
            PIECE = BLOCKS // BLANKS

            def blanks_for(b):
                blocks = (b + 1) * SEQ * TOP // P + EXPERTS - 1
                return min(BLANKS, -(-blocks // PIECE))

            def beat(steps, h, par, pre=True, main=True, post=True):
                nxt = (h, 1) if par == 0 else (h + 1, 0)
                prv = (h, 0) if par == 1 else (h - 1, 1)
                for p in range(PAIRS_OF_HEADS + 1):
                    if main:
                        steps["unit"](h, par, p)
                    if p < PAIRS_OF_HEADS:
                        if p % 2 == 0 and pre:
                            steps["pre"](*nxt, p // 2)
                        if p % 2 == 1 and post:
                            steps["post"](*prv, p // 2)
                if post:
                    steps["route"](*prv)

            def program(eng, steps):
                for t in range(TILES):
                    steps["pre"](0, 0, t)
                beat(steps, 0, 0, post=False)
                beat(steps, 0, 1)
                with eng.Fori(1, BATCH // 2 - 1) as h:
                    beat(steps, h, 0)
                    beat(steps, h, 1)
                beat(steps, BATCH // 2 - 1, 0)
                beat(steps, BATCH // 2 - 1, 1, pre=False)
                beat(steps, BATCH // 2, 0, pre=False, main=False)

            block = ctx.enter_context(nc.Block())

            @block.sync
            def _(sp):
                sp.dma_start(cst[:], const).then_inc(s_const, 16)
                sp.dma_start(wqkv_s[:], wqkv).then_inc(s_const, 16)
                for t in range(TILES):
                    sp.dma_start(xin[:, t, :], x_v[t]).then_inc(s_x[t], 16)
                sp.dma_start(wo_s[:], wo).then_inc(s_const, 16)
                sp.dma_start(wroute_s[:], wroute).then_inc(s_const, 16)
                sp.dma_start(shd_w[:], wshd).then_inc(s_const, 16)
                sp.wait_ge(s_memset, 1)
                blanks = rows_d.rearrange("(n j p) r -> n p j r", p=P, j=PIECE)
                for n in range(BLANKS):
                    if n >= 1:
                        sp.wait_ge(s_blank, 16 * n)
                    sp.dma_start(blanks[n], blank[:].unsqueeze(1).to_broadcast([P, PIECE, ROW])).then_inc(s_blank, 16)

                def pre(h, par, t):
                    if isinstance(h, int) and h * 2 + par == BATCH - 1:
                        return
                    tile = (h * 2 + par) * TILES + t
                    sp.wait_ge(s_xn, tile + 1)
                    sp.dma_start(xin[:, t, :], x_v[bass.ds(tile + TILES, 1)].rearrange("a p h -> p (a h)")
                                 ).then_inc(s_x[t], 16)

                def post(h, par, t):
                    tile = (h * 2 + par) * TILES + t
                    sp.wait_ge(s_xb, held(tile - 1))
                    sp.dma_start(xr[t % 2][:], x_v[bass.ds(tile, 1)].rearrange("a p h -> p (a h)")
                                 ).then_inc(s_xr[t % 2], 16)
                    sp.wait_ge(s_x2, tile + 1)
                    sp.wait_ge(s_pre, tile + 1)
                    sp.dma_start(x2_v[bass.ds(tile, 1)].rearrange("a p h -> p (a h)"), x2[t % 2][:]
                                 ).then_inc(s_x2out[t % 2], 16)

                program(sp, {"pre": pre, "unit": lambda h, par, p: None, "post": post, "route": lambda h, par: None})
                sp.wait_ge(s_x2out[0], 16 * ALL_TILES // 2)
                sp.wait_ge(s_x2out[1], 16 * ALL_TILES // 2)

            @block.gpsimd
            def _(pool):
                pool.memset(blank[:, 0:C_IDX], 0.0)
                pool.memset(blank[:, C_IDX:C_RW], -1.0)
                pool.memset(blank[:, C_RW:ROW], 0.0)
                pool.memset(ones_f[:], 1.0)
                pool.memset(minus_half[:], -0.5)
                pool.memset(col[:], 0.0)
                pool.memset(taken[:], 0.0)
                pool.memset(ks[:].bitcast(F32), 0.0)
                for k in range(2):
                    pool.memset(v1[k][:], 0.0)
                    pool.memset(qs[k][:].bitcast(F32), 0.0)
                    pool.memset(mt[k][:].bitcast(F32), 0.0)
                pool.memset(ones_b[:], 1.0).then_inc(s_memset, 1)
                pool.wait_ge(s_memset, 1)
                for k in range(2):
                    pool.memset(v1[k][:, :, :, 16:17], 1.0)
                for ab in range(2):
                    pool.memset(ks[:, :, ab, 3, ab:ab + 1].bitcast(F32), 1.0)
                    last = pool.memset(ks[:, :, ab, 3, ab + 2:ab + 3].bitcast(F32), 1.0)
                last.then_inc(s_memset, 1)
                pool.wait_ge(s_const, 80)

                def pre(h, par, t):
                    tile, u = (h * 2 + par) * TILES + t, t % 2
                    pool.wait_ge(s_ln1, tile + 1)
                    pool.sem_inc(met_pool)
                    pool.tensor_scalar(rstd[u][:], mv[u][:, 1:2], EPS, None, ALU.add).then_inc(s_var1, 1)
                    pool.wait_ge(s_var1, tile + 1)
                    pool.sem_inc(met_pool)
                    pool.tensor_tensor(rstd[u][:], rstd[u][:], minus_half[:], ALU.pow).then_inc(s_rstd1, 1)
                    pool.wait_ge(s_qkv, tile + 1)
                    pool.wait_ge(s_rope, held(tile - 1))
                    pool.sem_inc(met_pool)
                    heads = qkv[u][:, 0:QK_D].rearrange("p (n a d) -> p n a d", a=2, d=8)
                    sin = lambda c: cst[:, c + 8 * t:c + 8 * t + 8].unsqueeze(1).to_broadcast([P, QK_D // 16, 8])
                    pool.tensor_tensor(rot[u][:, :, 0, :], heads[:, :, 1, :], sin(C_NSIN), ALU.mult)
                    pool.tensor_tensor(rot[u][:, :, 1, :], heads[:, :, 0, :], sin(C_SIN), ALU.mult).then_inc(s_rot, 1)

                def post(h, par, t):
                    tile, u = (h * 2 + par) * TILES + t, t % 2
                    pool.wait_ge(s_xr[u], 16 * ((h * 2 + par) * 2 + t // 2 + 1))
                    pool.wait_ge(s_x2, held(tile - 1))
                    pool.sem_inc(met_pool)
                    pool.tensor_tensor(xb[u][:], xr[u][:], cst[:, C_BO:C_BO + D], ALU.add).then_inc(s_xb, 1)
                    pool.wait_ge(s_ln2, tile + 1)
                    pool.sem_inc(met_pool)
                    pool.tensor_scalar(rstd2[u][:], mv2[u][:, 1:2], EPS, None, ALU.add).then_inc(s_var2, 1)
                    pool.wait_ge(s_var2, tile + 1)
                    pool.sem_inc(met_pool)
                    pool.tensor_tensor(rstd2[u][:], rstd2[u][:], minus_half[:], ALU.pow).then_inc(s_rstd2, 1)

                def route(h, par):
                    b = h * 2 + par
                    step = [0]

                    def chain(ins, n=12):
                        step[0] += 1
                        ins.then_inc(s_pool, 1)
                        pool.wait_ge(s_pool, held(b * n + step[0]))
                        pool.sem_inc(met_pool)

                    c = lambda k, n=1: col[:, k:k + n]
                    pool.wait_ge(s_top, 4 * (b + 1))
                    pool.wait_ge(s_rw, held(b))
                    pool.sem_inc(met_pool)
                    pool.tensor_tensor(etop[:], topv[:], topv[:, :, 0:1].to_broadcast([P, TILES, TOP]),
                                       ALU.subtract).then_inc(s_shift, 1)
                    pool.tensor_copy(pay[par][:, :, C_IDX:C_IDX + TOP], topi[:])
                    pool.tensor_copy(pay[par][:, :, C_DST:C_DST + TOP],
                                     cst[:, bass.ds(C_DSTC + b * (TILES * TOP), TILES * TOP)]
                                     .rearrange("p (t k) -> p t k", k=TOP))
                    pool.wait_ge(s_cnt, b + 1)
                    pool.sem_inc(met_pool)
                    chain(pool.tensor_scalar(c(5), c(4), P / 2 - 0.5, 1.0 / P, ALU.add, ALU.mult))
                    chain(pool.tensor_scalar(c(5), c(5), 2.0 ** 23, None, ALU.add))
                    chain(pool.tensor_scalar(c(6), c(5), -(2.0 ** 23), float(P), ALU.add, ALU.mult))
                    pool.tensor_tensor(c(7), c(6), c(1), ALU.subtract).then_inc(s_new, 1)
                    pool.wait_ge(s_base, b + 1)
                    pool.sem_inc(met_pool)
                    chain(pool.tensor_tensor(c(10), c(8), c(1), ALU.subtract))
                    chain(pool.tensor_tensor(c(14), c(10), c(2), ALU.subtract))
                    chain(pool.tensor_scalar(c(12), c(0), c(2), 1.0, ALU.add, ALU.add))
                    chain(pool.tensor_scalar(c(13), c(1), c(2), 1.0, ALU.add, ALU.add))
                    chain(pool.tensor_tensor(c(9), c(8), c(7), ALU.add))
                    chain(pool.tensor_scalar(c(11), c(7), 0.0, c(14), ALU.is_gt, ALU.mult))
                    chain(pool.tensor_tensor(c(2), c(2), c(11), ALU.add))
                    chain(pool.tensor_copy(c(0), c(4)))
                    chain(pool.tensor_copy(c(1), c(6)))
                    pool.tensor_tensor(diag[:], cst[0:EXPERTS, C_IDENT:C_IDENT + EXPERTS].unsqueeze(1)
                                       .to_broadcast([EXPERTS, 3, EXPERTS]),
                                       c(12, 3).unsqueeze(2).to_broadcast([EXPERTS, 3, EXPERTS]),
                                       ALU.mult).then_inc(s_diag, 1)
                    pool.wait_ge(s_erec, b + 1)
                    pool.sem_inc(met_pool)
                    pool.tensor_tensor(pay[par][:, :, C_RW:C_RW + TOP], etop[:],
                                       erec[:].to_broadcast([P, TILES, TOP]), ALU.mult).then_inc(s_rw, 1)
                    pool.wait_ge(s_slot, b + 1)
                    pool.sem_inc(met_pool)
                    pool.tensor_scalar(slot_i[par][:], slot_f[:], -1.0, None, ALU.add).then_inc(s_sloti, 1)
                    pool.wait_ge(s_sloti, b + 1)
                    pool.wait_ge(s_rw, b + 1)
                    pool.sem_inc(met_pool)
                    pool.wait_ge(s_blank, 16 * (BLANKS if not isinstance(b, int) else blanks_for(b)))
                    for t in range(TILES):
                        for k in range(TOP):
                            pool.indirect_dma_start(
                                rows_d, bass.IndirectOffsetOnAxis(ap=slot_i[par][:, t, k:k + 1], axis=0),
                                pay[par][:, t, :], None).then_inc(s_scat[par], 16)

                program(pool, {"pre": pre, "unit": lambda h, par, p: None, "post": post, "route": route})
                for par in range(2):
                    pool.wait_ge(s_scat[par], 16 * TILES * TOP * BATCH // 2)

            @block.tensor
            def _(pe):
                pe.wait_ge(s_const, 80)
                pe.wait_ge(s_memset, 2)
                pe.wait_ge(s_conv, 1)

                def pre(h, par, t):
                    tile, u = (h * 2 + par) * TILES + t, t % 2
                    pe.wait_ge(s_xn, tile + 1)
                    pe.wait_ge(s_split, held(4 * tile - 1))
                    for k in range(KC):
                        last = pe.transpose(psp[:, 0, k * P:(k + 1) * P], xn[u][:, k * P:(k + 1) * P], ident)
                    last.then_inc(s_xnT_ps, 1)
                    pe.wait_ge(s_xnT, tile + 1)
                    pe.wait_ge(s_split, held(4 * tile))
                    for k in range(KC):
                        last = pe.matmul(psp[:, 1, 0:QKV_D], xnT[u][:, k, :], wqkv_s[:, k, :],
                                         start=(k == 0), stop=(k == KC - 1))
                    last.then_inc(s_qkv_ps, 1)
                    pe.wait_ge(s_lo, tile + 1)
                    for r in range(4):
                        src = (qs[u][:] if r < 2 else ks[:].rearrange("p g a c d -> p (g a) c d"))
                        if r >= 2:
                            pe.wait_ge(s_split, held(4 * tile + r - 1))
                        for n in range(4):
                            last = pe.transpose(psp[:, r % 2, n * P:(n + 1) * P].bitcast(F32R),
                                                src[:, 4 * (r % 2) + n].rearrange("p c d -> p (c d)"), ident_r[:])
                        last.then_inc(s_split_ps, 1)

                def unit(h, par, p):
                    b = h * 2 + par
                    U = b * PAIRS_OF_HEADS + p

                    def scores(bank, at, i, ab):
                        keys = (i + 1) * P
                        pe.matmul(ps1[:, bank, at:at + keys], qT[par][0:96, p, i * P:(i + 1) * P],
                                  kT[par][0:96, 2 * (p // 2) + ab, 0:keys], start=True, stop=False)
                        return pe.matmul(ps1[:, bank, at + i * P:at + keys], ident_b[:], mask1[:],
                                         start=False, stop=True)

                    def scoresT(bank, at, kt, ab):
                        q = p - 1
                        n = SEQ - kt * P
                        pe.matmul(ps2[:, bank, at:at + n], kT[par][:, 2 * (q // 2) + ab, kt * P:(kt + 1) * P],
                                  qT[par][:, q, kt * P:SEQ], start=True, stop=False)
                        return pe.matmul(ps2[:, bank, at:at + P], ident_b[:], mask2[:], start=False, stop=True)

                    def pass1(s):
                        if s == 0:
                            pe.wait_ge(s_red, 5 * U)
                            scores(1, 0, 3, 0).then_inc(s_s1, 1)
                        elif s == 1:
                            pe.wait_ge(s_m, U)
                            pe.wait_ge(s_red, held(5 * U - 1))
                            scores(0, 0, 3, 1).then_inc(s_s1, 1)
                        elif s in (2, 3):
                            pe.wait_ge(s_red, held(5 * U + s - 1))
                            bank = 1 if s == 2 else 0
                            scores(bank, 0, 2, s - 2)
                            scores(bank, 384, 0, s - 2).then_inc(s_s1, 1)
                        else:
                            pe.wait_ge(s_red, 5 * U + 3)
                            scores(1, 0, 1, 0)
                            scores(1, 256, 1, 1).then_inc(s_s1, 1)

                    def max_up():
                        pe.wait_ge(s_msplit, U)
                        pe.wait_ge(s_red, held(5 * U - 1))
                        u = (p - 1) % 2
                        for i in range(TILES):
                            last = pe.transpose(ps1[:, 0, i * P:(i + 1) * P].bitcast(F32R), mt[u][:, i, :], ident_r[:])
                        last.then_inc(s_m_ps, 1)

                    def pass2(s):
                        n = 5 * (U - 1) + s
                        bank = (5 * (p - 1) + s) % 2
                        pe.wait_ge(s_exp, held(n - 1))
                        if s == 0:
                            pe.wait_ge(s_m, U)
                        if s < 2:
                            scoresT(bank, 0, 0, s).then_inc(s_s2, 1)
                        elif s < 4:
                            scoresT(bank, 0, 1, s - 2)
                            scoresT(bank, 384, 3, s - 2).then_inc(s_s2, 1)
                        else:
                            scoresT(bank, 0, 2, 0)
                            scoresT(bank, 256, 2, 1).then_inc(s_s2, 1)

                    if p == 0:
                        pe.wait_ge(s_split, 16 * (b + 1))
                    for s in range(5):
                        if p < PAIRS_OF_HEADS:
                            pass1(s)
                        if p >= 1:
                            if s == 0:
                                max_up()
                            else:
                                pass2(s - 1)
                    if p >= 1:
                        pass2(4)
                    if p >= 3 and p % 2 == 1:
                        pv(h, par, (p - 3) // 2)
                    if p == PAIRS_OF_HEADS:
                        pv(h, par, KV_HEADS - 1)

                def pv(h, par, g):
                    b = h * 2 + par
                    pe.wait_ge(s_exp, held(5 * (b * PAIRS_OF_HEADS + 2 * g + 2)))
                    pe.wait_ge(s_oT, held(b * KV_HEADS + g))
                    pe.wait_ge(s_v, 4 * (b + 1))
                    for kt in range(TILES):
                        n = SEQ - kt * P
                        for hh in range(4):
                            ab = hh % 2
                            buf = pexp[(2 * g + hh // 2) % 4]
                            rhs = (buf[:, ab, :], buf[:, 2 + ab, 0:384], buf[:, 4, 256 * ab:256 * ab + 256],
                                   buf[:, 2 + ab, 384:512])[kt]
                            last = pe.matmul(psv[32 * hh:32 * hh + 32, kt * P:SEQ], v1[par][:, kt, g, :], rhs,
                                             start=(kt == 0), stop=(kt == TILES - 1), skip_group_check=True)
                    last.then_inc(s_pv, 1)

                def post(h, par, t):
                    b = h * 2 + par
                    tile, u = b * TILES + t, t % 2
                    pe.wait_ge(s_oT, 4 * (b + 1))
                    pe.wait_ge(s_pre, held(tile))
                    if t == 0:
                        pe.wait_ge(s_pl, held(b * 4))
                    for g in range(KV_HEADS):
                        last = pe.transpose(psq[:, g * P:(g + 1) * P], oT[par][:, g, t * P:(t + 1) * P], ident)
                    last.then_inc(s_o_ps, 1)
                    pe.wait_ge(s_y, tile + 1)
                    for k in range(KC):
                        last = pe.transpose(psq[:, k * P:(k + 1) * P], yb[u][:, k * P:(k + 1) * P], ident)
                    last.then_inc(s_yT_ps, 1)
                    pe.wait_ge(s_yT, tile + 1)
                    for k in range(KC):
                        last = pe.matmul(psq[:, 0:D], yT[u][:, k, :], wo_s[:, k, :], start=(k == 0), stop=(k == KC - 1))
                    last.then_inc(s_att_ps, 1)
                    pe.wait_ge(s_x2n, tile + 1)
                    for k in range(KC):
                        last = pe.transpose(psq[:, k * P:(k + 1) * P], pay[par][:, t, k * P:(k + 1) * P], ident)
                    last.then_inc(s_x2T_ps, 1)
                    pe.wait_ge(s_x2T, tile + 1)
                    for k in range(KC):
                        last = pe.matmul(psq[:, 0:EXPERTS + SHARED], x2T[u][:, k, :], wroute_s[:, k, :],
                                         start=(k == 0), stop=(k == KC - 1))
                    last.then_inc(s_pre_ps, 1)

                def route(h, par):
                    b = h * 2 + par
                    pe.wait_ge(s_chosen, b + 1)
                    pe.wait_ge(s_pre, 4 * (b + 1))
                    pe.sem_inc(met_pe)
                    for t in range(TILES):
                        last = pe.matmul(psq[0:EXPERTS, 0:1], chosen[:, t, :], ones_b[:, 0:1],
                                         start=(t == 0), stop=(t == TILES - 1))
                    last.then_inc(s_cnt_ps, 1)
                    pe.wait_ge(s_new, b + 1)
                    pe.sem_inc(met_pe)
                    pe.matmul(psq[0:EXPERTS, 0:1], cst[0:EXPERTS, C_TRI:C_TRI + EXPERTS], col[:, 7:8],
                              start=True, stop=True)
                    pe.matmul(psq[0:EXPERTS, 1:2], ones_f[0:EXPERTS, 0:EXPERTS], col[:, 7:8],
                              start=True, stop=True).then_inc(s_base_ps, 1)
                    pe.wait_ge(s_diag, b + 1)
                    pe.matmul(psq[:, 384:512], ones_f[0:EXPERTS, :], diag[:, 1:3, :].rearrange("p a e -> p (a e)"),
                              start=True, stop=True)
                    for t in range(TILES):
                        at = psq[:, t * EXPERTS:(t + 1) * EXPERTS]
                        pe.matmul(at, ones_f[0:EXPERTS, :], diag[:, 0, :], start=True, stop=False)
                        for t0 in range(t):
                            pe.matmul(at, ones_b[:], chosen[:, t0, :], start=False, stop=False)
                        last = pe.matmul(at, tri_b[:], chosen[:, t, :], start=False, stop=True)
                    last.then_inc(s_rank_ps, 1)

                program(pe, {"pre": pre, "unit": unit, "post": post, "route": route})

            @block.scalar
            def _(act):
                act.wait_ge(s_memset, 2)

                def pre(h, par, t):
                    b = h * 2 + par
                    tile, u = b * TILES + t, t % 2
                    act.wait_ge(s_xnT_ps, tile + 1)
                    act.wait_ge(s_qkv_ps, held(tile - 1))
                    act.copy(xnT[u][:], psp[:, 0, 0:D].rearrange("p (k n) -> p k n", k=KC)).then_inc(s_xnT, 1)
                    act.wait_ge(s_qkv, tile + 1)
                    act.wait_ge(s_pv, held(KV_HEADS * (b - 1)))
                    act.copy(v1[par][:, t, :, 0:HEAD_D],
                             qkv[u][:, QK_D:QKV_D].rearrange("p (g d) -> p g d", d=HEAD_D)).then_inc(s_v, 1)
                    act.wait_ge(s_rope, tile + 1)
                    act.wait_ge(s_split_ps, held(4 * tile))
                    flat = rope[u][:].rearrange("p n a d -> p (n a d)")
                    act.copy(qs[u][:, :, 0:2, :], flat[:, 0:D].rearrange("p (n d) -> p n d", d=32).unsqueeze(2)
                             .to_broadcast([P, PAIRS_OF_HEADS, 2, 32]))
                    kh = flat[:, D:QK_D].rearrange("p (g d) -> p g d", d=HEAD_D)
                    for ab in range(2):
                        dst = ks[:, :, ab, :, 16 * ab:16 * ab + 16]
                        last = act.copy(dst[:, :, 0, :], kh)
                        last = act.copy(dst[:, :, 2, :], kh)
                    last.then_inc(s_hi, 1)
                    if t == 0:
                        act.wait_ge(s_s2, held(40 * (b - 1)))
                    for r in range(4):
                        act.wait_ge(s_split_ps, 4 * tile + r + 1)
                        rows = 96 if r < 2 else P
                        dst = (qT if r < 2 else kT)[par][0:rows, 4 * (r % 2):4 * (r % 2) + 4, t * P:(t + 1) * P]
                        act.copy(dst, psp[0:rows, r % 2, :].bitcast(F32R).rearrange("p (n c) -> p n c", n=4)
                                 ).then_inc(s_split, 1)

                def unit(h, par, p):
                    if p == 0:
                        return
                    b = h * 2 + par
                    U = b * PAIRS_OF_HEADS + p - 1
                    act.wait_ge(s_m_ps, U + 1)
                    act.copy(qT[par][96:128, p - 1, :], ps1[96:128, 0, :].bitcast(F32R)).then_inc(s_m, 1)
                    if (p - 1) % 2 == 0:
                        act.wait_ge(s_pv, held(b * KV_HEADS + (p - 1) // 2 - 1))
                    for s in range(5):
                        act.wait_ge(s_s2, 5 * U + s + 1)
                        act.activation(pexp[(p - 1) % 4][:, s, :], ps2[:, (5 * (p - 1) + s) % 2, :], ACT.Exp,
                                       scale=HEAD_D ** -0.5).then_inc(s_exp, 1)
                    if p >= 3 and p % 2 == 1:
                        take_o(h, par, (p - 3) // 2)
                    if p == PAIRS_OF_HEADS:
                        take_o(h, par, KV_HEADS - 1)

                def take_o(h, par, g):
                    b = h * 2 + par
                    act.wait_ge(s_pv, b * KV_HEADS + g + 1)
                    act.wait_ge(s_o_ps, held(TILES * (b - 1)))
                    act.copy(oT[par][:, g, :], psv[:]).then_inc(s_oT, 1)

                def post(h, par, t):
                    tile, u = (h * 2 + par) * TILES + t, t % 2
                    act.wait_ge(s_yT_ps, tile + 1)
                    act.copy(yT[u][:], psq[:, 0:D].rearrange("p (k n) -> p k n", k=KC)).then_inc(s_yT, 1)
                    act.wait_ge(s_x2T_ps, tile + 1)
                    act.copy(x2T[u][:], psq[:, 0:D].rearrange("p (k n) -> p k n", k=KC)).then_inc(s_x2T, 1)
                    act.wait_ge(s_pre_ps, tile + 1)
                    act.copy(logit[par][:, t, :], psq[:, 0:EXPERTS])
                    act.wait_ge(s_x2out[u], held(16 * ((h * 2 + par) * 2 + t // 2)))
                    act.copy(x2[u][:, D:D + SHARED], psq[:, EXPERTS:EXPERTS + SHARED]).then_inc(s_pre, 1)

                def route(h, par):
                    b = h * 2 + par
                    act.wait_ge(s_shift, b + 1)
                    act.activation(etop[:], etop[:], ACT.Exp).then_inc(s_etop, 1)
                    act.wait_ge(s_rank_ps, b + 1)
                    act.copy(thd[:], psq[:, 384:512].rearrange("p (a e) -> p a e", a=2)).then_inc(s_thd, 1)

                program(act, {"pre": pre, "unit": unit, "post": post, "route": route})

            @block.vector
            def _(dve):
                dve.wait_ge(s_const, 80)
                dve.tensor_copy(ident_r[:], ident)
                dve.tensor_copy(ident_b[:], ident)
                dve.tensor_copy(mask1[:], cst[:, C_MASK1:C_MASK1 + P])
                dve.tensor_copy(mask2[:], cst[:, C_MASK2:C_MASK2 + P])
                dve.tensor_copy(tri_b[:], cst[:, C_TRI:C_TRI + P]).then_inc(s_conv, 1)
                dve.wait_ge(s_memset, 2)

                def pre(h, par, t):
                    tile, u = (h * 2 + par) * TILES + t, t % 2
                    dve.wait_ge(s_x[t], 16 * (h * 2 + par + 1))
                    dve.bn_stats(stat[u][:], xin[:, t, :]).then_inc(s_stat, 1)
                    dve.wait_ge(s_stat, tile + 1)
                    dve.sem_inc(met_dve)
                    dve.bn_aggr(mv[u][:], stat[u][:]).then_inc(s_ln1, 1)
                    dve.wait_ge(s_rstd1, tile + 1)
                    dve.wait_ge(s_ln1, tile + 1)
                    dve.wait_ge(s_xnT_ps, held(tile - 1))
                    dve.tensor_scalar(xn[u][:], xin[:, t, :], mv[u][:, 0:1], rstd[u][:], ALU.subtract,
                                      ALU.mult).then_inc(s_xn, 1)
                    dve.wait_ge(s_qkv_ps, tile + 1)
                    dve.wait_ge(s_rot, held(tile - 1))
                    dve.wait_ge(s_v, held(tile - 1))
                    dve.tensor_tensor(qkv[u][:], psp[:, 1, 0:QKV_D], cst[:, C_BQKV:C_BQKV + QKV_D],
                                      ALU.add).then_inc(s_qkv, 1)
                    dve.wait_ge(s_qkv, tile + 1)
                    dve.wait_ge(s_hi, held(tile - 1))
                    dve.tensor_tensor(rope[u][:], qkv[u][:, 0:QK_D].rearrange("p (n a d) -> p n a d", a=2, d=8),
                                      cst[:, C_COS + 8 * t:C_COS + 8 * t + 8].unsqueeze(1).unsqueeze(1)
                                      .to_broadcast([P, QK_D // 16, 2, 8]), ALU.mult).then_inc(s_cosd, 1)
                    dve.wait_ge(s_cosd, tile + 1)
                    dve.wait_ge(s_rot, tile + 1)
                    dve.tensor_tensor(rope[u][:], rope[u][:], rot[u][:], ALU.add).then_inc(s_rope, 1)
                    dve.wait_ge(s_hi, tile + 1)
                    flat = rope[u][:].rearrange("p n a d -> p (n a d)")
                    dve.tensor_tensor(qs[u][:, :, 2, :], flat[:, 0:D].rearrange("p (n d) -> p n d", d=32),
                                      qs[u][:, :, 0, :], ALU.subtract)
                    kf = flat[:, D:QK_D].rearrange("p (g d) -> p g d", d=HEAD_D)
                    for ab in range(2):
                        c = slice(16 * ab, 16 * ab + 16)
                        last = dve.tensor_tensor(ks[:, :, ab, 1, c], kf, ks[:, :, ab, 0, c], ALU.subtract)
                    last.then_inc(s_lo, 1)

                def unit(h, par, p):
                    if p == PAIRS_OF_HEADS:
                        return
                    U, u = (h * 2 + par) * PAIRS_OF_HEADS + p, p % 2

                    def largest(s, tile, bank, at, n, heads):
                        dve.wait_ge(s_s1, 5 * U + s + 1)
                        src = ps1[:, bank, at:at + n]
                        if len(heads) == 2:
                            src = src.rearrange("p (a n) -> p a n", a=2)
                        return dve.tensor_reduce(nmax[u][:, tile, heads[0]:heads[-1] + 1], src, AX.X, ALU.max,
                                                 negate=True)

                    largest(0, 3, 1, 0, 512, [0]).then_inc(s_red, 1)
                    largest(1, 3, 0, 0, 512, [1]).then_inc(s_red, 1)
                    for ab in range(2):
                        largest(2 + ab, 2, 1 - ab, 0, 384, [ab])
                        largest(2 + ab, 0, 1 - ab, 384, 128, [ab]).then_inc(s_red, 1)
                    largest(4, 1, 1, 0, 512, [0, 1]).then_inc(s_red, 1)
                    dve.wait_ge(s_red, 5 * U + 5)
                    dve.wait_ge(s_m_ps, held(U - 1))
                    dve.tensor_copy(mt[u][:, :, 96:98], nmax[u][:]).then_inc(s_mhi, 1)
                    dve.wait_ge(s_mhi, U + 1)
                    dve.tensor_tensor(mt[u][:, :, 98:100], nmax[u][:], mt[u][:, :, 96:98],
                                      ALU.subtract).then_inc(s_msplit, 1)

                def post(h, par, t):
                    b = h * 2 + par
                    tile, u = b * TILES + t, t % 2
                    dve.wait_ge(s_o_ps, tile + 1)
                    heads = psq[:].rearrange("p (n d) -> p n d", d=32)
                    dve.reciprocal(rden[u][:], heads[:, :, HEAD_D]).then_inc(s_rden, 1)
                    dve.wait_ge(s_rden, tile + 1)
                    dve.wait_ge(s_yT_ps, held(tile - 1))
                    dve.tensor_tensor(yb[u][:].rearrange("p (n d) -> p n d", d=HEAD_D), heads[:, :, 0:HEAD_D],
                                      rden[u][:].unsqueeze(2).to_broadcast([P, HEADS, HEAD_D]),
                                      ALU.mult).then_inc(s_y, 1)
                    dve.wait_ge(s_att_ps, tile + 1)
                    dve.wait_ge(s_xb, tile + 1)
                    dve.wait_ge(s_x2out[u], held(16 * (b * 2 + t // 2)))
                    dve.tensor_tensor(x2[u][:, 0:D], psq[:, 0:D], xb[u][:], ALU.add).then_inc(s_x2, 1)
                    dve.wait_ge(s_x2, tile + 1)
                    dve.bn_stats(stat2[u][:], x2[u][:, 0:D]).then_inc(s_stat2, 1)
                    dve.wait_ge(s_stat2, tile + 1)
                    dve.sem_inc(met_dve)
                    dve.bn_aggr(mv2[u][:], stat2[u][:]).then_inc(s_ln2, 1)
                    dve.wait_ge(s_rstd2, tile + 1)
                    dve.wait_ge(s_ln2, tile + 1)
                    if t == 0:
                        dve.wait_ge(s_scat[par], held(16 * TILES * TOP * h))
                    dve.tensor_scalar(pay[par][:, t, 0:D], x2[u][:, 0:D], mv2[u][:, 0:1], rstd2[u][:], ALU.subtract,
                                      ALU.mult).then_inc(s_x2n, 1)

                def route(h, par):
                    b = h * 2 + par
                    dve.wait_ge(s_pre, 4 * (b + 1))
                    dve.wait_ge(s_rw, held(b))
                    dve.sem_inc(met_dve)
                    for t in range(TILES):
                        dve.max(topv[:, t, :], logit[par][:, t, :]).then_inc(s_left, 1)
                    dve.wait_ge(s_left, 4 * (b + 1))
                    dve.sem_inc(met_dve)
                    for t in range(TILES):
                        dve.max_index(topi[:, t, :], topv[:, t, :], logit[par][:, t, :])
                        dve.match_replace(place[:, t, :], topv[:, t, :], logit[par][:, t, :], -3e38).then_inc(s_top, 1)
                    dve.wait_ge(s_top, 4 * (b + 1))
                    dve.tensor_tensor(chosen[:], place[:], logit[par][:], ALU.not_equal).then_inc(s_chosen, 1)
                    dve.wait_ge(s_cnt_ps, b + 1)
                    dve.tensor_tensor(col[:, 4:5], psq[0:EXPERTS, 0:1], col[:, 0:1], ALU.add).then_inc(s_cnt, 1)
                    dve.wait_ge(s_etop, b + 1)
                    dve.tensor_reduce(esum[:].rearrange("p t a -> p (t a)"), etop[:], AX.X, ALU.add).then_inc(s_esum, 1)
                    dve.wait_ge(s_esum, b + 1)
                    dve.reciprocal(erec[:], esum[:]).then_inc(s_erec, 1)
                    dve.wait_ge(s_base_ps, b + 1)
                    dve.tensor_tensor(col[:, 8:9], psq[0:EXPERTS, 0:1], col[:, 3:4], ALU.add).then_inc(s_tk, 1)
                    dve.wait_ge(s_tk, 4 * b + 1)
                    dve.tensor_tensor(col[:, 3:4], psq[0:EXPERTS, 1:2], col[:, 3:4], ALU.add).then_inc(s_base, 1)
                    dve.wait_ge(s_diag, b + 1)
                    blk = cst[0:EXPERTS, C_BLK:C_BLK + BLOCKS]
                    dve.scalar_tensor_tensor(out=taken[:], in0=blk, scalar=col[:, 8:9], in1=taken[:],
                                             op0=ALU.is_ge, op1=ALU.subtract).then_inc(s_tk, 1)
                    dve.wait_ge(s_tk, held(4 * b + 2))
                    dve.scalar_tensor_tensor(out=taken[:], in0=blk, scalar=col[:, 9:10], in1=taken[:],
                                             op0=ALU.is_ge, op1=ALU.subtract).then_inc(s_tk, 2)
                    dve.wait_ge(s_thd, b + 1)
                    rank = psq[:, 0:TILES * EXPERTS].rearrange("p (t e) -> p t e", e=EXPERTS)
                    wide = lambda a: thd[:, a, :].unsqueeze(1).to_broadcast([P, TILES, EXPERTS])
                    dve.tensor_tensor(place[:], rank, wide(0), ALU.is_ge).then_inc(s_pl, 1)
                    dve.wait_ge(s_pl, 4 * b + 1)
                    dve.tensor_tensor(place[:], place[:], wide(1), ALU.mult).then_inc(s_pl, 1)
                    dve.wait_ge(s_pl, held(4 * b + 2))
                    dve.tensor_tensor(place[:], rank, place[:], ALU.add).then_inc(s_pl, 1)
                    dve.wait_ge(s_pl, held(4 * b + 3))
                    dve.tensor_tensor(place[:], place[:], chosen[:], ALU.mult).then_inc(s_pl, 1)
                    dve.wait_ge(s_pl, held(4 * b + 4))
                    dve.wait_ge(s_sloti, held(b))
                    dve.sem_inc(met_dve)
                    for t in range(TILES):
                        last = dve.max(slot_f[:, t, :], place[:, t, :])
                    last.then_inc(s_slot, 1)

                program(dve, {"pre": pre, "unit": unit, "post": post, "route": route})

        with ExitStack() as ctx:
            sb = lambda n, s, d: ctx.enter_context(nc.sbuf_tensor(n, s, d))
            ps = lambda n, s: ctx.enter_context(nc.psum_tensor(n, s, F32))
            wgu_s = sb("wgu_s", [P, EXPERTS * KC * GU], F32)
            wdp_s = sb("wdp_s", [INNER, EXPERTS * D], F32)
            owner = sb("owner", [P, BLOCKS], F32)
            woff = sb("woff", [1, BLOCKS], I32)
            pidx_neg = sb("pidx_neg", [EXPERTS, P], F32)
            R = 4
            xg = sb("xg", [P, 2 * R, ROW], F32)
            xT = sb("xT", [P, 2, KC, P], F32)
            sg = sb("sg", [P, 2, INNER], F32)
            inner = sb("inner", [P, 2, INNER], F32)
            innerT = sb("innerT", [INNER, 2, P], F32)
            y = sb("y", [P, R, D], F32)
            hit = sb("hit", [P, 2, R, TOP], F32)
            hits = sb("hits", [P, 2, R, 2, TOP], F32)
            picked = sb("picked", [P, 2, R, 2], F32)
            dst_i = sb("dst_i", [P, 2 * R], I32)
            psA = ps("psA", [P, 2, SEQ])
            psB = ps("psB", [P, 2, SEQ])
            psC = ps("psC", [P, 2, SEQ])
            psD = ps("psD", [P, 2, SEQ])
            (e_w, e_neg, e_own_ps, e_own, e_woff, e_a_ps, e_a, e_b_ps, e_sg, e_in, e_c_ps, e_c, e_d_ps, e_d,
             e_hit, e_hits, e_pick, e_dst) = [sem(n) for n in (
                 "weights_in pidx_negated owner_psum owner_ready woff_ready xgT_psum xgT_ready gu_psum silu_ready "
                 "inner_ready innerT_psum innerT_ready down_psum yrow_ready hit_ready hits_ready picked_ready "
                 "dst_ready").split()]
            e_x = [sem(f"xg_in{k}") for k in range(2 * R)]
            e_out = [sem(f"y_out{k}") for k in range(R)]
            ROUNDS = BLOCKS // (2 * R)
            block = ctx.enter_context(nc.Block())

            def rounds(eng, step):
                step(0)
                with eng.Fori(1, ROUNDS) as n:
                    step(n)

            @block.sync
            def _(sp):
                half = EXPERTS * KC * GU // 2
                sp.dma_start(wgu_s[:, 0:half], wgu[:, 0:half]).then_inc(e_w, 16)
                sp.dma_start(wgu_s[:, half:], wgu[:, half:]).then_inc(e_w, 16)
                sp.dma_start(wdp_s[:], wdp).then_inc(e_w, 16)
                rows_v = rows_d.rearrange("(j p) r -> j p r", p=P)

                def step(n):
                    for k in range(2 * R):
                        j = n * (2 * R) + k
                        sp.wait_ge(e_a_ps, held(j - 2 * R + 1))
                        sp.wait_ge(e_pick, held((j - k) // 4 - 2 + 1 + k // 4 if isinstance(n, int) else n * 2 - 1 + k // 4))
                        sp.wait_ge(e_in, held(j - 2 * R + 1))
                        sp.dma_start(xg[:, k, :], rows_v[bass.ds(j, 1)].rearrange("a p r -> p (a r)")
                                     ).then_inc(e_x[k], 16)

                rounds(sp, step)

            @block.vector
            def _(dve):
                dve.tensor_scalar(pidx_neg[:], cst[0:EXPERTS, C_PIDX:C_PIDX + P], -1.0, None,
                                  ALU.mult).then_inc(e_neg, 1)
                dve.wait_ge(e_own_ps, 1)
                dve.tensor_copy(owner[:], psA[:, 0, 0:BLOCKS]).then_inc(e_own, 1)
                dve.wait_ge(e_own, 1)
                dve.tensor_scalar(woff[:], owner[0:1, :], float(KC * GU), None, ALU.mult).then_inc(e_woff, 1)

                def step(n):
                    for k in range(2 * R):
                        j = n * (2 * R) + k
                        if k % R == 0:
                            m = k // R
                            q = n * 2 + m
                            for r in range(R):
                                dve.wait_ge(e_x[k + r], 16 * (n + 1))
                            own = owner[:, bass.ds(j, R)].unsqueeze(2).to_broadcast([P, R, TOP])
                            dve.tensor_tensor(hit[:, m], xg[:, k:k + R, C_IDX:C_IDX + TOP], own,
                                              ALU.is_equal).then_inc(e_hit, 1)
                            dve.wait_ge(e_hit, q + 1)
                            dve.tensor_tensor(hits[:, m], xg[:, k:k + R, C_RW:C_RW + 2 * TOP].rearrange(
                                "p r (a k) -> p r a k", a=2), hit[:, m].unsqueeze(2).to_broadcast([P, R, 2, TOP]),
                                ALU.mult).then_inc(e_hits, 1)
                            dve.wait_ge(e_hits, q + 1)
                            dve.tensor_reduce(picked[:, m], hits[:, m], AX.X, ALU.add).then_inc(e_pick, 1)
                            dve.wait_ge(e_pick, q + 1)
                            for r in range(R):
                                dve.wait_ge(e_out[r], held(16 * (q - 1)))
                            dve.tensor_scalar(dst_i[:, k:k + R], picked[:, m, :, 1], SKIP, None,
                                              ALU.add).then_inc(e_dst, 1)
                        dve.wait_ge(e_sg, j + 1)
                        dve.wait_ge(e_c_ps, held(j - 1))
                        dve.scalar_tensor_tensor(out=inner[:, k % 2, :], in0=sg[:, k % 2, :],
                                                 scalar=picked[:, k // R, k % R, 0:1], in1=psB[:, k % 2, INNER:GU],
                                                 op0=ALU.mult, op1=ALU.mult).then_inc(e_in, 1)
                        dve.wait_ge(e_c_ps, j + 1)
                        dve.wait_ge(e_d_ps, held(j - 1))
                        dve.tensor_copy(innerT[:, k % 2, :], psC[0:INNER, k % 2, 0:P]).then_inc(e_c, 1)

                rounds(dve, step)

            @block.scalar
            def _(act):
                def step(n):
                    for k in range(2 * R):
                        j = n * (2 * R) + k
                        act.wait_ge(e_a_ps, j + 1)
                        act.wait_ge(e_b_ps, held(j - 1))
                        act.copy(xT[:, k % 2], psA[:, k % 2, 0:D].rearrange("p (k n) -> p k n", k=KC)).then_inc(e_a, 1)
                        act.wait_ge(e_b_ps, j + 1)
                        act.wait_ge(e_in, held(j - 1))
                        act.activation(sg[:, k % 2, :], psB[:, k % 2, 0:INNER], ACT.Silu).then_inc(e_sg, 1)
                        act.wait_ge(e_d_ps, j + 1)
                        q = n * 2 + k // R
                        act.wait_ge(e_out[k % R], held(16 * q))
                        act.copy(y[:, k % R, :], psD[:, k % 2, 0:D]).then_inc(e_d, 1)

                rounds(act, step)

            @block.tensor
            def _(pe):
                pe.wait_ge(e_neg, 1)
                pe.matmul(psA[:, 0, 0:BLOCKS], pidx_neg[:], taken[:], start=True, stop=True).then_inc(e_own_ps, 1)
                pe.wait_ge(e_woff, 1)
                pe.wait_ge(e_w, 48)

                def step(n):
                    for k in range(2 * R):
                        j = n * (2 * R) + k
                        off = pe.value_load(woff[0:1, bass.ds(j, 1)], min_val=0, max_val=(EXPERTS - 1) * D)
                        pe.wait_ge(e_x[k], 16 * (n + 1))
                        pe.wait_ge(e_a, held(j - 1))
                        for c in range(KC):
                            last = pe.transpose(psA[:, k % 2, c * P:(c + 1) * P], xg[:, k, c * P:(c + 1) * P], ident)
                        last.then_inc(e_a_ps, 1)
                        pe.wait_ge(e_a, j + 1)
                        pe.wait_ge(e_in, held(j - 1))
                        for c in range(KC):
                            last = pe.matmul(psB[:, k % 2, 0:GU], xT[:, k % 2, c, :], wgu_s[:, bass.ds(off + c * GU, GU)],
                                             start=(c == 0), stop=(c == KC - 1))
                        last.then_inc(e_b_ps, 1)
                        pe.wait_ge(e_in, j + 1)
                        pe.wait_ge(e_c, held(j - 1))
                        pe.sem_inc(met_pe)
                        pe.transpose(psC[0:INNER, k % 2, 0:P], inner[:, k % 2, :], ident).then_inc(e_c_ps, 1)
                        pe.wait_ge(e_c, j + 1)
                        pe.wait_ge(e_d, held(j - 1))
                        pe.matmul(psD[:, k % 2, 0:D], innerT[:, k % 2, :], wdp_s[:, bass.ds(off, D)],
                                  start=True, stop=True).then_inc(e_d_ps, 1)

                rounds(pe, step)

            @block.gpsimd
            def _(pool):
                def step(n):
                    for k in range(2 * R):
                        j = n * (2 * R) + k
                        pool.wait_ge(e_dst, n * 2 + k // R + 1)
                        pool.wait_ge(e_d, j + 1)
                        pool.sem_inc(met_pool)
                        pool.indirect_dma_start(
                            res_d, bass.IndirectOffsetOnAxis(ap=dst_i[:, k:k + 1], axis=0), y[:, k % R, :], None,
                            bounds_check=ROUTED - 1, oob_is_err=False).then_inc(e_out[k % R], 16)

                rounds(pool, step)
                for r in range(R):
                    pool.wait_ge(e_out[r], 16 * BLOCKS // R)

        with ExitStack() as ctx:
            sb = lambda n, s, d: ctx.enter_context(nc.sbuf_tensor(n, s, d))
            ps = lambda n, s: ctx.enter_context(nc.psum_tensor(n, s, F32))
            R = 4
            yk = sb("yk", [P, R, TOP, D], F32)
            xs = sb("xs", [P, R, D + SHARED], F32)
            gate = sb("gate", [P, 2, INNER], F32)
            sgate = sb("sgate", [P, 2, 1], F32)
            sh = sb("sh", [P, 2, INNER], F32)
            shT = sb("shT", [INNER, 2, P], F32)
            acc = sb("acc", [P, 2, D], F32)
            acc2 = sb("acc2", [P, 2, D], F32)
            fin = sb("fin", [P, 2, D], F32)
            psS = ps("psS", [P, 2, SEQ])
            psY = ps("psY", [P, 2, SEQ])
            (c_gate, c_sh, c_t_ps, c_t, c_y_ps, c_acc, c_acc2, c_fin) = [sem(n) for n in (
                "gate_ready sh_ready shT_psum shT_ready shdown_psum sum_ready sum2_ready fin_ready").split()]
            c_in = [sem(f"yk_in{k}") for k in range(R)]
            c_out = [sem(f"fin_out{k}") for k in range(2)]
            block = ctx.enter_context(nc.Block())

            def tiles(eng, step):
                step(0)
                with eng.Fori(1, ALL_TILES // R) as n:
                    step(n)

            @block.sync
            def _(sp):
                res_v = res_d.rearrange("(t p k) h -> t p k h", p=P, k=TOP)

                def step(n):
                    for k in range(R):
                        j = n * R + k
                        sp.wait_ge(c_acc, held(j - R + 1))
                        sp.wait_ge(c_acc2, held(j - R + 1))
                        sp.dma_start(yk[:, k], res_v[bass.ds(j, 1)].rearrange("a p k h -> p (a k) h")
                                     ).then_inc(c_in[k], 16)
                        sp.dma_start(xs[:, k], x2_v[bass.ds(j, 1)].rearrange("a p h -> p (a h)")
                                     ).then_inc(c_in[k], 16)

                tiles(sp, step)

            @block.scalar
            def _(act):
                out_v = out.rearrange("b (t p) h -> (b t) p h", p=P)

                def step(n):
                    for k in range(R):
                        j = n * R + k
                        act.wait_ge(c_in[k], 32 * (n + 1))
                        act.wait_ge(c_sh, held(j - 1))
                        act.activation(gate[:, k % 2, :], xs[:, k, D:D + INNER], ACT.Silu)
                        act.activation(sgate[:, k % 2, :], xs[:, k, D + 2 * INNER:D + SHARED],
                                       ACT.Sigmoid).then_inc(c_gate, 1)
                        act.wait_ge(c_t_ps, j + 1)
                        act.wait_ge(c_y_ps, held(j - 1))
                        act.copy(shT[:, k % 2, :], psS[0:INNER, k % 2, 0:P]).then_inc(c_t, 1)
                        act.wait_ge(c_fin, j + 1)
                        act.dma_start(out_v[bass.ds(j, 1)].rearrange("a p h -> p (a h)"), fin[:, k % 2, :]
                                      ).then_inc(c_out[k % 2], 16)

                tiles(act, step)
                for k in range(2):
                    act.wait_ge(c_out[k], 16 * ALL_TILES // 2)

            @block.tensor
            def _(pe):
                def step(n):
                    for k in range(R):
                        j = n * R + k
                        pe.wait_ge(c_sh, j + 1)
                        pe.wait_ge(c_t, held(j - 1))
                        pe.sem_inc(met_pe)
                        pe.transpose(psS[0:INNER, k % 2, 0:P], sh[:, k % 2, :], ident).then_inc(c_t_ps, 1)
                        pe.wait_ge(c_t, j + 1)
                        pe.wait_ge(c_fin, held(j - 1))
                        pe.matmul(psY[:, k % 2, 0:D], shT[:, k % 2, :], shd_w[:], start=True,
                                  stop=True).then_inc(c_y_ps, 1)

                tiles(pe, step)

            @block.vector
            def _(dve):
                def step(n):
                    for k in range(R):
                        j = n * R + k
                        dve.wait_ge(c_gate, j + 1)
                        dve.wait_ge(c_t_ps, held(j - 1))
                        dve.scalar_tensor_tensor(out=sh[:, k % 2, :], in0=gate[:, k % 2, :],
                                                 scalar=sgate[:, k % 2, :], in1=xs[:, k, D + INNER:D + 2 * INNER],
                                                 op0=ALU.mult, op1=ALU.mult).then_inc(c_sh, 1)
                        dve.wait_ge(c_in[k], 32 * (n + 1))
                        dve.tensor_reduce(acc[:, k % 2, :], yk[:, k].rearrange("p k h -> p h k"), AX.X,
                                          ALU.add).then_inc(c_acc, 1)
                        dve.wait_ge(c_acc, j + 1)
                        dve.tensor_tensor(acc2[:, k % 2, :], acc[:, k % 2, :], xs[:, k, 0:D], ALU.add
                                          ).then_inc(c_acc2, 1)
                        dve.wait_ge(c_acc2, j + 1)
                        dve.wait_ge(c_y_ps, j + 1)
                        dve.wait_ge(c_out[k % 2], held(16 * (n * 2 + k // 2)))
                        dve.tensor_tensor(fin[:, k % 2, :], psY[:, k % 2, 0:D], acc2[:, k % 2, :],
                                          ALU.add).then_inc(c_fin, 1)

                tiles(dve, step)


def constants():
    c = np.zeros((P, C_END), np.float32)
    p = np.arange(P)
    c[:, C_IDENT:C_IDENT + P] = np.eye(P)
    c[:, C_MASK1:C_MASK1 + P] = np.where(p[None, :] > p[:, None], MASKED, 0.0)
    c[:, C_MASK2:C_MASK2 + P] = np.where(p[:, None] > p[None, :], MASKED, 0.0)
    c[:, C_TRI:C_TRI + P] = p[:, None] < p[None, :]
    c[:, C_PIDX:C_PIDX + P] = p[:, None]
    i = np.arange(1, HEAD_D // 2 + 1, dtype=np.float32)
    thetas = np.float32(10000.0) ** (np.float32(-2.0) * (i - np.float32(1.0)) / np.float32(HEAD_D))
    ang = np.arange(1, SEQ + 1, dtype=np.float32)[:, None] * thetas.astype(np.float32)
    for at, table in ((C_COS, np.cos(ang)), (C_SIN, np.sin(ang)), (C_NSIN, -np.sin(ang))):
        c[:, at:at + TILES * 8] = table.astype(np.float32).reshape(TILES, P, 8).transpose(1, 0, 2).reshape(P, -1)
    c[:, C_BLK:C_BLK + BLOCKS] = P * np.arange(BLOCKS)
    token = np.arange(ALL_TILES)[None, :, None] * P + p[:, None, None]
    c[:, C_DSTC:C_END] = (token * TOP + np.arange(TOP) - SKIP).reshape(P, -1)
    return c


def kernel(**inputs):
    import concourse.bacc as _bacc
    from concourse.bass_utils import run_bass_kernel_spmd as _run

    a = {k.replace("L0_", ""): np.asarray(v) for k, v in inputs.items()}

    def rows(w):
        return np.ascontiguousarray(w.T.reshape(KC, P, -1).transpose(1, 0, 2))

    const = constants()
    const[:, C_BQKV:C_BQKV + QKV_D] = np.concatenate([a["attn_bq"], a["attn_bk"], a["attn_bv"]])[None, :]
    const[:, C_BO:C_BO + D] = a["attn_bo"][None, :]
    arrays = {
        "x_in": a["attn_x"],
        "const_in_d": const,
        "wqkv_in": rows(np.concatenate([a["attn_Wq"], a["attn_Wk"], a["attn_Wv"]])),
        "wo_in": rows(a["attn_Wo"]),
        "wroute_in": rows(np.concatenate([a["ffn_gate_w"], a["ffn_sh_gate_w"], a["ffn_sh_up_w"],
                                          a["ffn_sh_gate1_w"]])),
        "wgu_in": np.ascontiguousarray(
            a["ffn_gu_w"].reshape(EXPERTS, GU, KC, P).transpose(3, 0, 2, 1).reshape(P, -1)),
        "wdp_in": np.ascontiguousarray(a["ffn_dp_w"].transpose(2, 0, 1).reshape(INNER, -1)),
        "wshd_in": np.ascontiguousarray(a["ffn_sh_down_w"].T),
    }
    nc = _bacc.Bacc("TRN2", target_bir_lowering=False, num_devices=1)
    args = []
    for name, v in arrays.items():
        arrays[name] = np.ascontiguousarray(v)
        args.append(nc.dram_tensor(name, v.shape, mybir.dt.from_np(v.dtype), kind="ExternalInput").ap())
    args.append(nc.dram_tensor("out_d", (BATCH, SEQ, D), F32, kind="ExternalOutput").ap())
    build(nc, *args)
    r = _run(nc, [arrays], core_ids=[0])
    return r.results[0]["out_d"]
```

```python
from contextlib import ExitStack

import numpy as np

import concourse.bass as bass
from concourse import mybir

F32 = mybir.dt.float32
F32R = mybir.dt.float32r
BF16 = mybir.dt.bfloat16
I32 = mybir.dt.int32
U32 = mybir.dt.uint32
ALU = mybir.AluOpType
ACT = mybir.ActivationFunctionType
AX = mybir.AxisListType

P = 128
BATCH, SEQ, D = 8, 512, 256
HEADS, KV_HEADS, HEAD_D = 16, 4, 16
KV_D = KV_HEADS * HEAD_D
QK_D = D + KV_D
QKV_D = D + 2 * KV_D
PAIRS_OF_HEADS = HEADS // 2
TILES = SEQ // P
TOKENS = BATCH * SEQ
ALL_TILES = TOKENS // P
KC = D // P
EXPERTS, INNER, TOP = 64, 64, 8
GU = 2 * INNER
SHARED = 2 * INNER + 1
ROUTED = TOKENS * TOP
BLOCKS = ROUTED // P + EXPERTS
ROW = D + 3 * TOP
C_IDX, C_RW, C_DST = D, D + TOP, D + 2 * TOP
EPS = 1e-5
MASKED = -1e30
SKIP = 65536.0

C_IDENT, C_MASK1, C_MASK2, C_TRI, C_PIDX = 0, P, 2 * P, 3 * P, 4 * P
C_COS = 5 * P
C_SIN = C_COS + TILES * 8
C_NSIN = C_SIN + TILES * 8
C_BQKV = C_NSIN + TILES * 8
C_BO = C_BQKV + QKV_D
C_BLK = C_BO + D
C_DSTC = C_BLK + BLOCKS
C_DIGIT = C_DSTC + ALL_TILES * TOP
C_END = C_DIGIT + 4


def held(value):
    return max(value, 0) if isinstance(value, int) else value


def build(nc, x, const, wqkv, wo, wroute, wgu, wdp, wshd, out):
    rows_d = nc.dram_tensor("rows_d", (BLOCKS * P, ROW), F32, kind="Internal").ap()
    res_d = nc.dram_tensor("res_d", (ROUTED, D), F32, kind="Internal").ap()
    x2_d = nc.dram_tensor("x2_d", (TOKENS, D + SHARED), F32, kind="Internal").ap()
    x_v = x.rearrange("b (t p) h -> (b t) p h", p=P)
    x2_v = x2_d.rearrange("(t p) h -> t p h", p=P)

    with ExitStack() as top:
        sem = lambda n: top.enter_context(nc.semaphore(n))
        ksb = lambda n, s, d: top.enter_context(nc.sbuf_tensor(n, s, d))
        cst = ksb("cst", [P, C_END], F32)
        shd_w = ksb("shd_w", [P, D], F32)
        taken = ksb("taken", [EXPERTS, BLOCKS], F32)
        ident = cst[:, C_IDENT:C_IDENT + P]
        met_pe, met_dve, met_pool = sem("waits_met_pe"), sem("waits_met_dve"), sem("waits_met_pool")

        with ExitStack() as ctx:
            sb = lambda n, s, d: ctx.enter_context(nc.sbuf_tensor(n, s, d))
            ps = lambda n, s: ctx.enter_context(nc.psum_tensor(n, s, F32))
            two = lambda n, s, d: [sb(f"{n}{k}", s, d) for k in range(2)]
            wqkv_s = sb("wqkv_s", [P, KC, QKV_D], F32)
            wo_s = sb("wo_s", [P, KC, D], F32)
            wroute_s = sb("wroute_s", [P, KC, EXPERTS + SHARED], F32)
            ident_r = sb("ident_r", [P, P], F32R)
            ident_b = sb("ident_b", [P, P], BF16)
            mask1 = sb("mask1", [P, P], BF16)
            mask2 = sb("mask2", [P, P], BF16)
            tri_b = sb("tri_b", [P, P], BF16)
            ones_b = sb("ones_b", [P, P], BF16)
            ones_f = sb("ones_f", [P, P], F32)
            minus_half = sb("minus_half", [P, 1], F32)
            blank = sb("blank", [P, ROW], F32)
            xin = sb("xin", [P, TILES, D], F32)
            xr = two("xr", [P, D], F32)
            stat = two("stat", [P, 6], F32)
            mv = two("mv", [P, 2], F32)
            rstd = two("rstd", [P, 1], F32)
            xn = two("xn", [P, D], F32)
            xnT = two("xnT", [P, KC, P], F32)
            qkv = two("qkv", [P, QKV_D], F32)
            rot = two("rot", [P, QK_D // 16, 2, 8], F32)
            rope = two("rope", [P, QK_D // 16, 2, 8], F32)
            qs = two("qs", [P, PAIRS_OF_HEADS, 4, 32], F32R)
            ks = sb("ks", [P, KV_HEADS, 2, 4, 32], F32R)
            qT = two("qT", [P, PAIRS_OF_HEADS, SEQ], F32R)
            kT = two("kT", [P, 2 * KV_HEADS, SEQ], F32R)
            v1 = two("v1", [P, TILES, KV_HEADS, 32], F32)
            nmax = two("nmax", [P, TILES, 2], F32)
            mt = two("mt", [P, TILES, P], F32R)
            pexp = [sb(f"pexp{k}", [P, 5, SEQ], F32) for k in range(4)]
            oT = two("oT", [P, KV_HEADS, SEQ], F32)
            rden = two("rden", [P, HEADS], F32)
            yb = two("yb", [P, D], F32)
            yT = two("yT", [P, KC, P], F32)
            xb = two("xb", [P, D], F32)
            x2 = two("x2", [P, D + SHARED], F32)
            stat2 = two("stat2", [P, 6], F32)
            mv2 = two("mv2", [P, 2], F32)
            rstd2 = two("rstd2", [P, 1], F32)
            x2T = two("x2T", [P, KC, P], F32)
            pay = two("pay", [P, TILES, ROW], F32)
            logit = two("logit", [P, TILES, EXPERTS], F32)
            chosen = sb("chosen", [P, TILES, EXPERTS], BF16)
            topv = sb("topv", [P, TILES, TOP], F32)
            topi = sb("topi", [P, TILES, TOP], U32)
            etop = sb("etop", [P, TILES, TOP], F32)
            esum = sb("esum", [P, TILES, 1], F32)
            erec = sb("erec", [P, TILES, 1], F32)
            col = sb("col", [EXPERTS, 16], F32)
            diag = sb("diag", [EXPERTS, 3, EXPERTS], F32)
            thd = sb("thd", [P, 2, EXPERTS], F32)
            left = sb("left", [P, TILES, EXPERTS], F32)
            place = sb("place", [P, TILES, EXPERTS], F32)
            slot_f = sb("slot_f", [P, TILES, TOP], F32)
            slot_i = two("slot_i", [P, TILES, TOP], I32)

            ps1 = ps("ps1", [P, 2, SEQ])
            ps2 = ps("ps2", [P, 2, SEQ])
            psv = ps("psv", [P, SEQ])
            psp = ps("psp", [P, 2, SEQ])
            psq = ps("psq", [P, SEQ])

            (s_const, s_memset, s_conv, s_stat, s_ln1, s_rstd1, s_xn, s_xnT_ps, s_xnT, s_qkv_ps, s_qkv,
             s_rot, s_cosd, s_rope, s_v, s_hi, s_lo, s_split_ps, s_split, s_s1, s_red, s_msplit, s_m_ps,
             s_m, s_s2, s_exp, s_pv, s_oT, s_o_ps, s_rden, s_y, s_yT_ps, s_yT, s_att_ps, s_xb, s_x2, s_stat2,
             s_ln2, s_rstd2, s_x2n, s_x2T_ps, s_x2T, s_pre_ps, s_pre, s_top, s_left, s_chosen, s_shift, s_etop,
             s_esum, s_erec, s_rw, s_cnt_ps, s_cnt, s_new, s_base_ps, s_base, s_diag, s_rank_ps, s_thd, s_pl,
             s_slot, s_sloti, s_tk, s_pool, s_mhi, s_var1, s_var2) = [sem(n) for n in (
                 "const_in memsets consts_converted stats1 moments1 rstd1_ready xn_ready xnT_psum xnT_ready "
                 "qkv_psum qkv_ready rot_ready cos_done rope_ready v_ready hi_ready lo_ready split_psum split_ready "
                 "scores1_psum max_read max_split maxT_psum maxT_ready scores2_psum exp_done pv_psum oT_ready "
                 "o_psum den_ready y_ready yT_psum yT_ready att_psum xb_ready x2_ready stats2 moments2 rstd2_ready "
                 "x2n_ready x2nT_psum x2nT_ready preact_psum preact_ready top_ready left_ready chosen_ready "
                 "top_shifted top_exp exp_sum exp_recip weights_ready count_psum count_ready new_ready base_psum "
                 "base_ready diag_ready rank_psum rows_read place_chain slots_ready slot_ints taken_step "
                 "pool_chain max_hi var1_ready var2_ready").split()]
            s_x = [sem(f"x_in{k}") for k in range(TILES)]
            s_blank = [sem(f"blank_rows{k}") for k in range(8)]
            s_xr = [sem(f"x_again{k}") for k in range(2)]
            s_x2out = [sem(f"x2_out{k}") for k in range(2)]
            s_scat = [sem(f"scattered{k}") for k in range(2)]

            BLANKS = 8
            PIECE = BLOCKS // BLANKS

            def blanks_for(b):
                blocks = (b + 1) * SEQ * TOP // P + EXPERTS - 1
                return min(BLANKS, -(-blocks // PIECE))

            UNIT = 5
            SLOTS = PAIRS_OF_HEADS * UNIT
            PRE_AT, PRE_EVERY, PRE_PARTS = 2, 9, 11
            POST_AT, POST_EVERY, POST_PARTS = 11, 7, 8
            SCATTER_AT = 12

            def beat(steps, h, par, pre=True, main=True, behind=True, late=True):
                nxt = (h, 1) if par == 0 else (h + 1, 0)
                prv = (h, 0) if par == 1 else (h - 1, 1)
                for slot in range(SLOTS):
                    p, s = divmod(slot, UNIT)
                    ago = [((h, par, p - n) if main else None) if p >= n else
                           ((*prv, PAIRS_OF_HEADS + p - n) if behind else None) for n in (1, 2)]
                    steps["main"]((h, par, p) if main else None, *ago, s)
                    for t in reversed(range(TILES)):
                        k = slot - PRE_AT - PRE_EVERY * t
                        if pre and -PRE_AT <= k < PRE_PARTS:
                            steps["pre"](*nxt, t, k)
                    for t in reversed(range(TILES)):
                        k = slot - POST_AT - POST_EVERY * t
                        if behind and -1 <= k < POST_PARTS:
                            steps["post"](*prv, t, k)
                    if late and slot < SCATTER_AT:
                        steps["route"](h - 1, par, slot)
                    for n in range(TILES * TOP):
                        if late and slot == SCATTER_AT + n * (SLOTS - SCATTER_AT) // (TILES * TOP):
                            steps["scatter"](h - 1, par, n)
                    steps["products"](*ago, s)

            def program(eng, steps):
                for name in ("main", "pre", "post", "route", "scatter", "products"):
                    steps.setdefault(name, lambda *a: None)
                for slot in range(-PRE_AT, PRE_EVERY * (TILES - 1) + PRE_PARTS):
                    for t in reversed(range(TILES)):
                        if -PRE_AT <= slot - PRE_EVERY * t < PRE_PARTS:
                            steps["pre"](0, 0, t, slot - PRE_EVERY * t)
                half = BATCH // 2
                beat(steps, 0, 0, behind=False, late=False)
                beat(steps, 0, 1, late=False)
                beat(steps, 1, 0)
                with eng.Fori(1, half - 1) as h:
                    beat(steps, h, 1)
                    beat(steps, h + 1, 0)
                beat(steps, half - 1, 1, pre=False)
                beat(steps, half, 0, pre=False, main=False)
                beat(steps, half, 1, pre=False, main=False, behind=False)

            block = ctx.enter_context(nc.Block())

            @block.sync
            def _(sp):
                sp.dma_start(cst[:], const).then_inc(s_const, 16)
                sp.dma_start(wqkv_s[:], wqkv).then_inc(s_const, 16)
                sp.dma_start(wo_s[:], wo).then_inc(s_const, 16)
                sp.dma_start(wroute_s[:], wroute).then_inc(s_const, 16)
                sp.dma_start(shd_w[0:INNER, :], wshd).then_inc(s_const, 16)

                def pre(h, par, t, k):
                    tile = (h * 2 + par) * TILES + t
                    if k == -PRE_AT:
                        sp.wait_ge(s_xn, held(tile - TILES + 1))
                        sp.dma_start(xin[:, t, :], x_v[bass.ds(tile, 1)].rearrange("a p h -> p (a h)")
                                     ).then_inc(s_x[t], 16)

                def post(h, par, t, k):
                    tile = (h * 2 + par) * TILES + t
                    if k == 0:
                        sp.wait_ge(s_xb, held(tile - 1))
                        sp.dma_start(xr[t % 2][:], x_v[bass.ds(tile, 1)].rearrange("a p h -> p (a h)")
                                     ).then_inc(s_xr[t % 2], 16)
                    if k == 7:
                        sp.wait_ge(s_x2, tile + 1)
                        sp.wait_ge(s_pre, tile + 1)
                        sp.dma_start(x2_v[bass.ds(tile, 1)].rearrange("a p h -> p (a h)"), x2[t % 2][:]
                                     ).then_inc(s_x2out[t % 2], 16)

                program(sp, {"pre": pre, "post": post})
                sp.wait_ge(s_x2out[0], 16 * ALL_TILES // 2)
                sp.wait_ge(s_x2out[1], 16 * ALL_TILES // 2)

            @block.gpsimd
            def _(pool):
                pool.memset(blank[:, 0:C_IDX], 0.0)
                pool.memset(blank[:, C_IDX:C_RW], -1.0)
                pool.memset(blank[:, C_RW:ROW], 0.0)
                pool.memset(ones_f[:], 1.0)
                pool.memset(minus_half[:], -0.5)
                pool.memset(col[:], 0.0)
                pool.memset(taken[:], 0.0)
                pool.memset(ks[:].bitcast(F32), 0.0)
                for k in range(2):
                    pool.memset(v1[k][:], 0.0)
                    pool.memset(qs[k][:].bitcast(F32), 0.0)
                    pool.memset(mt[k][:].bitcast(F32), 0.0)
                pool.memset(ones_b[:], 1.0).then_inc(s_memset, 1)
                pool.wait_ge(s_memset, 1)
                for k in range(2):
                    pool.memset(v1[k][:, :, :, 16:17], 1.0)
                for ab in range(2):
                    pool.memset(ks[:, :, ab, 3, ab:ab + 1].bitcast(F32), 1.0)
                    last = pool.memset(ks[:, :, ab, 3, ab + 2:ab + 3].bitcast(F32), 1.0)
                last.then_inc(s_memset, 1)
                pool.wait_ge(s_const, 80)

                def pre(h, par, t, k):
                    tile, u = (h * 2 + par) * TILES + t, t % 2
                    if k == 0:
                        pool.wait_ge(s_ln1, tile + 1)
                        pool.sem_inc(met_pool)
                        pool.tensor_scalar(rstd[u][:], mv[u][:, 1:2], EPS, None, ALU.add).then_inc(s_var1, 1)
                        pool.wait_ge(s_var1, tile + 1)
                        pool.tensor_tensor(rstd[u][:], rstd[u][:], minus_half[:], ALU.pow).then_inc(s_rstd1, 1)
                    if k == 4:
                        pool.wait_ge(s_qkv, tile + 1)
                        pool.wait_ge(s_rope, held(tile - 1))
                        heads = qkv[u][:, 0:QK_D].rearrange("p (n a d) -> p n a d", a=2, d=8)
                        sin = lambda c: cst[:, c + 8 * t:c + 8 * t + 8].unsqueeze(1).to_broadcast([P, QK_D // 16, 8])
                        pool.tensor_tensor(rot[u][:, :, 0, :], heads[:, :, 1, :], sin(C_NSIN), ALU.mult)
                        pool.tensor_tensor(rot[u][:, :, 1, :], heads[:, :, 0, :], sin(C_SIN),
                                           ALU.mult).then_inc(s_rot, 1)

                def post(h, par, t, k):
                    tile, u = (h * 2 + par) * TILES + t, t % 2
                    if k == 1:
                        pool.wait_ge(s_xr[u], 16 * ((h * 2 + par) * 2 + t // 2 + 1))
                        pool.wait_ge(s_x2, held(tile - 1))
                        pool.tensor_tensor(xb[u][:], xr[u][:], cst[:, C_BO:C_BO + D], ALU.add).then_inc(s_xb, 1)
                    if k == 3:
                        pool.wait_ge(s_ln2, tile + 1)
                        pool.sem_inc(met_pool)
                        pool.tensor_scalar(rstd2[u][:], mv2[u][:, 1:2], EPS, None, ALU.add).then_inc(s_var2, 1)
                        pool.wait_ge(s_var2, tile + 1)
                        pool.tensor_tensor(rstd2[u][:], rstd2[u][:], minus_half[:], ALU.pow).then_inc(s_rstd2, 1)

                def route(h, par, k):
                    b = h * 2 + par
                    c = lambda k, n=1: col[:, k:k + n]

                    def chained(ins, step):
                        ins.then_inc(s_pool, 1)
                        pool.wait_ge(s_pool, b * STEPS + step)
                        pool.sem_inc(met_pool)

                    STEPS = 12
                    if k == 0:
                        pool.wait_ge(s_top, 4 * (b + 1))
                        pool.tensor_tensor(etop[:], topv[:], topv[:, :, 0:1].to_broadcast([P, TILES, TOP]),
                                           ALU.subtract).then_inc(s_shift, 1)
                        pool.tensor_copy(pay[par][:, :, C_IDX:C_IDX + TOP], topi[:])
                        pool.tensor_copy(pay[par][:, :, C_DST:C_DST + TOP],
                                         cst[:, bass.ds(C_DSTC + b * (TILES * TOP), TILES * TOP)]
                                         .rearrange("p (t k) -> p t k", k=TOP))
                    if k == 2:
                        pool.wait_ge(s_cnt, b + 1)
                        pool.sem_inc(met_pool)
                        chained(pool.tensor_scalar(c(5), c(4), P / 2 - 0.5, 1.0 / P, ALU.add, ALU.mult), 1)
                        chained(pool.tensor_scalar(c(5), c(5), 2.0 ** 23, None, ALU.add), 2)
                        chained(pool.tensor_scalar(c(6), c(5), -(2.0 ** 23), float(P), ALU.add, ALU.mult), 3)
                        pool.tensor_tensor(c(7), c(6), c(1), ALU.subtract).then_inc(s_new, 1)
                        chained(pool.tensor_scalar(c(12), c(0), c(2), 1.0, ALU.add, ALU.add), 4)
                        chained(pool.tensor_scalar(c(13), c(1), c(2), 1.0, ALU.add, ALU.add), 5)
                    if k == 4:
                        pool.wait_ge(s_erec, b + 1)
                        pool.tensor_tensor(pay[par][:, :, C_RW:C_RW + TOP], etop[:],
                                           erec[:].to_broadcast([P, TILES, TOP]), ALU.mult).then_inc(s_rw, 1)
                    if k == 5:
                        pool.wait_ge(s_base, b + 1)
                        chained(pool.tensor_tensor(c(10), c(8), c(1), ALU.subtract), 6)
                        chained(pool.tensor_tensor(c(14), c(10), c(2), ALU.subtract), 7)
                        pool.tensor_tensor(diag[:], cst[0:EXPERTS, C_IDENT:C_IDENT + EXPERTS].unsqueeze(1)
                                           .to_broadcast([EXPERTS, 3, EXPERTS]),
                                           c(12, 3).unsqueeze(2).to_broadcast([EXPERTS, 3, EXPERTS]),
                                           ALU.mult).then_inc(s_diag, 1)
                        chained(pool.tensor_tensor(c(9), c(8), c(7), ALU.add), 8)
                        chained(pool.tensor_scalar(c(11), c(7), 0.0, c(14), ALU.is_gt, ALU.mult), 9)
                        chained(pool.tensor_tensor(c(2), c(2), c(11), ALU.add), 10)
                        chained(pool.tensor_copy(c(0), c(4)), 11)
                        chained(pool.tensor_copy(c(1), c(6)), 12)
                    if k == 11:
                        pool.wait_ge(s_slot, b + 1)
                        pool.sem_inc(met_pool)
                        pool.tensor_scalar(slot_i[par][:], slot_f[:], -1.0, None, ALU.add).then_inc(s_sloti, 1)

                def scatter(h, par, n):
                    b = h * 2 + par
                    if n == 0:
                        pool.wait_ge(s_sloti, b + 1)
                        pool.wait_ge(s_rw, b + 1)
                        pool.sem_inc(met_pool)
                        for piece in range(blanks_for(b) if isinstance(b, int) else BLANKS):
                            pool.wait_ge(s_blank[piece], 16)
                    t, k = divmod(n, TOP)
                    pool.indirect_dma_start(
                        rows_d, bass.IndirectOffsetOnAxis(ap=slot_i[par][:, t, k:k + 1], axis=0),
                        pay[par][:, t, :], None).then_inc(s_scat[par], 16)

                program(pool, {"pre": pre, "post": post, "route": route, "scatter": scatter})
                for par in range(2):
                    pool.wait_ge(s_scat[par], 16 * TILES * TOP * BATCH // 2)

            @block.tensor
            def _(pe):
                pe.wait_ge(s_const, 80)
                pe.wait_ge(s_memset, 2)
                pe.wait_ge(s_conv, 1)

                def pre(h, par, t, k):
                    tile, u = (h * 2 + par) * TILES + t, t % 2
                    if k == 2:
                        pe.wait_ge(s_xn, tile + 1)
                        pe.wait_ge(s_split, held(4 * tile - 1))
                        for c in range(KC):
                            last = pe.transpose(psp[:, 0, c * P:(c + 1) * P], xn[u][:, c * P:(c + 1) * P], ident)
                        last.then_inc(s_xnT_ps, 1)
                    if k == 3:
                        pe.wait_ge(s_xnT, tile + 1)
                        pe.wait_ge(s_split, held(4 * tile))
                        for c in range(KC):
                            last = pe.matmul(psp[:, 1, 0:QKV_D], xnT[u][:, c, :], wqkv_s[:, c, :],
                                             start=(c == 0), stop=(c == KC - 1))
                        last.then_inc(s_qkv_ps, 1)
                    if k in (7, 8):
                        if k == 7:
                            pe.wait_ge(s_lo, tile + 1)
                            src = qs[u][:]
                        else:
                            src = ks[:].rearrange("p g a c d -> p (g a) c d")
                        for half in range(2):
                            if k == 8:
                                pe.wait_ge(s_split, 4 * tile + half + 1)
                            for n in range(4):
                                last = pe.transpose(psp[:, half, n * P:(n + 1) * P].bitcast(F32R),
                                                    src[:, 4 * half + n].rearrange("p c d -> p (c d)"), ident_r[:])
                            last.then_inc(s_split_ps, 1)

                def scores(h, par, p, bank, at, i, ab):
                    keys = (i + 1) * P
                    pe.matmul(ps1[:, bank, at:at + keys], qT[par][0:96, p, i * P:(i + 1) * P],
                              kT[par][0:96, 2 * (p // 2) + ab, 0:keys], start=True, stop=False)
                    return pe.matmul(ps1[:, bank, at + i * P:at + keys], ident_b[:], mask1[:],
                                     start=False, stop=True)

                def pass1(h, par, p, s):
                    U = (h * 2 + par) * PAIRS_OF_HEADS + p
                    if s == 0:
                        if p == 0:
                            pe.wait_ge(s_split, 16 * (h * 2 + par + 1))
                        pe.wait_ge(s_red, held(5 * U - 1))
                        scores(h, par, p, 0, 0, 3, 0).then_inc(s_s1, 1)
                    elif s == 1:
                        pe.wait_ge(s_red, held(5 * U))
                        scores(h, par, p, 1, 0, 3, 1).then_inc(s_s1, 1)
                    elif s in (2, 3):
                        if s == 2:
                            pe.wait_ge(s_red, 5 * U + 2)
                        else:
                            pe.wait_ge(s_red, 5 * U + 1)
                            pe.wait_ge(s_m, held(U))
                        scores(h, par, p, 3 - s, 0, 2, s - 2)
                        scores(h, par, p, 3 - s, 384, 0, s - 2).then_inc(s_s1, 1)
                    else:
                        pe.wait_ge(s_red, 5 * U + 3)
                        scores(h, par, p, 1, 0, 1, 0)
                        scores(h, par, p, 1, 256, 1, 1).then_inc(s_s1, 1)

                def max_up(h, par, p, beside):
                    U = (h * 2 + par) * PAIRS_OF_HEADS + p
                    pe.wait_ge(s_msplit, U + 1)
                    if beside:
                        pe.wait_ge(s_red, 5 * U + 6)
                    for i in range(TILES):
                        last = pe.transpose(ps1[:, 0, i * P:(i + 1) * P].bitcast(F32R), mt[p % 2][:, i, :], ident_r[:])
                    last.then_inc(s_m_ps, 1)

                def scoresT(h, par, p, bank, at, kt, ab):
                    n = SEQ - kt * P
                    pe.matmul(ps2[:, bank, at:at + n], kT[par][:, 2 * (p // 2) + ab, kt * P:(kt + 1) * P],
                              qT[par][:, p, kt * P:SEQ], start=True, stop=False)
                    return pe.matmul(ps2[:, bank, at:at + P], ident_b[:], mask2[:], start=False, stop=True)

                def pass2(h, par, p, s):
                    U = (h * 2 + par) * PAIRS_OF_HEADS + p
                    bank = (5 * p + s) % 2
                    pe.wait_ge(s_exp, held(5 * U + s - 1))
                    if s == 0:
                        pe.wait_ge(s_m, U + 1)
                    if s < 2:
                        scoresT(h, par, p, bank, 0, 0, s).then_inc(s_s2, 1)
                    elif s < 4:
                        scoresT(h, par, p, bank, 0, 1, s - 2)
                        scoresT(h, par, p, bank, 384, 3, s - 2).then_inc(s_s2, 1)
                    else:
                        scoresT(h, par, p, bank, 0, 2, 0)
                        scoresT(h, par, p, bank, 256, 2, 1).then_inc(s_s2, 1)

                def main(now, one, two, s):
                    if now:
                        pass1(*now, s)
                    if one and s == 1:
                        max_up(*one, now is not None)

                def products(one, two, s):
                    if s < 2 and two:
                        pass2(*two, s + 3)
                    if s >= 2 and one:
                        pass2(*one, s - 2)
                    if s >= 2 and two and two[2] % 2 == 1:
                        for kt in ((0,), (1,), (2, 3))[s - 2]:
                            pv(*two[0:2], two[2] // 2, kt)

                def pv(h, par, g, kt):
                    b = h * 2 + par
                    if kt == 0:
                        pe.wait_ge(s_exp, 5 * (b * PAIRS_OF_HEADS + 2 * g + 2))
                        pe.wait_ge(s_oT, held(b * KV_HEADS + g))
                        pe.wait_ge(s_v, 4 * (b + 1))
                    for hh in range(4):
                        ab = hh % 2
                        buf = pexp[(2 * g + hh // 2) % 4]
                        rhs = (buf[:, ab, :], buf[:, 2 + ab, 0:384], buf[:, 4, 256 * ab:256 * ab + 256],
                               buf[:, 2 + ab, 384:512])[kt]
                        last = pe.matmul(psv[32 * hh:32 * hh + 32, kt * P:SEQ], v1[par][:, kt, g, :], rhs,
                                         start=(kt == 0), stop=(kt == TILES - 1), skip_group_check=True)
                    if kt == TILES - 1:
                        last.then_inc(s_pv, 1)

                def post(h, par, t, k):
                    b = h * 2 + par
                    tile, u = b * TILES + t, t % 2
                    if k == 0:
                        pe.wait_ge(s_oT, 4 * (b + 1))
                        pe.wait_ge(s_pre, held(tile))
                        if t == 0:
                            pe.wait_ge(s_pl, held(b * 4))
                        for g in range(KV_HEADS):
                            last = pe.transpose(psq[:, g * P:(g + 1) * P], oT[par][:, g, t * P:(t + 1) * P], ident)
                        last.then_inc(s_o_ps, 1)
                    if k == 2:
                        pe.wait_ge(s_y, tile + 1)
                        for c in range(KC):
                            last = pe.transpose(psq[:, c * P:(c + 1) * P], yb[u][:, c * P:(c + 1) * P], ident)
                        last.then_inc(s_yT_ps, 1)
                    if k == 3:
                        pe.wait_ge(s_yT, tile + 1)
                        for c in range(KC):
                            last = pe.matmul(psq[:, 0:D], yT[u][:, c, :], wo_s[:, c, :],
                                             start=(c == 0), stop=(c == KC - 1))
                        last.then_inc(s_att_ps, 1)
                    if k == 5:
                        pe.wait_ge(s_x2n, tile + 1)
                        for c in range(KC):
                            last = pe.transpose(psq[:, c * P:(c + 1) * P], pay[par][:, t, c * P:(c + 1) * P], ident)
                        last.then_inc(s_x2T_ps, 1)
                    if k == 6:
                        pe.wait_ge(s_x2T, tile + 1)
                        for c in range(KC):
                            last = pe.matmul(psq[:, 0:EXPERTS + SHARED], x2T[u][:, c, :], wroute_s[:, c, :],
                                             start=(c == 0), stop=(c == KC - 1))
                        last.then_inc(s_pre_ps, 1)

                def route(h, par, k):
                    b = h * 2 + par
                    if k == 0:
                        pe.wait_ge(s_chosen, 4 * (b + 1))
                        pe.wait_ge(s_pre, 4 * (b + 1))
                        pe.sem_inc(met_pe)
                        for t in range(TILES):
                            last = pe.matmul(psq[0:EXPERTS, 0:1], chosen[:, t, :], ones_b[:, 0:1],
                                             start=(t == 0), stop=(t == TILES - 1))
                        last.then_inc(s_cnt_ps, 1)
                    if k == 3:
                        pe.wait_ge(s_new, b + 1)
                        pe.sem_inc(met_pe)
                        pe.matmul(psq[0:EXPERTS, 0:1], cst[0:EXPERTS, C_TRI:C_TRI + EXPERTS], col[:, 7:8],
                                  start=True, stop=True)
                        pe.matmul(psq[0:EXPERTS, 1:2], ones_f[0:EXPERTS, 0:EXPERTS], col[:, 7:8],
                                  start=True, stop=True).then_inc(s_base_ps, 1)
                    if k == 7:
                        pe.wait_ge(s_diag, b + 1)
                        pe.matmul(psq[:, 384:512], ones_f[0:EXPERTS, :], diag[:, 1:3, :].rearrange("p a e -> p (a e)"),
                                  start=True, stop=True)
                        for t in range(TILES):
                            at = psq[:, t * EXPERTS:(t + 1) * EXPERTS]
                            pe.matmul(at, ones_f[0:EXPERTS, :], diag[:, 0, :], start=True, stop=False)
                            for t0 in range(t):
                                pe.matmul(at, ones_b[:], chosen[:, t0, :], start=False, stop=False)
                            last = pe.matmul(at, tri_b[:], chosen[:, t, :], start=False, stop=True)
                        last.then_inc(s_rank_ps, 1)

                program(pe, {"pre": pre, "main": main, "products": products, "post": post, "route": route})

            @block.scalar
            def _(act):
                act.wait_ge(s_memset, 1)
                blanks = rows_d.rearrange("(n j p) r -> n p j r", p=P, j=PIECE)
                act.wait_ge(s_memset, 2)

                def pre(h, par, t, k):
                    b = h * 2 + par
                    tile, u = b * TILES + t, t % 2
                    if k == 2:
                        act.wait_ge(s_xnT_ps, tile + 1)
                        act.wait_ge(s_qkv_ps, held(tile - 1))
                        act.copy(xnT[u][:], psp[:, 0, 0:D].rearrange("p (k n) -> p k n", k=KC)).then_inc(s_xnT, 1)
                    if k == 5:
                        act.wait_ge(s_rope, tile + 1)
                        act.wait_ge(s_split_ps, held(4 * tile))
                        flat = rope[u][:].rearrange("p n a d -> p (n a d)")
                        act.copy(qs[u][:, :, 0:2, :], flat[:, 0:D].rearrange("p (n d) -> p n d", d=32).unsqueeze(2)
                                 .to_broadcast([P, PAIRS_OF_HEADS, 2, 32]))
                        kh = flat[:, D:QK_D].rearrange("p (g d) -> p g d", d=HEAD_D)
                        for ab in range(2):
                            dst = ks[:, :, ab, :, 16 * ab:16 * ab + 16]
                            last = act.copy(dst[:, :, 0, :], kh)
                            last = act.copy(dst[:, :, 2, :], kh)
                        last.then_inc(s_hi, 1)
                    if k in (7, 8):
                        if t == 0 and k == 7:
                            act.wait_ge(s_s2, held(40 * (b - 1)))
                        rows = 96 if k == 7 else P
                        for half in range(2):
                            act.wait_ge(s_split_ps, 4 * tile + 2 * (k - 7) + half + 1)
                            act.copy((qT if k == 7 else kT)[par][0:rows, 4 * half:4 * half + 4, t * P:(t + 1) * P],
                                     psp[0:rows, half, :].bitcast(F32R).rearrange("p (n c) -> p n c", n=4)
                                     ).then_inc(s_split, 1)
                    if k == 10:
                        act.wait_ge(s_qkv, tile + 1)
                        act.wait_ge(s_pv, held(KV_HEADS * (b - 1)))
                        act.copy(v1[par][:, t, :, 0:HEAD_D],
                                 qkv[u][:, QK_D:QKV_D].rearrange("p (g d) -> p g d", d=HEAD_D)).then_inc(s_v, 1)

                def exps(h, par, p, s):
                    b = h * 2 + par
                    U = b * PAIRS_OF_HEADS + p
                    if s == 0 and p % 2 == 0:
                        act.wait_ge(s_pv, held(b * KV_HEADS + p // 2 - 1))
                    act.wait_ge(s_s2, 5 * U + s + 1)
                    act.activation(pexp[p % 4][:, s, :], ps2[:, (5 * p + s) % 2, :], ACT.Exp,
                                   scale=HEAD_D ** -0.5).then_inc(s_exp, 1)

                def main(now, one, two, s):
                    if now and isinstance(now[0], int):
                        n, off = divmod(3 * ((now[0] * 2 + now[1]) * SLOTS + now[2] * UNIT + s), SLOTS)
                        if n < BLANKS and off < 3:
                            act.dma_start(blanks[n], blank[:].unsqueeze(1).to_broadcast([P, PIECE, ROW])
                                          ).then_inc(s_blank[n], 16)
                    if s == 1 and one:
                        h, par, p = one
                        act.wait_ge(s_m_ps, (h * 2 + par) * PAIRS_OF_HEADS + p + 1)
                        act.copy(qT[par][96:128, p, :], ps1[96:128, 0, :].bitcast(F32R)).then_inc(s_m, 1)
                    if s == 0 and two and two[2] in (2, 4, 6):
                        take_o(*two[0:2], two[2] // 2 - 1)

                def products(one, two, s):
                    if s < 2 and two:
                        exps(*two, s + 3)
                    if s >= 2 and one:
                        exps(*one, s - 2)

                def take_o(h, par, g):
                    b = h * 2 + par
                    act.wait_ge(s_pv, b * KV_HEADS + g + 1)
                    act.wait_ge(s_o_ps, held(TILES * (b - 1)))
                    act.copy(oT[par][:, g, :], psv[:]).then_inc(s_oT, 1)

                def post(h, par, t, k):
                    tile, u = (h * 2 + par) * TILES + t, t % 2
                    if t == 0 and k == -1:
                        take_o(h, par, KV_HEADS - 1)
                    if k == 2:
                        act.wait_ge(s_yT_ps, tile + 1)
                        act.copy(yT[u][:], psq[:, 0:D].rearrange("p (k n) -> p k n", k=KC)).then_inc(s_yT, 1)
                    if k == 5:
                        act.wait_ge(s_x2T_ps, tile + 1)
                        act.copy(x2T[u][:], psq[:, 0:D].rearrange("p (k n) -> p k n", k=KC)).then_inc(s_x2T, 1)
                    if k == 6:
                        act.wait_ge(s_pre_ps, tile + 1)
                        act.copy(logit[par][:, t, :], psq[:, 0:EXPERTS])
                        act.wait_ge(s_x2out[u], held(16 * ((h * 2 + par) * 2 + t // 2)))
                        act.copy(x2[u][:, D:D + SHARED], psq[:, EXPERTS:EXPERTS + SHARED]).then_inc(s_pre, 1)

                def route(h, par, k):
                    b = h * 2 + par
                    if k == 1:
                        act.wait_ge(s_shift, b + 1)
                        act.activation(etop[:], etop[:], ACT.Exp).then_inc(s_etop, 1)
                    if k == 8:
                        act.wait_ge(s_rank_ps, b + 1)
                        act.copy(thd[:], psq[:, 384:512].rearrange("p (a e) -> p a e", a=2)).then_inc(s_thd, 1)

                program(act, {"pre": pre, "main": main, "products": products, "post": post, "route": route})

            @block.vector
            def _(dve):
                dve.wait_ge(s_const, 80)
                dve.memset(shd_w[INNER:P, :], 0.0)
                dve.tensor_copy(ident_r[:], ident)
                dve.tensor_copy(ident_b[:], ident)
                dve.tensor_copy(mask1[:], cst[:, C_MASK1:C_MASK1 + P])
                dve.tensor_copy(mask2[:], cst[:, C_MASK2:C_MASK2 + P])
                dve.tensor_copy(tri_b[:], cst[:, C_TRI:C_TRI + P]).then_inc(s_conv, 1)
                dve.wait_ge(s_memset, 2)

                def pre(h, par, t, k):
                    tile, u = (h * 2 + par) * TILES + t, t % 2
                    if k == 0:
                        dve.wait_ge(s_x[t], 16 * (h * 2 + par + 1))
                        dve.bn_stats(stat[u][:], xin[:, t, :]).then_inc(s_stat, 1)
                        dve.wait_ge(s_stat, tile + 1)
                        dve.sem_inc(met_dve)
                        dve.bn_aggr(mv[u][:], stat[u][:]).then_inc(s_ln1, 1)
                    if k == 1:
                        dve.wait_ge(s_rstd1, tile + 1)
                        dve.wait_ge(s_ln1, tile + 1)
                        dve.wait_ge(s_xnT_ps, held(tile - 1))
                        dve.tensor_scalar(xn[u][:], xin[:, t, :], mv[u][:, 0:1], rstd[u][:], ALU.subtract,
                                          ALU.mult).then_inc(s_xn, 1)
                    if k == 3:
                        dve.wait_ge(s_qkv_ps, tile + 1)
                        dve.wait_ge(s_rot, held(tile - 1))
                        dve.wait_ge(s_v, held(tile - 1))
                        dve.tensor_tensor(qkv[u][:], psp[:, 1, 0:QKV_D], cst[:, C_BQKV:C_BQKV + QKV_D],
                                          ALU.add).then_inc(s_qkv, 1)
                    if k == 4:
                        dve.wait_ge(s_qkv, tile + 1)
                        dve.wait_ge(s_hi, held(tile - 1))
                        dve.tensor_tensor(rope[u][:], qkv[u][:, 0:QK_D].rearrange("p (n a d) -> p n a d", a=2, d=8),
                                          cst[:, C_COS + 8 * t:C_COS + 8 * t + 8].unsqueeze(1).unsqueeze(1)
                                          .to_broadcast([P, QK_D // 16, 2, 8]), ALU.mult).then_inc(s_cosd, 1)
                    if k == 5:
                        dve.wait_ge(s_cosd, tile + 1)
                        dve.wait_ge(s_rot, tile + 1)
                        dve.tensor_tensor(rope[u][:], rope[u][:], rot[u][:], ALU.add).then_inc(s_rope, 1)
                    if k == 6:
                        dve.wait_ge(s_hi, tile + 1)
                        flat = rope[u][:].rearrange("p n a d -> p (n a d)")
                        dve.tensor_tensor(qs[u][:, :, 2, :], flat[:, 0:D].rearrange("p (n d) -> p n d", d=32),
                                          qs[u][:, :, 0, :], ALU.subtract)
                        kf = flat[:, D:QK_D].rearrange("p (g d) -> p g d", d=HEAD_D)
                        for ab in range(2):
                            c = slice(16 * ab, 16 * ab + 16)
                            last = dve.tensor_tensor(ks[:, :, ab, 1, c], kf, ks[:, :, ab, 0, c], ALU.subtract)
                        last.then_inc(s_lo, 1)

                def main(now, one, two, s):
                    if not now:
                        return
                    h, par, p = now
                    U, u = (h * 2 + par) * PAIRS_OF_HEADS + p, p % 2

                    def largest(tile, bank, at, n, heads):
                        src = ps1[:, bank, at:at + n]
                        if len(heads) == 2:
                            src = src.rearrange("p (a n) -> p a n", a=2)
                        return dve.tensor_reduce(nmax[u][:, tile, heads[0]:heads[-1] + 1], src, AX.X, ALU.max,
                                                 negate=True)

                    dve.wait_ge(s_s1, 5 * U + s + 1)
                    if s < 2:
                        largest(3, s, 0, 512, [s]).then_inc(s_red, 1)
                    elif s < 4:
                        largest(2, 3 - s, 0, 384, [s - 2])
                        largest(0, 3 - s, 384, 128, [s - 2]).then_inc(s_red, 1)
                    else:
                        largest(1, 1, 0, 512, [0, 1]).then_inc(s_red, 1)
                        dve.wait_ge(s_red, 5 * U + 5)
                        dve.wait_ge(s_m_ps, held(U - 1))
                        dve.tensor_copy(mt[u][:, :, 96:98], nmax[u][:]).then_inc(s_mhi, 1)
                        dve.wait_ge(s_mhi, U + 1)
                        dve.tensor_tensor(mt[u][:, :, 98:100], nmax[u][:], mt[u][:, :, 96:98],
                                          ALU.subtract).then_inc(s_msplit, 1)

                def post(h, par, t, k):
                    b = h * 2 + par
                    tile, u = b * TILES + t, t % 2
                    if k == 0:
                        dve.wait_ge(s_o_ps, tile + 1)
                        heads = psq[:].rearrange("p (n d) -> p n d", d=32)
                        dve.reciprocal(rden[u][:], heads[:, :, HEAD_D]).then_inc(s_rden, 1)
                        dve.wait_ge(s_rden, tile + 1)
                        dve.wait_ge(s_yT_ps, held(tile - 1))
                        dve.tensor_tensor(yb[u][:].rearrange("p (n d) -> p n d", d=HEAD_D), heads[:, :, 0:HEAD_D],
                                          rden[u][:].unsqueeze(2).to_broadcast([P, HEADS, HEAD_D]),
                                          ALU.mult).then_inc(s_y, 1)
                    if k == 3:
                        dve.wait_ge(s_att_ps, tile + 1)
                        dve.wait_ge(s_xb, tile + 1)
                        dve.wait_ge(s_x2out[u], held(16 * (b * 2 + t // 2)))
                        dve.tensor_tensor(x2[u][:, 0:D], psq[:, 0:D], xb[u][:], ALU.add).then_inc(s_x2, 1)
                        dve.wait_ge(s_x2, tile + 1)
                        dve.bn_stats(stat2[u][:], x2[u][:, 0:D]).then_inc(s_stat2, 1)
                        dve.wait_ge(s_stat2, tile + 1)
                        dve.sem_inc(met_dve)
                        dve.bn_aggr(mv2[u][:], stat2[u][:]).then_inc(s_ln2, 1)
                    if k == 4:
                        dve.wait_ge(s_rstd2, tile + 1)
                        dve.wait_ge(s_ln2, tile + 1)
                        if t == 0:
                            dve.wait_ge(s_scat[par], held(16 * TILES * TOP * h))
                        dve.tensor_scalar(pay[par][:, t, 0:D], x2[u][:, 0:D], mv2[u][:, 0:1], rstd2[u][:],
                                          ALU.subtract, ALU.mult).then_inc(s_x2n, 1)
                    if k == 7:
                        dve.wait_ge(s_pre, tile + 1)
                        dve.wait_ge(s_rw, held(b))
                        dve.sem_inc(met_dve)
                        dve.max(topv[:, t, :], logit[par][:, t, :]).then_inc(s_left, 1)
                        dve.wait_ge(s_left, tile + 1)
                        dve.sem_inc(met_dve)
                        dve.max_index(topi[:, t, :], topv[:, t, :], logit[par][:, t, :])
                        dve.match_replace(left[:, t, :], topv[:, t, :], logit[par][:, t, :], -3e38).then_inc(s_top, 1)
                        dve.wait_ge(s_top, tile + 1)
                        dve.tensor_tensor(chosen[:, t, :], left[:, t, :], logit[par][:, t, :],
                                          ALU.not_equal).then_inc(s_chosen, 1)

                def route(h, par, k):
                    b = h * 2 + par
                    if k == 1:
                        dve.wait_ge(s_cnt_ps, b + 1)
                        dve.tensor_tensor(col[:, 4:5], psq[0:EXPERTS, 0:1], col[:, 0:1], ALU.add).then_inc(s_cnt, 1)
                    if k == 2:
                        dve.wait_ge(s_etop, b + 1)
                        dve.tensor_reduce(esum[:].rearrange("p t a -> p (t a)"), etop[:], AX.X,
                                          ALU.add).then_inc(s_esum, 1)
                        dve.wait_ge(s_esum, b + 1)
                        dve.reciprocal(erec[:], esum[:]).then_inc(s_erec, 1)
                    if k == 4:
                        dve.wait_ge(s_base_ps, b + 1)
                        dve.tensor_tensor(col[:, 8:9], psq[0:EXPERTS, 0:1], col[:, 3:4], ALU.add).then_inc(s_tk, 1)
                        dve.wait_ge(s_tk, 4 * b + 1)
                        dve.tensor_tensor(col[:, 3:4], psq[0:EXPERTS, 1:2], col[:, 3:4], ALU.add).then_inc(s_base, 1)
                    if k == 8:
                        dve.wait_ge(s_pool, 12 * b + 8)
                        blk = cst[0:EXPERTS, C_BLK:C_BLK + BLOCKS]
                        dve.scalar_tensor_tensor(out=taken[:], in0=blk, scalar=col[:, 8:9], in1=taken[:],
                                                 op0=ALU.is_ge, op1=ALU.subtract).then_inc(s_tk, 1)
                        dve.wait_ge(s_tk, 4 * b + 2)
                        dve.scalar_tensor_tensor(out=taken[:], in0=blk, scalar=col[:, 9:10], in1=taken[:],
                                                 op0=ALU.is_ge, op1=ALU.subtract).then_inc(s_tk, 2)
                    if k == 9:
                        dve.wait_ge(s_thd, b + 1)
                        rank = psq[:, 0:TILES * EXPERTS].rearrange("p (t e) -> p t e", e=EXPERTS)
                        wide = lambda a: thd[:, a, :].unsqueeze(1).to_broadcast([P, TILES, EXPERTS])
                        dve.tensor_tensor(place[:], rank, wide(0), ALU.is_ge).then_inc(s_pl, 1)
                        dve.wait_ge(s_pl, 4 * b + 1)
                        dve.tensor_tensor(place[:], place[:], wide(1), ALU.mult).then_inc(s_pl, 1)
                        dve.wait_ge(s_pl, 4 * b + 2)
                        dve.tensor_tensor(place[:], rank, place[:], ALU.add).then_inc(s_pl, 1)
                        dve.wait_ge(s_pl, 4 * b + 3)
                        dve.tensor_tensor(place[:], place[:], chosen[:], ALU.mult).then_inc(s_pl, 1)
                    if k == 10:
                        dve.wait_ge(s_pl, 4 * b + 4)
                        dve.sem_inc(met_dve)
                        for t in range(TILES):
                            last = dve.max(slot_f[:, t, :], place[:, t, :])
                        last.then_inc(s_slot, 1)

                program(dve, {"pre": pre, "main": main, "post": post, "route": route})

        with ExitStack() as ctx:
            sb = lambda n, s, d: ctx.enter_context(nc.sbuf_tensor(n, s, d))
            ps = lambda n, s: ctx.enter_context(nc.psum_tensor(n, s, F32))
            wgu_s = sb("wgu_s", [P, EXPERTS * KC * GU], F32)
            wdp_s = sb("wdp_s", [P, EXPERTS * D], F32)
            owner = sb("owner", [P, BLOCKS], F32)
            digits = sb("digits", [1, BLOCKS // 4, 4], F32)
            words_f = sb("words_f", [1, BLOCKS // 4], F32)
            words = sb("words", [1, BLOCKS // 4], I32)
            pidx_neg = sb("pidx_neg", [EXPERTS, P], F32)
            R = 4
            xg = sb("xg", [P, 2 * R, ROW], F32)
            xT = sb("xT", [P, 2, KC, P], F32)
            sg = sb("sg", [P, 2, INNER], F32)
            inner = sb("inner", [P, 2, P], F32)
            innerT = sb("innerT", [P, 2, P], F32)
            y = sb("y", [P, 2 * R, D], F32)
            hit = sb("hit", [P, 2, R, TOP], F32)
            hits = sb("hits", [P, 2, R, 2, TOP], F32)
            picked = sb("picked", [P, 2, R, 2], F32)
            dst_i = sb("dst_i", [P, 2 * R], I32)
            psA = ps("psA", [P, 2, SEQ])
            psB = ps("psB", [P, 2, SEQ])
            psC = ps("psC", [P, 2, SEQ])
            psD = ps("psD", [P, 2, SEQ])
            (e_w, e_neg, e_own_ps, e_own, e_words, e_a_ps, e_a, e_b_ps, e_sg, e_in, e_c_ps, e_c, e_d_ps, e_d,
             e_hit, e_hits, e_pick, e_dst, e_zero) = [sem(n) for n in (
                 "weights_in pidx_negated owner_psum owner_ready words_ready xgT_psum xgT_ready gu_psum silu_ready "
                 "inner_ready innerT_psum innerT_ready down_psum yrow_ready hit_ready hits_ready picked_ready "
                 "dst_ready zeros").split()]
            e_x = [sem(f"xg_in{k}") for k in range(2 * R)]
            e_out = [sem(f"y_out{k}") for k in range(2 * R)]
            ROUNDS = BLOCKS // (2 * R)
            block = ctx.enter_context(nc.Block())

            def rounds(eng, *stages):
                def blocks(n, ks):
                    for k in ks:
                        for behind, stage in stages:
                            back = k < behind
                            if (isinstance(n, int) and not 0 <= n * (2 * R) + k - behind < BLOCKS
                                    and stage.__name__ != "load_offsets"):
                                continue
                            stage(n - 1 if back else n, (k - behind) % (2 * R))

                blocks(0, range(2 * R))
                blocks(1, range(2 * R))
                with eng.Fori(2, ROUNDS) as n:
                    blocks(n, range(2 * R))
                blocks(ROUNDS, range(max(behind for behind, _ in stages)))

            @block.sync
            def _(sp):
                half = EXPERTS * KC * GU // 2
                sp.dma_start(wgu_s[:, 0:half], wgu[:, 0:half]).then_inc(e_w, 16)
                sp.dma_start(wgu_s[:, half:], wgu[:, half:]).then_inc(e_w, 16)
                sp.dma_start(wdp_s[0:INNER, :], wdp).then_inc(e_w, 16)
                rows_v = rows_d.rearrange("(j p) r -> j p r", p=P)

                def load(n, k):
                    j = n * (2 * R) + k
                    sp.wait_ge(e_a_ps, held(j - 2 * R + 1))
                    sp.wait_ge(e_pick, held(n * 2 - 1 + k // R))
                    sp.wait_ge(e_in, held(j - 2 * R + 1))
                    sp.dma_start(xg[:, k, :], rows_v[bass.ds(j, 1)].rearrange("a p r -> p (a r)")
                                 ).then_inc(e_x[k], 16)

                rounds(sp, (0, load))

            @block.vector
            def _(dve):
                dve.tensor_scalar(pidx_neg[:], cst[0:EXPERTS, C_PIDX:C_PIDX + P], -1.0, None,
                                  ALU.mult).then_inc(e_neg, 1)
                dve.wait_ge(e_own_ps, 1)
                dve.tensor_copy(owner[:], psA[:, 0, 0:BLOCKS]).then_inc(e_own, 1)
                dve.wait_ge(e_own, 1)
                dve.tensor_tensor(digits[:], owner[0:1, :].rearrange("o (w r) -> o w r", r=4),
                                  cst[0:1, C_DIGIT:C_END].unsqueeze(1).to_broadcast([1, BLOCKS // 4, 4]),
                                  ALU.mult).then_inc(e_words, 1)
                dve.wait_ge(e_words, 1)
                dve.tensor_reduce(words_f[:], digits[:], AX.X, ALU.add).then_inc(e_words, 1)
                dve.wait_ge(e_words, 2)
                dve.tensor_copy(words[:], words_f[:]).then_inc(e_words, 1)

                def pick(n, k):
                    if k % R != 0:
                        return
                    j, m = n * (2 * R) + k, k // R
                    q = n * 2 + m
                    for r in range(R):
                        dve.wait_ge(e_x[k + r], 16 * (n + 1))
                    own = owner[:, bass.ds(j, R)].unsqueeze(2).to_broadcast([P, R, TOP])
                    dve.tensor_tensor(hit[:, m], xg[:, k:k + R, C_IDX:C_IDX + TOP], own,
                                      ALU.is_equal).then_inc(e_hit, 1)
                    dve.wait_ge(e_hit, q + 1)
                    dve.tensor_tensor(hits[:, m], xg[:, k:k + R, C_RW:C_RW + 2 * TOP].rearrange(
                        "p r (a k) -> p r a k", a=2), hit[:, m].unsqueeze(2).to_broadcast([P, R, 2, TOP]),
                        ALU.mult).then_inc(e_hits, 1)
                    dve.wait_ge(e_hits, q + 1)
                    dve.tensor_reduce(picked[:, m], hits[:, m], AX.X, ALU.add).then_inc(e_pick, 1)

                def destine(n, k):
                    if k % R != 0:
                        return
                    m = k // R
                    dve.wait_ge(e_pick, n * 2 + m + 1)
                    for r in range(R):
                        dve.wait_ge(e_out[k + r], 16 * n)
                    dve.tensor_scalar(dst_i[:, k:k + R], picked[:, m, :, 1], SKIP, None, ALU.add).then_inc(e_dst, 1)

                def gated(n, k):
                    j = n * (2 * R) + k
                    dve.wait_ge(e_sg, j + 1)
                    dve.wait_ge(e_pick, n * 2 + k // R + 1)
                    dve.wait_ge(e_c_ps, held(j - 1))
                    dve.scalar_tensor_tensor(out=inner[:, k % 2, 0:INNER], in0=sg[:, k % 2, :],
                                             scalar=picked[:, k // R, k % R, 0:1], in1=psB[:, k % 2, INNER:GU],
                                             op0=ALU.mult, op1=ALU.mult).then_inc(e_in, 1)

                def innerT_copy(n, k):
                    j = n * (2 * R) + k
                    dve.wait_ge(e_c_ps, j + 1)
                    dve.wait_ge(e_d_ps, held(j - 1))
                    dve.tensor_copy(innerT[:, k % 2, :], psC[:, k % 2, 0:P]).then_inc(e_c, 1)

                rounds(dve, (2, innerT_copy), (1, gated), (3, destine), (0, pick))

            @block.scalar
            def _(act):
                def xT_copy(n, k):
                    j = n * (2 * R) + k
                    act.wait_ge(e_a_ps, j + 1)
                    act.wait_ge(e_b_ps, held(j - 1))
                    act.copy(xT[:, k % 2], psA[:, k % 2, 0:D].rearrange("p (k n) -> p k n", k=KC)).then_inc(e_a, 1)

                def silu(n, k):
                    j = n * (2 * R) + k
                    act.wait_ge(e_b_ps, j + 1)
                    act.wait_ge(e_in, held(j - 1))
                    act.activation(sg[:, k % 2, :], psB[:, k % 2, 0:INNER], ACT.Silu).then_inc(e_sg, 1)

                def y_copy(n, k):
                    j = n * (2 * R) + k
                    act.wait_ge(e_d_ps, j + 1)
                    act.wait_ge(e_out[k], 16 * n)
                    act.copy(y[:, k, :], psD[:, k % 2, 0:D]).then_inc(e_d, 1)

                rounds(act, (0, xT_copy), (1, silu), (3, y_copy))

            @block.tensor
            def _(pe):
                pe.wait_ge(e_neg, 1)
                pe.matmul(psA[:, 0, 0:BLOCKS], pidx_neg[:], taken[:], start=True, stop=True).then_inc(e_own_ps, 1)
                pe.wait_ge(e_words, 3)
                pe.wait_ge(e_w, 48)
                pe.wait_ge(e_zero, 2)

                offsets = {}

                def load_offsets(n, k):
                    if k == 0:
                        first = -1 if not isinstance(n, int) or n > 0 else 0
                        count = (0 if isinstance(n, int) and n == ROUNDS else 2) - first
                        _, values = nc.values_load_multi_w_load_instructions(
                            words[0:1, bass.ds(n * 2 + first, count)], engines=(mybir.EngineType.PE,),
                            min_val=0, max_val=EXPERTS ** 4 - 1)
                        for w in range(count):
                            for r in range(4):
                                offsets[4 * (first + w) + r] = ((values[w] >> (6 * r)) & (EXPERTS - 1)) * D

                def turn_x(n, k):
                    j = n * (2 * R) + k
                    pe.wait_ge(e_x[k], 16 * (n + 1))
                    pe.wait_ge(e_a, held(j - 1))
                    for c in range(KC):
                        last = pe.transpose(psA[:, k % 2, c * P:(c + 1) * P], xg[:, k, c * P:(c + 1) * P], ident)
                    last.then_inc(e_a_ps, 1)

                def gate_up(n, k):
                    j = n * (2 * R) + k
                    off = offsets[k - 2 * R if k >= 2 * R - 1 else k]
                    pe.wait_ge(e_a, j + 1)
                    pe.wait_ge(e_in, held(j - 1))
                    for c in range(KC):
                        last = pe.matmul(psB[:, k % 2, 0:GU], xT[:, k % 2, c, :], wgu_s[:, bass.ds(off + c * GU, GU)],
                                         start=(c == 0), stop=(c == KC - 1))
                    last.then_inc(e_b_ps, 1)

                def turn_inner(n, k):
                    j = n * (2 * R) + k
                    pe.wait_ge(e_in, j + 1)
                    pe.wait_ge(e_c, held(j - 1))
                    pe.transpose(psC[:, k % 2, 0:P], inner[:, k % 2, :], ident).then_inc(e_c_ps, 1)

                def down(n, k):
                    j = n * (2 * R) + k
                    off = offsets[k - 2 * R if k >= 2 * R - 3 else k]
                    pe.wait_ge(e_c, j + 1)
                    pe.wait_ge(e_d, held(j - 1))
                    pe.matmul(psD[:, k % 2, 0:D], innerT[:, k % 2, :], wdp_s[:, bass.ds(off, D)],
                              start=True, stop=True).then_inc(e_d_ps, 1)

                rounds(pe, (0, load_offsets), (0, turn_x), (1, gate_up), (2, turn_inner), (3, down))

            @block.gpsimd
            def _(pool):
                pool.memset(inner[:], 0.0).then_inc(e_zero, 1)
                pool.wait_ge(e_zero, 1)
                pool.memset(wdp_s[INNER:P, :], 0.0).then_inc(e_zero, 1)

                def scatter(n, k):
                    j = n * (2 * R) + k
                    pool.wait_ge(e_dst, n * 2 + k // R + 1)
                    pool.wait_ge(e_d, j + 1)
                    pool.sem_inc(met_pool)
                    pool.indirect_dma_start(
                        res_d, bass.IndirectOffsetOnAxis(ap=dst_i[:, k:k + 1], axis=0), y[:, k, :], None,
                        bounds_check=ROUTED - 1, oob_is_err=False).then_inc(e_out[k], 16)

                rounds(pool, (0, scatter))
                for k in range(2 * R):
                    pool.wait_ge(e_out[k], 16 * ROUNDS)

        with ExitStack() as ctx:
            sb = lambda n, s, d: ctx.enter_context(nc.sbuf_tensor(n, s, d))
            ps = lambda n, s: ctx.enter_context(nc.psum_tensor(n, s, F32))
            R = 4
            yk = sb("yk", [P, R, TOP, D], F32)
            xs = sb("xs", [P, R, D + SHARED], F32)
            sig = sb("sig", [P, 2, INNER + 1], F32)
            prod = sb("prod", [P, 2, INNER], F32)
            sh = sb("sh", [P, 2, P], F32)
            shT = sb("shT", [P, 2, P], F32)
            acc = sb("acc", [P, 2, D], F32)
            fin = sb("fin", [P, 2, D], F32)
            psS = ps("psS", [P, 2, SEQ])
            psY = ps("psY", [P, 2, SEQ])
            ON_PE = 2
            (c_zero, c_sig, c_prod, c_sh, c_t_ps, c_t, c_y_ps, c_acc, c_fin) = [sem(n) for n in (
                "zero_padding sigmoid_ready product_ready sh_ready shT_psum shT_ready added_psum sum_ready "
                "fin_ready").split()]
            c_in = [sem(f"yk_in{k}") for k in range(R)]
            c_out = [sem(f"fin_out{k}") for k in range(2)]
            block = ctx.enter_context(nc.Block())

            def tiles(eng, *stages):
                def some(n, ks):
                    for k in ks:
                        for behind, stage in stages:
                            if not isinstance(n, int) or 0 <= n * R + k - behind < ALL_TILES:
                                stage(n - 1 if k < behind else n, (k - behind) % R)

                some(0, range(R))
                with eng.Fori(1, ALL_TILES // R) as n:
                    some(n, range(R))
                some(ALL_TILES // R, range(max(behind for behind, _ in stages)))

            @block.sync
            def _(sp):
                res_v = res_d.rearrange("(t p k) h -> t p k h", p=P, k=TOP)

                def load(n, k):
                    j = n * R + k
                    sp.wait_ge(c_acc, held(j - R + 1))
                    sp.wait_ge(c_y_ps, held(j - R + 1))
                    sp.dma_start(yk[:, k], res_v[bass.ds(j, 1)].rearrange("a p k h -> p (a k) h")
                                 ).then_inc(c_in[k], 16)
                    sp.dma_start(xs[:, k], x2_v[bass.ds(j, 1)].rearrange("a p h -> p (a h)")
                                 ).then_inc(c_in[k], 16)

                tiles(sp, (0, load))

            @block.gpsimd
            def _(pool):
                pool.memset(sh[:], 0.0).then_inc(c_zero, 1)
                pool.wait_ge(c_zero, 1)
                pool.memset(shT[:], 0.0).then_inc(c_zero, 1)

            @block.scalar
            def _(act):
                out_v = out.rearrange("b (t p) h -> (b t) p h", p=P)

                def sigmoid(n, k):
                    j = n * R + k
                    act.wait_ge(c_in[k], 32 * (n + 1))
                    act.wait_ge(c_sh, held(j - 1))
                    act.activation(sig[:, k % 2, :], xs[:, k, D:D + INNER + 1], ACT.Sigmoid).then_inc(c_sig, 1)

                def shT_copy(n, k):
                    j = n * R + k
                    act.wait_ge(c_t_ps, j + 1)
                    act.wait_ge(c_y_ps, held(j - 1))
                    act.copy(shT[:, k % 2, :], psS[:, k % 2, 0:P]).then_inc(c_t, 1)

                def store(n, k):
                    j = n * R + k
                    act.wait_ge(c_fin, j + 1)
                    act.dma_start(out_v[bass.ds(j, 1)].rearrange("a p h -> p (a h)"), fin[:, k % 2, :]
                                  ).then_inc(c_out[k % 2], 16)

                tiles(act, (0, sigmoid), (1, shT_copy), (3, store))
                for k in range(2):
                    act.wait_ge(c_out[k], 16 * ALL_TILES // 2)

            @block.tensor
            def _(pe):
                pe.wait_ge(c_zero, 2)

                def turn(n, k):
                    j = n * R + k
                    pe.wait_ge(c_sh, j + 1)
                    pe.wait_ge(c_t, held(j - 1))
                    pe.transpose(psS[:, k % 2, 0:P], sh[:, k % 2, :], ident).then_inc(c_t_ps, 1)

                def add(n, k):
                    j = n * R + k
                    pe.wait_ge(c_in[k], 32 * (n + 1))
                    pe.wait_ge(c_fin, held(j - 1))
                    at = psY[:, k % 2, 0:D]
                    pe.matmul(at, ident, xs[:, k, 0:D], start=True, stop=False)
                    for c in range(ON_PE):
                        pe.matmul(at, ident, yk[:, k, c, :], start=False, stop=False)
                    pe.wait_ge(c_t, j + 1)
                    pe.matmul(at, shT[:, k % 2, :], shd_w[:], start=False, stop=True).then_inc(c_y_ps, 1)

                tiles(pe, (1, turn), (2, add))

            @block.vector
            def _(dve):
                dve.wait_ge(c_zero, 2)

                def gated(n, k):
                    j = n * R + k
                    dve.wait_ge(c_in[k], 32 * (n + 1))
                    dve.tensor_tensor(prod[:, k % 2, :], xs[:, k, D:D + INNER], xs[:, k, D + INNER + 1:D + SHARED],
                                      ALU.mult).then_inc(c_prod, 1)
                    dve.wait_ge(c_prod, j + 1)
                    dve.wait_ge(c_sig, j + 1)
                    dve.wait_ge(c_t_ps, held(j - 1))
                    dve.scalar_tensor_tensor(out=sh[:, k % 2, 0:INNER], in0=sig[:, k % 2, 0:INNER],
                                             scalar=sig[:, k % 2, INNER:INNER + 1], in1=prod[:, k % 2, :],
                                             op0=ALU.mult, op1=ALU.mult).then_inc(c_sh, 1)

                def total(n, k):
                    dve.wait_ge(c_in[k], 32 * (n + 1))
                    dve.tensor_reduce(acc[:, k % 2, :], yk[:, k, ON_PE:TOP].rearrange("p k h -> p h k"), AX.X,
                                      ALU.add).then_inc(c_acc, 1)

                def finish(n, k):
                    j = n * R + k
                    dve.wait_ge(c_acc, j + 1)
                    dve.wait_ge(c_y_ps, j + 1)
                    dve.wait_ge(c_out[k % 2], held(16 * (n * 2 + k // 2)))
                    dve.tensor_tensor(fin[:, k % 2, :], psY[:, k % 2, 0:D], acc[:, k % 2, :], ALU.add
                                      ).then_inc(c_fin, 1)

                tiles(dve, (0, gated), (2, finish), (1, total))


def constants():
    c = np.zeros((P, C_END), np.float32)
    p = np.arange(P)
    c[:, C_IDENT:C_IDENT + P] = np.eye(P)
    c[:, C_MASK1:C_MASK1 + P] = np.where(p[None, :] > p[:, None], MASKED, 0.0)
    c[:, C_MASK2:C_MASK2 + P] = np.where(p[:, None] > p[None, :], MASKED, 0.0)
    c[:, C_TRI:C_TRI + P] = p[:, None] < p[None, :]
    c[:, C_PIDX:C_PIDX + P] = p[:, None]
    i = np.arange(1, HEAD_D // 2 + 1, dtype=np.float32)
    thetas = np.float32(10000.0) ** (np.float32(-2.0) * (i - np.float32(1.0)) / np.float32(HEAD_D))
    ang = np.arange(1, SEQ + 1, dtype=np.float32)[:, None] * thetas.astype(np.float32)
    for at, table in ((C_COS, np.cos(ang)), (C_SIN, np.sin(ang)), (C_NSIN, -np.sin(ang))):
        c[:, at:at + TILES * 8] = table.astype(np.float32).reshape(TILES, P, 8).transpose(1, 0, 2).reshape(P, -1)
    c[:, C_BLK:C_BLK + BLOCKS] = P * np.arange(BLOCKS)
    token = np.arange(ALL_TILES)[None, :, None] * P + p[:, None, None]
    c[:, C_DIGIT:C_END] = float(EXPERTS) ** np.arange(4)
    c[:, C_DSTC:C_DIGIT] = (token * TOP + np.arange(TOP) - SKIP).reshape(P, -1)
    return c


def kernel(**inputs):
    import concourse.bacc as _bacc
    from concourse.bass_utils import run_bass_kernel_spmd as _run

    a = {k.replace("L0_", ""): np.asarray(v) for k, v in inputs.items()}

    def rows(w):
        return np.ascontiguousarray(w.T.reshape(KC, P, -1).transpose(1, 0, 2))

    const = constants()
    const[:, C_BQKV:C_BQKV + QKV_D] = np.concatenate([a["attn_bq"], a["attn_bk"], a["attn_bv"]])[None, :]
    const[:, C_BO:C_BO + D] = a["attn_bo"][None, :]
    arrays = {
        "x_in": a["attn_x"],
        "const_in_d": const,
        "wqkv_in": rows(np.concatenate([a["attn_Wq"], a["attn_Wk"], a["attn_Wv"]])),
        "wo_in": rows(a["attn_Wo"]),
        "wroute_in": rows(np.concatenate([a["ffn_gate_w"], a["ffn_sh_gate_w"], a["ffn_sh_gate1_w"],
                                          a["ffn_sh_up_w"]])),
        "wgu_in": np.ascontiguousarray(
            a["ffn_gu_w"].reshape(EXPERTS, GU, KC, P).transpose(3, 0, 2, 1).reshape(P, -1)),
        "wdp_in": np.ascontiguousarray(a["ffn_dp_w"].transpose(2, 0, 1).reshape(INNER, -1)),
        "wshd_in": np.ascontiguousarray(a["ffn_sh_down_w"].T),
    }
    nc = _bacc.Bacc("TRN2", target_bir_lowering=False, num_devices=1)
    args = []
    for name, v in arrays.items():
        arrays[name] = np.ascontiguousarray(v)
        args.append(nc.dram_tensor(name, v.shape, mybir.dt.from_np(v.dtype), kind="ExternalInput").ap())
    args.append(nc.dram_tensor("out_d", (BATCH, SEQ, D), F32, kind="ExternalOutput").ap())
    build(nc, *args)
    r = _run(nc, [arrays], core_ids=[0])
    return r.results[0]["out_d"]
```

```python
from contextlib import ExitStack

import numpy as np

import concourse.bass as bass
from concourse import mybir

F32 = mybir.dt.float32
F32R = mybir.dt.float32r
BF16 = mybir.dt.bfloat16
I32 = mybir.dt.int32
U32 = mybir.dt.uint32
ALU = mybir.AluOpType
ACT = mybir.ActivationFunctionType
AX = mybir.AxisListType

P = 128
BATCH, SEQ, D = 8, 512, 256
HEADS, KV_HEADS, HEAD_D = 16, 4, 16
KV_D = KV_HEADS * HEAD_D
QK_D = D + KV_D
QKV_D = D + 2 * KV_D
PAIRS_OF_HEADS = HEADS // 2
TILES = SEQ // P
TOKENS = BATCH * SEQ
ALL_TILES = TOKENS // P
KC = D // P
EXPERTS, INNER, TOP = 64, 64, 8
GU = 2 * INNER
SHARED = 2 * INNER + 1
ROUTED = TOKENS * TOP
BLOCKS = ROUTED // P + EXPERTS
ROW = D + 3 * TOP
C_IDX, C_RW, C_DST = D, D + TOP, D + 2 * TOP
EPS = 1e-5
MASKED = -1e30
SKIP = 65536.0

C_IDENT, C_MASK1, C_MASK2, C_TRI, C_PIDX = 0, P, 2 * P, 3 * P, 4 * P
C_COS = 5 * P
C_SIN = C_COS + TILES * 8
C_NSIN = C_SIN + TILES * 8
C_BQKV = C_NSIN + TILES * 8
C_BO = C_BQKV + QKV_D
C_BLK = C_BO + D
C_DSTC = C_BLK + BLOCKS
C_DIGIT = C_DSTC + ALL_TILES * TOP
C_END = C_DIGIT + 4


def held(value):
    return max(value, 0) if isinstance(value, int) else value


def build(nc, x, const, wqkv, wo, wroute, wgu, wdp, wshd, out):
    rows_d = nc.dram_tensor("rows_d", (BLOCKS * P, ROW), F32, kind="Internal").ap()
    res_d = nc.dram_tensor("res_d", (ROUTED, D), F32, kind="Internal").ap()
    x2_d = nc.dram_tensor("x2_d", (TOKENS, D + SHARED), F32, kind="Internal").ap()
    x_v = x.rearrange("b (t p) h -> (b t) p h", p=P)
    x2_v = x2_d.rearrange("(t p) h -> t p h", p=P)

    with ExitStack() as top:
        sem = lambda n: top.enter_context(nc.semaphore(n))
        ksb = lambda n, s, d: top.enter_context(nc.sbuf_tensor(n, s, d))
        cst = ksb("cst", [P, C_END], F32)
        shd_w = ksb("shd_w", [P, D], F32)
        taken = ksb("taken", [EXPERTS, BLOCKS], F32)
        ident = cst[:, C_IDENT:C_IDENT + P]
        wgu_s = ksb("wgu_s", [P, EXPERTS * KC * GU], F32)
        e_w = sem("weights_in")
        waits_met = sem("waits_met")

        with ExitStack() as ctx:
            sb = lambda n, s, d: ctx.enter_context(nc.sbuf_tensor(n, s, d))
            ps = lambda n, s: ctx.enter_context(nc.psum_tensor(n, s, F32))
            two = lambda n, s, d: [sb(f"{n}{k}", s, d) for k in range(2)]
            taken_up = [0]

            def room(*shape):
                at = taken_up[0]
                taken_up[0] += int(np.prod(shape))
                names = "abcd"[:len(shape)]
                return wgu_s[:, at:taken_up[0]].rearrange(
                    f"p ({' '.join(names)}) -> p {' '.join(names)}", **dict(zip(names[1:], shape[1:])))

            pexp = [room(5, SEQ) for _ in range(4)]
            v1 = [room(TILES, KV_HEADS, 32) for _ in range(2)]
            xin = room(TILES, D)
            xn = [room(D) for _ in range(2)]
            xnT = [room(KC, P) for _ in range(2)]
            qkv = [room(QKV_D) for _ in range(2)]
            rot = [room(QK_D // 16, 2, 8) for _ in range(2)]
            rope = [room(QK_D // 16, 2, 8) for _ in range(2)]
            wqkv_s = room(KC, QKV_D)
            qT = two("qT", [P, PAIRS_OF_HEADS, SEQ], F32R)
            kT = two("kT", [P, 2 * KV_HEADS, SEQ], F32R)
            mt = two("mt", [P, TILES, P], F32R)
            qs = two("qs", [P, PAIRS_OF_HEADS, 4, 32], F32R)
            ks = sb("ks", [P, KV_HEADS, 2, 4, 32], F32R)
            wo_s = sb("wo_s", [P, KC, D], F32)
            wroute_s = sb("wroute_s", [P, KC, EXPERTS + SHARED], F32)
            ident_r = sb("ident_r", [P, P], F32R)
            ident_b = sb("ident_b", [P, P], BF16)
            mask1 = sb("mask1", [P, P], BF16)
            mask2 = sb("mask2", [P, P], BF16)
            tri_b = sb("tri_b", [P, P], BF16)
            ones_b = sb("ones_b", [P, P], BF16)
            ones_f = sb("ones_f", [P, P], F32)
            minus_half = sb("minus_half", [P, 1], F32)
            blank = sb("blank", [P, ROW], F32)
            xr = two("xr", [P, D], F32)
            stat = two("stat", [P, 6], F32)
            mv = two("mv", [P, 2], F32)
            rstd = two("rstd", [P, 1], F32)
            nmax = two("nmax", [P, TILES, 2], F32)
            oT = two("oT", [P, KV_HEADS, SEQ], F32)
            rden = two("rden", [P, HEADS], F32)
            yb = two("yb", [P, D], F32)
            yT = two("yT", [P, KC, P], F32)
            xb = two("xb", [P, D], F32)
            x2 = two("x2", [P, D + SHARED], F32)
            stat2 = two("stat2", [P, 6], F32)
            mv2 = two("mv2", [P, 2], F32)
            rstd2 = two("rstd2", [P, 1], F32)
            x2T = two("x2T", [P, KC, P], F32)
            pay = two("pay", [P, TILES, ROW], F32)
            logit = two("logit", [P, TILES, EXPERTS], F32)
            chosen = sb("chosen", [P, TILES, EXPERTS], BF16)
            topv = sb("topv", [P, TILES, TOP], F32)
            topi = sb("topi", [P, TILES, TOP], U32)
            etop = sb("etop", [P, TILES, TOP], F32)
            esum = sb("esum", [P, TILES, 1], F32)
            erec = sb("erec", [P, TILES, 1], F32)
            col = sb("col", [EXPERTS, 16], F32)
            diag = sb("diag", [EXPERTS, 3, EXPERTS], F32)
            thd = sb("thd", [P, 2, EXPERTS], F32)
            left = sb("left", [P, TILES, EXPERTS], F32)
            place = sb("place", [P, TILES, EXPERTS], F32)
            slot_f = sb("slot_f", [P, TILES, TOP], F32)
            slot_i = two("slot_i", [P, TILES, TOP], I32)

            ps1 = ps("ps1", [P, 2, SEQ])
            ps2 = ps("ps2", [P, 2, SEQ])
            psv = ps("psv", [P, SEQ])
            psp = ps("psp", [P, 2, SEQ])
            psq = ps("psq", [P, SEQ])

            (s_const, s_memset, s_conv, s_stat, s_ln1, s_rstd1, s_xn, s_xnT_ps, s_xnT, s_qkv_ps, s_qkv,
             s_rot, s_cosd, s_rope, s_v, s_hi, s_lo, s_split_ps, s_split, s_s1, s_red, s_msplit, s_m_ps,
             s_m, s_s2, s_exp, s_pv, s_oT, s_o_ps, s_rden, s_y, s_yT_ps, s_yT, s_att_ps, s_xb, s_x2, s_stat2,
             s_ln2, s_rstd2, s_x2n, s_x2T_ps, s_x2T, s_pre_ps, s_pre, s_top, s_left, s_chosen, s_shift, s_etop,
             s_esum, s_erec, s_rw, s_cnt_ps, s_cnt, s_new, s_base_ps, s_base, s_diag, s_rank_ps, s_thd, s_pl,
             s_slot, s_sloti, s_tk, s_pool, s_mhi, s_var1, s_var2) = [sem(n) for n in (
                 "const_in memsets consts_converted stats1 moments1 rstd1_ready xn_ready xnT_psum xnT_ready "
                 "qkv_psum qkv_ready rot_ready cos_done rope_ready v_ready hi_ready lo_ready split_psum split_ready "
                 "scores1_psum max_read max_split maxT_psum maxT_ready scores2_psum exp_done pv_psum oT_ready "
                 "o_psum den_ready y_ready yT_psum yT_ready att_psum xb_ready x2_ready stats2 moments2 rstd2_ready "
                 "x2n_ready x2nT_psum x2nT_ready preact_psum preact_ready top_ready left_ready chosen_ready "
                 "top_shifted top_exp exp_sum exp_recip weights_ready count_psum count_ready new_ready base_psum "
                 "base_ready diag_ready rank_psum rows_read place_chain slots_ready slot_ints taken_step "
                 "pool_chain max_hi var1_ready var2_ready").split()]
            s_late = sem("later_consts_in")
            s_x = [sem(f"x_in{k}") for k in range(TILES)]
            s_blank = [sem(f"blank_rows{k}") for k in range(8)]
            s_xr = [sem(f"x_again{k}") for k in range(2)]
            s_x2out = [sem(f"x2_out{k}") for k in range(2)]
            s_scat = [sem(f"scattered{k}") for k in range(2)]

            BLANKS = 8
            PIECE = BLOCKS // BLANKS

            def blanks_for(b):
                blocks = (b + 1) * SEQ * TOP // P + EXPERTS - 1
                return min(BLANKS, -(-blocks // PIECE))

            UNIT = 5
            SLOTS = PAIRS_OF_HEADS * UNIT
            PRE_AT, PRE_EVERY, PRE_PARTS = 2, 9, 11
            POST_AT, POST_EVERY, POST_PARTS = 11, 7, 8
            SCATTER_AT = 12

            FIRST_EVERY = 5

            def banks(h, par, t):
                first = isinstance(h, int) and h * 2 + par == 0
                return (ps1 if first and t % 2 else psp), (2 if first and t else 1)

            def beat(steps, h, par, pre=True, main=True, behind=True, late=True):
                nxt = (h, 1) if par == 0 else (h + 1, 0)
                prv = (h, 0) if par == 1 else (h - 1, 1)
                for slot in range(SLOTS):
                    p, s = divmod(slot, UNIT)
                    ago = [((h, par, p - n) if main else None) if p >= n else
                           ((*prv, PAIRS_OF_HEADS + p - n) if behind else None) for n in (1, 2)]
                    if late and slot < SCATTER_AT:
                        steps["route"](h - 1, par, slot)
                    for n in range(TILES * TOP):
                        if late and slot == SCATTER_AT + n * (SLOTS - SCATTER_AT) // (TILES * TOP):
                            steps["scatter"](h - 1, par, n)
                    for t in reversed(range(TILES)):
                        k = slot - PRE_AT - PRE_EVERY * t
                        if pre and -PRE_AT <= k < PRE_PARTS:
                            steps["pre"](*nxt, t, k)
                    steps["main"]((h, par, p) if main else None, *ago, s)
                    for t in reversed(range(TILES)):
                        k = slot - POST_AT - POST_EVERY * t
                        if behind and -1 <= k < POST_PARTS:
                            steps["post"](*prv, t, k)
                    steps["products"](*ago, s)

            def program(eng, steps):
                for name in ("main", "pre", "post", "route", "scatter", "products"):
                    steps.setdefault(name, lambda *a: None)
                for slot in range(-PRE_AT, FIRST_EVERY * (TILES - 1) + PRE_PARTS):
                    for t in range(TILES):
                        if -PRE_AT <= slot - FIRST_EVERY * t < PRE_PARTS:
                            steps["pre"](0, 0, t, slot - FIRST_EVERY * t)
                half = BATCH // 2
                beat(steps, 0, 0, behind=False, late=False)
                beat(steps, 0, 1, late=False)
                beat(steps, 1, 0)
                with eng.Fori(1, half - 1) as h:
                    beat(steps, h, 1)
                    beat(steps, h + 1, 0)
                beat(steps, half - 1, 1, pre=False)
                beat(steps, half, 0, pre=False, main=False)
                beat(steps, half, 1, pre=False, main=False, behind=False)

            block = ctx.enter_context(nc.Block())

            @block.sync
            def _(sp):
                for t in range(TILES):
                    sp.dma_start(xin[:, t, :], x_v[t]).then_inc(s_x[t], 16)
                sp.dma_start(cst[:], const).then_inc(s_const, 16)
                sp.dma_start(wqkv_s[:], wqkv).then_inc(s_const, 16)
                sp.dma_start(wo_s[:], wo).then_inc(s_late, 16)
                sp.dma_start(wroute_s[:], wroute).then_inc(s_late, 16)
                sp.dma_start(shd_w[0:INNER, :], wshd).then_inc(s_late, 16)

                def pre(h, par, t, k):
                    tile = (h * 2 + par) * TILES + t
                    if k == -PRE_AT and not (isinstance(h, int) and h * 2 + par == 0):
                        sp.wait_ge(s_xn, held(tile - TILES + 1))
                        sp.dma_start(xin[:, t, :], x_v[bass.ds(tile, 1)].rearrange("a p h -> p (a h)")
                                     ).then_inc(s_x[t], 16)

                def post(h, par, t, k):
                    tile = (h * 2 + par) * TILES + t
                    if k == 0:
                        sp.wait_ge(s_xb, held(tile - 1))
                        sp.dma_start(xr[t % 2][:], x_v[bass.ds(tile, 1)].rearrange("a p h -> p (a h)")
                                     ).then_inc(s_xr[t % 2], 16)
                    if k == 7:
                        sp.wait_ge(s_x2, tile + 1)
                        sp.wait_ge(s_pre, tile + 1)
                        sp.dma_start(x2_v[bass.ds(tile, 1)].rearrange("a p h -> p (a h)"), x2[t % 2][:]
                                     ).then_inc(s_x2out[t % 2], 16)

                program(sp, {"pre": pre, "post": post})
                sp.wait_ge(s_x2out[0], 16 * ALL_TILES // 2)
                sp.wait_ge(s_x2out[1], 16 * ALL_TILES // 2)

            @block.gpsimd
            def _(pool):
                pool.memset(blank[:, 0:C_IDX], 0.0)
                pool.memset(blank[:, C_IDX:C_RW], -1.0)
                pool.memset(blank[:, C_RW:ROW], 0.0)
                pool.memset(ones_f[:], 1.0)
                pool.memset(minus_half[:], -0.5)
                pool.memset(col[:], 0.0)
                pool.memset(taken[:], 0.0)
                pool.memset(ks[:].bitcast(F32), 0.0)
                for k in range(2):
                    pool.memset(v1[k][:], 0.0)
                    pool.memset(qs[k][:].bitcast(F32), 0.0)
                    pool.memset(mt[k][:].bitcast(F32), 0.0)
                pool.memset(ones_b[:], 1.0).then_inc(s_memset, 1)
                pool.wait_ge(s_memset, 1)
                for k in range(2):
                    pool.memset(v1[k][:, :, :, 16:17], 1.0)
                for ab in range(2):
                    pool.memset(ks[:, :, ab, 3, ab:ab + 1].bitcast(F32), 1.0)
                    last = pool.memset(ks[:, :, ab, 3, ab + 2:ab + 3].bitcast(F32), 1.0)
                last.then_inc(s_memset, 1)
                pool.wait_ge(s_const, 32)

                def pre(h, par, t, k):
                    tile, u = (h * 2 + par) * TILES + t, t % 2
                    if k == 0:
                        pool.wait_ge(s_ln1, tile + 1)
                        pool.sem_inc(waits_met)
                        pool.tensor_scalar(rstd[u][:], mv[u][:, 1:2], EPS, None, ALU.add).then_inc(s_var1, 1)
                        pool.wait_ge(s_var1, tile + 1)
                        pool.tensor_tensor(rstd[u][:], rstd[u][:], minus_half[:], ALU.pow).then_inc(s_rstd1, 1)
                    if k == 4:
                        pool.wait_ge(s_qkv, tile + 1)
                        pool.wait_ge(s_rope, held(tile - 1))
                        heads = qkv[u][:, 0:QK_D].rearrange("p (n a d) -> p n a d", a=2, d=8)
                        sin = lambda c: cst[:, c + 8 * t:c + 8 * t + 8].unsqueeze(1).to_broadcast([P, QK_D // 16, 8])
                        pool.tensor_tensor(rot[u][:, :, 0, :], heads[:, :, 1, :], sin(C_NSIN), ALU.mult)
                        pool.tensor_tensor(rot[u][:, :, 1, :], heads[:, :, 0, :], sin(C_SIN),
                                           ALU.mult).then_inc(s_rot, 1)

                def post(h, par, t, k):
                    tile, u = (h * 2 + par) * TILES + t, t % 2
                    if k == 1:
                        pool.wait_ge(s_xr[u], 16 * ((h * 2 + par) * 2 + t // 2 + 1))
                        pool.wait_ge(s_x2, held(tile - 1))
                        pool.tensor_tensor(xb[u][:], xr[u][:], cst[:, C_BO:C_BO + D], ALU.add).then_inc(s_xb, 1)
                    if k == 2:
                        pool.wait_ge(s_ln2, tile + 1)
                        pool.sem_inc(waits_met)
                        pool.tensor_scalar(rstd2[u][:], mv2[u][:, 1:2], EPS, None, ALU.add).then_inc(s_var2, 1)
                        pool.wait_ge(s_var2, tile + 1)
                        pool.tensor_tensor(rstd2[u][:], rstd2[u][:], minus_half[:], ALU.pow).then_inc(s_rstd2, 1)

                def route(h, par, k):
                    b = h * 2 + par
                    c = lambda k, n=1: col[:, k:k + n]

                    def chained(ins, step):
                        ins.then_inc(s_pool, 1)
                        pool.wait_ge(s_pool, b * STEPS + step)
                        pool.sem_inc(waits_met)

                    STEPS = 12
                    if k == 0:
                        pool.wait_ge(s_top, 4 * (b + 1))
                        pool.tensor_tensor(etop[:], topv[:], topv[:, :, 0:1].to_broadcast([P, TILES, TOP]),
                                           ALU.subtract).then_inc(s_shift, 1)
                        pool.tensor_copy(pay[par][:, :, C_IDX:C_IDX + TOP], topi[:])
                        pool.tensor_copy(pay[par][:, :, C_DST:C_DST + TOP],
                                         cst[:, bass.ds(C_DSTC + b * (TILES * TOP), TILES * TOP)]
                                         .rearrange("p (t k) -> p t k", k=TOP))
                    if k == 2:
                        pool.wait_ge(s_cnt, b + 1)
                        pool.sem_inc(waits_met)
                        chained(pool.tensor_scalar(c(5), c(4), P / 2 - 0.5, 1.0 / P, ALU.add, ALU.mult), 1)
                        chained(pool.tensor_scalar(c(5), c(5), 2.0 ** 23, None, ALU.add), 2)
                        chained(pool.tensor_scalar(c(6), c(5), -(2.0 ** 23), float(P), ALU.add, ALU.mult), 3)
                        pool.tensor_tensor(c(7), c(6), c(1), ALU.subtract).then_inc(s_new, 1)
                        chained(pool.tensor_scalar(c(12), c(0), c(2), 1.0, ALU.add, ALU.add), 4)
                        chained(pool.tensor_scalar(c(13), c(1), c(2), 1.0, ALU.add, ALU.add), 5)
                    if k == 4:
                        pool.wait_ge(s_erec, b + 1)
                        pool.tensor_tensor(pay[par][:, :, C_RW:C_RW + TOP], etop[:],
                                           erec[:].to_broadcast([P, TILES, TOP]), ALU.mult).then_inc(s_rw, 1)
                    if k == 5:
                        pool.wait_ge(s_base, b + 1)
                        chained(pool.tensor_tensor(c(10), c(8), c(1), ALU.subtract), 6)
                        chained(pool.tensor_tensor(c(14), c(10), c(2), ALU.subtract), 7)
                        pool.tensor_tensor(diag[:], cst[0:EXPERTS, C_IDENT:C_IDENT + EXPERTS].unsqueeze(1)
                                           .to_broadcast([EXPERTS, 3, EXPERTS]),
                                           c(12, 3).unsqueeze(2).to_broadcast([EXPERTS, 3, EXPERTS]),
                                           ALU.mult).then_inc(s_diag, 1)
                        chained(pool.tensor_tensor(c(9), c(8), c(7), ALU.add), 8)
                        chained(pool.tensor_scalar(c(11), c(7), 0.0, c(14), ALU.is_gt, ALU.mult), 9)
                        chained(pool.tensor_tensor(c(2), c(2), c(11), ALU.add), 10)
                        chained(pool.tensor_copy(c(0), c(4)), 11)
                        chained(pool.tensor_copy(c(1), c(6)), 12)
                    if k == 11:
                        pool.wait_ge(s_slot, b + 1)
                        pool.sem_inc(waits_met)
                        pool.tensor_scalar(slot_i[par][:], slot_f[:], -1.0, None, ALU.add).then_inc(s_sloti, 1)

                def scatter(h, par, n):
                    b = h * 2 + par
                    if n == 0:
                        pool.wait_ge(s_sloti, b + 1)
                        pool.wait_ge(s_rw, b + 1)
                        pool.sem_inc(waits_met)
                        for piece in range(blanks_for(b) if isinstance(b, int) else BLANKS):
                            pool.wait_ge(s_blank[piece], 16)
                    t, k = divmod(n, TOP)
                    pool.indirect_dma_start(
                        rows_d, bass.IndirectOffsetOnAxis(ap=slot_i[par][:, t, k:k + 1], axis=0),
                        pay[par][:, t, :], None).then_inc(s_scat[par], 16)

                program(pool, {"pre": pre, "post": post, "route": route, "scatter": scatter})
                for par in range(2):
                    pool.wait_ge(s_scat[par], 16 * TILES * TOP * BATCH // 2)

            @block.tensor
            def _(pe):
                pe.wait_ge(s_const, 32)
                pe.wait_ge(s_memset, 2)
                pe.wait_ge(s_conv, 1)

                def pre(h, par, t, k):
                    tile, u = (h * 2 + par) * TILES + t, t % 2
                    psp, ago = banks(h, par, t)
                    if k == 2:
                        pe.wait_ge(s_xn, tile + 1)
                        pe.wait_ge(s_split, held(4 * (tile - ago + 1) - 1))
                        for c in range(KC):
                            last = pe.transpose(psp[:, 0, c * P:(c + 1) * P], xn[u][:, c * P:(c + 1) * P], ident)
                        last.then_inc(s_xnT_ps, 1)
                    if k == 3:
                        pe.wait_ge(s_xnT, tile + 1)
                        pe.wait_ge(s_split, held(4 * (tile - ago + 1)))
                        for c in range(KC):
                            last = pe.matmul(psp[:, 1, 0:QKV_D], xnT[u][:, c, :], wqkv_s[:, c, :],
                                             start=(c == 0), stop=(c == KC - 1))
                        last.then_inc(s_qkv_ps, 1)
                    if k in (9, 10):
                        if k == 9:
                            pe.wait_ge(s_lo, tile + 1)
                            src = qs[u][:]
                        else:
                            src = ks[:].rearrange("p g a c d -> p (g a) c d")
                        for half in range(2):
                            if k == 10:
                                pe.wait_ge(s_split, 4 * tile + half + 1)
                            for n in range(4):
                                last = pe.transpose(psp[:, half, n * P:(n + 1) * P].bitcast(F32R),
                                                    src[:, 4 * half + n].rearrange("p c d -> p (c d)"), ident_r[:])
                            last.then_inc(s_split_ps, 1)

                def scores(h, par, p, bank, at, i, ab):
                    keys = (i + 1) * P
                    pe.matmul(ps1[:, bank, at:at + keys], qT[par][0:96, p, i * P:(i + 1) * P],
                              kT[par][0:96, 2 * (p // 2) + ab, 0:keys], start=True, stop=False)
                    return pe.matmul(ps1[:, bank, at + i * P:at + keys], ident_b[:], mask1[:],
                                     start=False, stop=True)

                def pass1(h, par, p, s):
                    U = (h * 2 + par) * PAIRS_OF_HEADS + p
                    if s == 0:
                        if p == 0:
                            pe.wait_ge(s_split, 16 * (h * 2 + par + 1))
                        pe.wait_ge(s_red, held(5 * U - 1))
                        scores(h, par, p, 0, 0, 3, 0).then_inc(s_s1, 1)
                    elif s == 1:
                        pe.wait_ge(s_red, held(5 * U))
                        scores(h, par, p, 1, 0, 3, 1).then_inc(s_s1, 1)
                    elif s in (2, 3):
                        if s == 2:
                            pe.wait_ge(s_red, 5 * U + 2)
                        else:
                            pe.wait_ge(s_red, 5 * U + 1)
                            pe.wait_ge(s_m, held(U))
                        scores(h, par, p, 3 - s, 0, 2, s - 2)
                        scores(h, par, p, 3 - s, 384, 0, s - 2).then_inc(s_s1, 1)
                    else:
                        pe.wait_ge(s_red, 5 * U + 3)
                        scores(h, par, p, 1, 0, 1, 0)
                        scores(h, par, p, 1, 256, 1, 1).then_inc(s_s1, 1)

                def max_up(h, par, p, beside):
                    U = (h * 2 + par) * PAIRS_OF_HEADS + p
                    pe.wait_ge(s_msplit, U + 1)
                    if beside:
                        pe.wait_ge(s_red, 5 * U + 6)
                    for i in range(TILES):
                        last = pe.transpose(ps1[:, 0, i * P:(i + 1) * P].bitcast(F32R), mt[p % 2][:, i, :], ident_r[:])
                    last.then_inc(s_m_ps, 1)

                def scoresT(h, par, p, bank, at, kt, ab):
                    n = SEQ - kt * P
                    pe.matmul(ps2[:, bank, at:at + n], kT[par][:, 2 * (p // 2) + ab, kt * P:(kt + 1) * P],
                              qT[par][:, p, kt * P:SEQ], start=True, stop=False)
                    return pe.matmul(ps2[:, bank, at:at + P], ident_b[:], mask2[:], start=False, stop=True)

                def pass2(h, par, p, s):
                    U = (h * 2 + par) * PAIRS_OF_HEADS + p
                    bank = (5 * p + s) % 2
                    pe.wait_ge(s_exp, held(5 * U + s - 1))
                    if s == 0:
                        pe.wait_ge(s_m, U + 1)
                    if s < 2:
                        scoresT(h, par, p, bank, 0, 0, s).then_inc(s_s2, 1)
                    elif s < 4:
                        scoresT(h, par, p, bank, 0, 1, s - 2)
                        scoresT(h, par, p, bank, 384, 3, s - 2).then_inc(s_s2, 1)
                    else:
                        scoresT(h, par, p, bank, 0, 2, 0)
                        scoresT(h, par, p, bank, 256, 2, 1).then_inc(s_s2, 1)

                def main(now, one, two, s):
                    if now:
                        pass1(*now, s)
                    if one and s == 1:
                        max_up(*one, now is not None)

                def products(one, two, s):
                    if s < 2 and two:
                        pass2(*two, s + 3)
                    if s >= 2 and one:
                        pass2(*one, s - 2)
                    if s >= 2 and two and two[2] % 2 == 1:
                        for kt in ((0,), (1,), (2, 3))[s - 2]:
                            pv(*two[0:2], two[2] // 2, kt)

                def pv(h, par, g, kt):
                    b = h * 2 + par
                    if kt == 0:
                        pe.wait_ge(s_exp, 5 * (b * PAIRS_OF_HEADS + 2 * g + 2))
                        pe.wait_ge(s_oT, held(b * KV_HEADS + g))
                        pe.wait_ge(s_v, 4 * (b + 1))
                    for hh in range(4):
                        ab = hh % 2
                        buf = pexp[(2 * g + hh // 2) % 4]
                        rhs = (buf[:, ab, :], buf[:, 2 + ab, 0:384], buf[:, 4, 256 * ab:256 * ab + 256],
                               buf[:, 2 + ab, 384:512])[kt]
                        last = pe.matmul(psv[32 * hh:32 * hh + 32, kt * P:SEQ], v1[par][:, kt, g, :], rhs,
                                         start=(kt == 0), stop=(kt == TILES - 1), skip_group_check=True)
                    if kt == TILES - 1:
                        last.then_inc(s_pv, 1)

                def post(h, par, t, k):
                    b = h * 2 + par
                    tile, u = b * TILES + t, t % 2
                    if k == 0:
                        if isinstance(b, int) and tile == 0:
                            pe.wait_ge(s_late, 48)
                        pe.wait_ge(s_oT, 4 * (b + 1))
                        pe.wait_ge(s_pre, held(tile))
                        if t == 0:
                            pe.wait_ge(s_pl, held(b * 4))
                        for g in range(KV_HEADS):
                            last = pe.transpose(psq[:, g * P:(g + 1) * P], oT[par][:, g, t * P:(t + 1) * P], ident)
                        last.then_inc(s_o_ps, 1)
                    if k == 1:
                        pe.wait_ge(s_y, tile + 1)
                        for c in range(KC):
                            last = pe.transpose(psq[:, c * P:(c + 1) * P], yb[u][:, c * P:(c + 1) * P], ident)
                        last.then_inc(s_yT_ps, 1)
                    if k == 2:
                        pe.wait_ge(s_yT, tile + 1)
                        for c in range(KC):
                            last = pe.matmul(psq[:, 0:D], yT[u][:, c, :], wo_s[:, c, :],
                                             start=(c == 0), stop=(c == KC - 1))
                        last.then_inc(s_att_ps, 1)
                    if k == 5:
                        pe.wait_ge(s_x2n, tile + 1)
                        for c in range(KC):
                            last = pe.transpose(psq[:, c * P:(c + 1) * P], pay[par][:, t, c * P:(c + 1) * P], ident)
                        last.then_inc(s_x2T_ps, 1)
                    if k == 6:
                        pe.wait_ge(s_x2T, tile + 1)
                        for c in range(KC):
                            last = pe.matmul(psq[:, 0:EXPERTS + SHARED], x2T[u][:, c, :], wroute_s[:, c, :],
                                             start=(c == 0), stop=(c == KC - 1))
                        last.then_inc(s_pre_ps, 1)

                def route(h, par, k):
                    b = h * 2 + par
                    if k == 0:
                        pe.wait_ge(s_chosen, 4 * (b + 1))
                        pe.wait_ge(s_pre, 4 * (b + 1))
                        pe.sem_inc(waits_met)
                        for t in range(TILES):
                            last = pe.matmul(psq[0:EXPERTS, 0:1], chosen[:, t, :], ones_b[:, 0:1],
                                             start=(t == 0), stop=(t == TILES - 1))
                        last.then_inc(s_cnt_ps, 1)
                    if k == 3:
                        pe.wait_ge(s_new, b + 1)
                        pe.sem_inc(waits_met)
                        pe.matmul(psq[0:EXPERTS, 0:1], cst[0:EXPERTS, C_TRI:C_TRI + EXPERTS], col[:, 7:8],
                                  start=True, stop=True)
                        pe.matmul(psq[0:EXPERTS, 1:2], ones_f[0:EXPERTS, 0:EXPERTS], col[:, 7:8],
                                  start=True, stop=True).then_inc(s_base_ps, 1)
                    if k == 7:
                        pe.wait_ge(s_diag, b + 1)
                        pe.matmul(psq[:, 384:512], ones_f[0:EXPERTS, :], diag[:, 1:3, :].rearrange("p a e -> p (a e)"),
                                  start=True, stop=True)
                        for t in range(TILES):
                            at = psq[:, t * EXPERTS:(t + 1) * EXPERTS]
                            pe.matmul(at, ones_f[0:EXPERTS, :], diag[:, 0, :], start=True, stop=False)
                            for t0 in range(t):
                                pe.matmul(at, ones_b[:], chosen[:, t0, :], start=False, stop=False)
                            last = pe.matmul(at, tri_b[:], chosen[:, t, :], start=False, stop=True)
                        last.then_inc(s_rank_ps, 1)

                program(pe, {"pre": pre, "main": main, "products": products, "post": post, "route": route})

            @block.scalar
            def _(act):
                act.wait_ge(s_memset, 1)
                blanks = rows_d.rearrange("(n j p) r -> n p j r", p=P, j=PIECE)
                act.wait_ge(s_memset, 2)

                def pre(h, par, t, k):
                    b = h * 2 + par
                    tile, u = b * TILES + t, t % 2
                    psp, _ = banks(h, par, t)
                    if k == 2:
                        act.wait_ge(s_xnT_ps, tile + 1)
                        act.wait_ge(s_qkv_ps, held(tile - 1))
                        act.copy(xnT[u][:], psp[:, 0, 0:D].rearrange("p (k n) -> p k n", k=KC)).then_inc(s_xnT, 1)
                    if k == 7:
                        act.wait_ge(s_rope, tile + 1)
                        act.wait_ge(s_split_ps, held(4 * tile))
                        flat = rope[u][:].rearrange("p n a d -> p (n a d)")
                        act.copy(qs[u][:, :, 0:2, :], flat[:, 0:D].rearrange("p (n d) -> p n d", d=32).unsqueeze(2)
                                 .to_broadcast([P, PAIRS_OF_HEADS, 2, 32]))
                        kh = flat[:, D:QK_D].rearrange("p (g d) -> p g d", d=HEAD_D)
                        for ab in range(2):
                            dst = ks[:, :, ab, :, 16 * ab:16 * ab + 16]
                            last = act.copy(dst[:, :, 0, :], kh)
                            last = act.copy(dst[:, :, 2, :], kh)
                        last.then_inc(s_hi, 1)
                    if k in (9, 10):
                        if t == 0 and k == 9:
                            act.wait_ge(s_s2, held(40 * (b - 1)))
                        rows = 96 if k == 9 else P
                        for half in range(2):
                            act.wait_ge(s_split_ps, 4 * tile + 2 * (k - 9) + half + 1)
                            act.copy((qT if k == 9 else kT)[par][0:rows, 4 * half:4 * half + 4, t * P:(t + 1) * P],
                                     psp[0:rows, half, :].bitcast(F32R).rearrange("p (n c) -> p n c", n=4)
                                     ).then_inc(s_split, 1)
                    if k == 10:
                        act.wait_ge(s_qkv, tile + 1)
                        act.wait_ge(s_pv, held(KV_HEADS * (b - 1)))
                        act.copy(v1[par][:, t, :, 0:HEAD_D],
                                 qkv[u][:, QK_D:QKV_D].rearrange("p (g d) -> p g d", d=HEAD_D)).then_inc(s_v, 1)

                def exps(h, par, p, s):
                    b = h * 2 + par
                    U = b * PAIRS_OF_HEADS + p
                    if s == 0 and p % 2 == 0:
                        act.wait_ge(s_pv, held(b * KV_HEADS + p // 2 - 1))
                    act.wait_ge(s_s2, 5 * U + s + 1)
                    act.activation(pexp[p % 4][:, s, :], ps2[:, (5 * p + s) % 2, :], ACT.Exp,
                                   scale=HEAD_D ** -0.5).then_inc(s_exp, 1)

                def main(now, one, two, s):
                    if now and isinstance(now[0], int):
                        n, off = divmod(3 * ((now[0] * 2 + now[1]) * SLOTS + now[2] * UNIT + s), SLOTS)
                        if n < BLANKS and off < 3:
                            act.dma_start(blanks[n], blank[:].unsqueeze(1).to_broadcast([P, PIECE, ROW])
                                          ).then_inc(s_blank[n], 16)
                    if s == 1 and one:
                        h, par, p = one
                        act.wait_ge(s_m_ps, (h * 2 + par) * PAIRS_OF_HEADS + p + 1)
                        act.copy(qT[par][96:128, p, :], ps1[96:128, 0, :].bitcast(F32R)).then_inc(s_m, 1)
                    if s == 0 and two and two[2] in (2, 4, 6):
                        take_o(*two[0:2], two[2] // 2 - 1)

                def products(one, two, s):
                    if s < 2 and two:
                        exps(*two, s + 3)
                    if s >= 2 and one:
                        exps(*one, s - 2)

                def take_o(h, par, g):
                    b = h * 2 + par
                    act.wait_ge(s_pv, b * KV_HEADS + g + 1)
                    act.wait_ge(s_o_ps, held(TILES * (b - 1)))
                    act.copy(oT[par][:, g, :], psv[:]).then_inc(s_oT, 1)

                def post(h, par, t, k):
                    tile, u = (h * 2 + par) * TILES + t, t % 2
                    if t == 0 and k == -1:
                        take_o(h, par, KV_HEADS - 1)
                    if k in (0, 3) and isinstance(h, int) and h * 2 + par == BATCH - 1:
                        act.wait_ge(s_pv, BATCH * KV_HEADS)
                        part, width = t * 2 + k // 3, EXPERTS * KC * GU // (2 * TILES)
                        act.dma_start(wgu_s[:, part * width:(part + 1) * width],
                                      wgu[:, part * width:(part + 1) * width]).then_inc(e_w, 16)
                    if k == 1:
                        act.wait_ge(s_yT_ps, tile + 1)
                        act.copy(yT[u][:], psq[:, 0:D].rearrange("p (k n) -> p k n", k=KC)).then_inc(s_yT, 1)
                    if k == 5:
                        act.wait_ge(s_x2T_ps, tile + 1)
                        act.copy(x2T[u][:], psq[:, 0:D].rearrange("p (k n) -> p k n", k=KC)).then_inc(s_x2T, 1)
                    if k == 6:
                        act.wait_ge(s_pre_ps, tile + 1)
                        act.copy(logit[par][:, t, :], psq[:, 0:EXPERTS])
                        act.wait_ge(s_x2out[u], held(16 * ((h * 2 + par) * 2 + t // 2)))
                        act.copy(x2[u][:, D:D + SHARED], psq[:, EXPERTS:EXPERTS + SHARED]).then_inc(s_pre, 1)

                def route(h, par, k):
                    b = h * 2 + par
                    if k == 1:
                        act.wait_ge(s_shift, b + 1)
                        act.activation(etop[:], etop[:], ACT.Exp).then_inc(s_etop, 1)
                    if k == 8:
                        act.wait_ge(s_rank_ps, b + 1)
                        act.copy(thd[:], psq[:, 384:512].rearrange("p (a e) -> p a e", a=2)).then_inc(s_thd, 1)

                program(act, {"pre": pre, "main": main, "products": products, "post": post, "route": route})

            @block.vector
            def _(dve):
                dve.wait_ge(s_const, 32)
                dve.memset(shd_w[INNER:P, :], 0.0)
                dve.tensor_copy(ident_r[:], ident)
                dve.tensor_copy(ident_b[:], ident)
                dve.tensor_copy(mask1[:], cst[:, C_MASK1:C_MASK1 + P])
                dve.tensor_copy(mask2[:], cst[:, C_MASK2:C_MASK2 + P])
                dve.tensor_copy(tri_b[:], cst[:, C_TRI:C_TRI + P]).then_inc(s_conv, 1)
                dve.wait_ge(s_memset, 2)

                def pre(h, par, t, k):
                    tile, u = (h * 2 + par) * TILES + t, t % 2
                    psp, _ = banks(h, par, t)
                    if k == 0:
                        dve.wait_ge(s_x[t], 16 * (h * 2 + par + 1))
                        dve.bn_stats(stat[u][:], xin[:, t, :]).then_inc(s_stat, 1)
                        dve.wait_ge(s_stat, tile + 1)
                        dve.sem_inc(waits_met)
                        dve.bn_aggr(mv[u][:], stat[u][:]).then_inc(s_ln1, 1)
                    if k == 1:
                        dve.wait_ge(s_rstd1, tile + 1)
                        dve.wait_ge(s_ln1, tile + 1)
                        dve.wait_ge(s_xnT_ps, held(tile - 1))
                        dve.tensor_scalar(xn[u][:], xin[:, t, :], mv[u][:, 0:1], rstd[u][:], ALU.subtract,
                                          ALU.mult).then_inc(s_xn, 1)
                    if k == 3:
                        dve.wait_ge(s_qkv_ps, tile + 1)
                        dve.wait_ge(s_rot, held(tile - 1))
                        dve.wait_ge(s_v, held(tile - 1))
                        dve.tensor_tensor(qkv[u][:], psp[:, 1, 0:QKV_D], cst[:, C_BQKV:C_BQKV + QKV_D],
                                          ALU.add).then_inc(s_qkv, 1)
                    if k == 4:
                        dve.wait_ge(s_qkv, tile + 1)
                        dve.wait_ge(s_hi, held(tile - 1))
                        dve.tensor_tensor(rope[u][:], qkv[u][:, 0:QK_D].rearrange("p (n a d) -> p n a d", a=2, d=8),
                                          cst[:, C_COS + 8 * t:C_COS + 8 * t + 8].unsqueeze(1).unsqueeze(1)
                                          .to_broadcast([P, QK_D // 16, 2, 8]), ALU.mult).then_inc(s_cosd, 1)
                    if k == 6:
                        dve.wait_ge(s_cosd, tile + 1)
                        dve.wait_ge(s_rot, tile + 1)
                        dve.tensor_tensor(rope[u][:], rope[u][:], rot[u][:], ALU.add).then_inc(s_rope, 1)
                    if k == 8:
                        dve.wait_ge(s_hi, tile + 1)
                        flat = rope[u][:].rearrange("p n a d -> p (n a d)")
                        dve.tensor_tensor(qs[u][:, :, 2, :], flat[:, 0:D].rearrange("p (n d) -> p n d", d=32),
                                          qs[u][:, :, 0, :], ALU.subtract)
                        kf = flat[:, D:QK_D].rearrange("p (g d) -> p g d", d=HEAD_D)
                        for ab in range(2):
                            c = slice(16 * ab, 16 * ab + 16)
                            last = dve.tensor_tensor(ks[:, :, ab, 1, c], kf, ks[:, :, ab, 0, c], ALU.subtract)
                        last.then_inc(s_lo, 1)

                def main(now, one, two, s):
                    if not now:
                        return
                    h, par, p = now
                    U, u = (h * 2 + par) * PAIRS_OF_HEADS + p, p % 2

                    def largest(tile, bank, at, n, heads):
                        src = ps1[:, bank, at:at + n]
                        if len(heads) == 2:
                            src = src.rearrange("p (a n) -> p a n", a=2)
                        return dve.tensor_reduce(nmax[u][:, tile, heads[0]:heads[-1] + 1], src, AX.X, ALU.max,
                                                 negate=True)

                    dve.wait_ge(s_s1, 5 * U + s + 1)
                    if s < 2:
                        largest(3, s, 0, 512, [s]).then_inc(s_red, 1)
                    elif s < 4:
                        largest(2, 3 - s, 0, 384, [s - 2])
                        largest(0, 3 - s, 384, 128, [s - 2]).then_inc(s_red, 1)
                    else:
                        largest(1, 1, 0, 512, [0, 1]).then_inc(s_red, 1)
                        dve.wait_ge(s_red, 5 * U + 5)
                        dve.wait_ge(s_m_ps, held(U - 1))
                        dve.tensor_copy(mt[u][:, :, 96:98], nmax[u][:]).then_inc(s_mhi, 1)
                        dve.wait_ge(s_mhi, U + 1)
                        dve.tensor_tensor(mt[u][:, :, 98:100], nmax[u][:], mt[u][:, :, 96:98],
                                          ALU.subtract).then_inc(s_msplit, 1)

                def post(h, par, t, k):
                    b = h * 2 + par
                    tile, u = b * TILES + t, t % 2
                    if k == 0:
                        dve.wait_ge(s_o_ps, tile + 1)
                        heads = psq[:].rearrange("p (n d) -> p n d", d=32)
                        dve.reciprocal(rden[u][:], heads[:, :, HEAD_D]).then_inc(s_rden, 1)
                        dve.wait_ge(s_rden, tile + 1)
                        dve.wait_ge(s_yT_ps, held(tile - 1))
                        dve.tensor_tensor(yb[u][:].rearrange("p (n d) -> p n d", d=HEAD_D), heads[:, :, 0:HEAD_D],
                                          rden[u][:].unsqueeze(2).to_broadcast([P, HEADS, HEAD_D]),
                                          ALU.mult).then_inc(s_y, 1)
                    if k == 2:
                        dve.wait_ge(s_att_ps, tile + 1)
                        dve.wait_ge(s_xb, tile + 1)
                        dve.wait_ge(s_x2out[u], held(16 * (b * 2 + t // 2)))
                        dve.tensor_tensor(x2[u][:, 0:D], psq[:, 0:D], xb[u][:], ALU.add).then_inc(s_x2, 1)
                        dve.wait_ge(s_x2, tile + 1)
                        dve.bn_stats(stat2[u][:], x2[u][:, 0:D]).then_inc(s_stat2, 1)
                        dve.wait_ge(s_stat2, tile + 1)
                        dve.sem_inc(waits_met)
                        dve.bn_aggr(mv2[u][:], stat2[u][:]).then_inc(s_ln2, 1)
                    if k == 4:
                        dve.wait_ge(s_rstd2, tile + 1)
                        dve.wait_ge(s_ln2, tile + 1)
                        if t == 0:
                            dve.wait_ge(s_scat[par], held(16 * TILES * TOP * h))
                        dve.tensor_scalar(pay[par][:, t, 0:D], x2[u][:, 0:D], mv2[u][:, 0:1], rstd2[u][:],
                                          ALU.subtract, ALU.mult).then_inc(s_x2n, 1)
                    if k == 7:
                        dve.wait_ge(s_pre, tile + 1)
                        dve.wait_ge(s_rw, held(b))
                        dve.sem_inc(waits_met)
                        dve.max(topv[:, t, :], logit[par][:, t, :]).then_inc(s_left, 1)
                        dve.wait_ge(s_left, tile + 1)
                        dve.sem_inc(waits_met)
                        dve.max_index(topi[:, t, :], topv[:, t, :], logit[par][:, t, :])
                        dve.match_replace(left[:, t, :], topv[:, t, :], logit[par][:, t, :], -3e38).then_inc(s_top, 1)
                        dve.wait_ge(s_top, tile + 1)
                        dve.tensor_tensor(chosen[:, t, :], left[:, t, :], logit[par][:, t, :],
                                          ALU.not_equal).then_inc(s_chosen, 1)

                def route(h, par, k):
                    b = h * 2 + par
                    if k == 1:
                        dve.wait_ge(s_cnt_ps, b + 1)
                        dve.tensor_tensor(col[:, 4:5], psq[0:EXPERTS, 0:1], col[:, 0:1], ALU.add).then_inc(s_cnt, 1)
                    if k == 2:
                        dve.wait_ge(s_etop, b + 1)
                        dve.tensor_reduce(esum[:].rearrange("p t a -> p (t a)"), etop[:], AX.X,
                                          ALU.add).then_inc(s_esum, 1)
                        dve.wait_ge(s_esum, b + 1)
                        dve.reciprocal(erec[:], esum[:]).then_inc(s_erec, 1)
                    if k == 4:
                        dve.wait_ge(s_base_ps, b + 1)
                        dve.tensor_tensor(col[:, 8:9], psq[0:EXPERTS, 0:1], col[:, 3:4], ALU.add).then_inc(s_tk, 1)
                        dve.wait_ge(s_tk, 4 * b + 1)
                        dve.tensor_tensor(col[:, 3:4], psq[0:EXPERTS, 1:2], col[:, 3:4], ALU.add).then_inc(s_base, 1)
                    if k == 8:
                        dve.wait_ge(s_pool, 12 * b + 8)
                        blk = cst[0:EXPERTS, C_BLK:C_BLK + BLOCKS]
                        dve.scalar_tensor_tensor(out=taken[:], in0=blk, scalar=col[:, 8:9], in1=taken[:],
                                                 op0=ALU.is_ge, op1=ALU.subtract).then_inc(s_tk, 1)
                        dve.wait_ge(s_tk, 4 * b + 2)
                        dve.scalar_tensor_tensor(out=taken[:], in0=blk, scalar=col[:, 9:10], in1=taken[:],
                                                 op0=ALU.is_ge, op1=ALU.subtract).then_inc(s_tk, 2)
                    if k == 9:
                        dve.wait_ge(s_thd, b + 1)
                        rank = psq[:, 0:TILES * EXPERTS].rearrange("p (t e) -> p t e", e=EXPERTS)
                        wide = lambda a: thd[:, a, :].unsqueeze(1).to_broadcast([P, TILES, EXPERTS])
                        dve.tensor_tensor(place[:], rank, wide(0), ALU.is_ge).then_inc(s_pl, 1)
                        dve.wait_ge(s_pl, 4 * b + 1)
                        dve.tensor_tensor(place[:], place[:], wide(1), ALU.mult).then_inc(s_pl, 1)
                        dve.wait_ge(s_pl, 4 * b + 2)
                        dve.tensor_tensor(place[:], rank, place[:], ALU.add).then_inc(s_pl, 1)
                        dve.wait_ge(s_pl, 4 * b + 3)
                        dve.tensor_tensor(place[:], place[:], chosen[:], ALU.mult).then_inc(s_pl, 1)
                    if k == 10:
                        dve.wait_ge(s_pl, 4 * b + 4)
                        dve.sem_inc(waits_met)
                        for t in range(TILES):
                            last = dve.max(slot_f[:, t, :], place[:, t, :])
                        last.then_inc(s_slot, 1)

                program(dve, {"pre": pre, "main": main, "post": post, "route": route})

        with ExitStack() as ctx:
            sb = lambda n, s, d: ctx.enter_context(nc.sbuf_tensor(n, s, d))
            ps = lambda n, s: ctx.enter_context(nc.psum_tensor(n, s, F32))
            wdp_s = sb("wdp_s", [P, EXPERTS * D], F32)
            owner = sb("owner", [P, BLOCKS], F32)
            digits = sb("digits", [1, BLOCKS // 4, 4], F32)
            words_f = sb("words_f", [1, BLOCKS // 4], F32)
            words = sb("words", [1, BLOCKS // 4], I32)
            pidx_neg = sb("pidx_neg", [EXPERTS, P], F32)
            G, R = 16, 4
            xg = sb("xg", [P, G, ROW], F32)
            xT = sb("xT", [P, 2, KC, P], F32)
            sg = sb("sg", [P, 2, INNER], F32)
            inner = sb("inner", [P, 2, P], F32)
            innerT = sb("innerT", [P, 2, P], F32)
            y = sb("y", [P, G, D], F32)
            hit = sb("hit", [P, G // R, R, TOP], F32)
            hits = sb("hits", [P, G // R, R, 2, TOP], F32)
            picked = sb("picked", [P, G // R, R, 2], F32)
            dst_i = sb("dst_i", [P, G], I32)
            psA = ps("psA", [P, 2, SEQ])
            psB = ps("psB", [P, 2, SEQ])
            psC = ps("psC", [P, 2, SEQ])
            psD = ps("psD", [P, 2, SEQ])
            (e_wdp, e_zero_dve, e_zero, e_neg, e_own_ps, e_own, e_words, e_a_ps, e_a, e_b_ps, e_sg, e_in,
             e_c_ps, e_c, e_d_ps, e_d,
             e_hit, e_hits, e_pick, e_dst) = [sem(n) for n in (
                 "down_weights_in zeros_dve zeros pidx_negated owner_psum owner_ready words_ready xgT_psum xgT_ready "
                 "gu_psum silu_ready "
                 "inner_ready innerT_psum innerT_ready down_psum yrow_ready hit_ready hits_ready picked_ready "
                 "dst_ready").split()]
            e_x = [sem(f"xg_in{k}") for k in range(G)]
            e_out = [sem(f"y_out{k}") for k in range(G)]
            ROUNDS, TURN = BLOCKS // G, 3
            block = ctx.enter_context(nc.Block())

            def rounds(eng, *stages):
                def blocks(n, ks):
                    for k in ks:
                        for behind, stage in stages:
                            back = k < behind
                            if (isinstance(n, int) and not 0 <= n * G + k - behind < BLOCKS
                                    and stage.__name__ != "load_offsets"):
                                continue
                            stage(n - 1 if back else n, (k - behind) % G)

                blocks(0, range(G))
                blocks(1, range(G))
                with eng.Fori(0, (ROUNDS - 2) // TURN) as turn:
                    for r in range(TURN):
                        blocks(turn * TURN + (2 + r), range(G))
                blocks(ROUNDS, range(max(behind for behind, _ in stages)))

            @block.sync
            def _(sp):
                rows_v = rows_d.rearrange("(j p) r -> j p r", p=P)

                def load(n, k):
                    if isinstance(n, int) and n == 0 and k == 4:
                        sp.dma_start(wdp_s[0:INNER, :], wdp).then_inc(e_wdp, 16)
                    j = n * G + k
                    sp.wait_ge(e_a_ps, held(j - G + 1))
                    sp.wait_ge(e_in, held(j - G + 1))
                    sp.dma_start(xg[:, k, :], rows_v[bass.ds(j, 1)].rearrange("a p r -> p (a r)")
                                 ).then_inc(e_x[k], 16)

                rounds(sp, (0, load))

            @block.vector
            def _(dve):
                dve.tensor_scalar(pidx_neg[:], cst[0:EXPERTS, C_PIDX:C_PIDX + P], -1.0, None,
                                  ALU.mult).then_inc(e_neg, 1)
                dve.wait_ge(e_own_ps, 1)
                dve.tensor_copy(owner[:], psA[:, 0, 0:BLOCKS]).then_inc(e_own, 1)
                dve.wait_ge(e_own, 1)
                dve.tensor_tensor(digits[:], owner[0:1, :].rearrange("o (w r) -> o w r", r=4),
                                  cst[0:1, C_DIGIT:C_END].unsqueeze(1).to_broadcast([1, BLOCKS // 4, 4]),
                                  ALU.mult).then_inc(e_words, 1)
                dve.wait_ge(e_words, 1)
                dve.tensor_reduce(words_f[:], digits[:], AX.X, ALU.add).then_inc(e_words, 1)
                dve.wait_ge(e_words, 2)
                dve.tensor_copy(words[:], words_f[:]).then_inc(e_words, 1)
                dve.memset(wdp_s[INNER:P, EXPERTS * D // 2:EXPERTS * D], 0.0).then_inc(e_zero_dve, 1)
                dve.wait_ge(e_zero, 1)

                def pick(n, k):
                    if k % R != 0:
                        return
                    j, m = n * G + k, k // R
                    q = n * (G // R) + m
                    for r in range(R):
                        dve.wait_ge(e_x[k + r], 16 * (n + 1))
                    own = owner[:, bass.ds(j, R)].unsqueeze(2).to_broadcast([P, R, TOP])
                    dve.tensor_tensor(hit[:, m], xg[:, k:k + R, C_IDX:C_IDX + TOP], own,
                                      ALU.is_equal).then_inc(e_hit, 1)
                    dve.wait_ge(e_hit, q + 1)
                    dve.tensor_tensor(hits[:, m], xg[:, k:k + R, C_RW:C_RW + 2 * TOP].rearrange(
                        "p r (a k) -> p r a k", a=2), hit[:, m].unsqueeze(2).to_broadcast([P, R, 2, TOP]),
                        ALU.mult).then_inc(e_hits, 1)
                    dve.wait_ge(e_hits, q + 1)
                    dve.tensor_reduce(picked[:, m], hits[:, m], AX.X, ALU.add).then_inc(e_pick, 1)

                def destine(n, k):
                    if k % R != 0:
                        return
                    m = k // R
                    dve.wait_ge(e_pick, n * (G // R) + m + 1)
                    for r in range(R):
                        dve.wait_ge(e_out[k + r], 16 * n)
                    dve.tensor_scalar(dst_i[:, k:k + R], picked[:, m, :, 1], SKIP, None, ALU.add).then_inc(e_dst, 1)

                def gated(n, k):
                    j = n * G + k
                    dve.wait_ge(e_sg, j + 1)
                    dve.wait_ge(e_pick, n * (G // R) + k // R + 1)
                    dve.wait_ge(e_c_ps, held(j - 1))
                    dve.scalar_tensor_tensor(out=inner[:, k % 2, 0:INNER], in0=sg[:, k % 2, :],
                                             scalar=picked[:, k // R, k % R, 0:1], in1=psB[:, k % 2, INNER:GU],
                                             op0=ALU.mult, op1=ALU.mult).then_inc(e_in, 1)

                def innerT_copy(n, k):
                    j = n * G + k
                    dve.wait_ge(e_c_ps, j + 1)
                    dve.wait_ge(e_d_ps, held(j - 1))
                    dve.tensor_copy(innerT[:, k % 2, :], psC[:, k % 2, 0:P]).then_inc(e_c, 1)

                rounds(dve, (2, innerT_copy), (1, gated), (3, destine), (0, pick))

            @block.scalar
            def _(act):
                def xT_copy(n, k):
                    j = n * G + k
                    act.wait_ge(e_a_ps, j + 1)
                    act.wait_ge(e_b_ps, held(j - 1))
                    act.copy(xT[:, k % 2], psA[:, k % 2, 0:D].rearrange("p (k n) -> p k n", k=KC)).then_inc(e_a, 1)

                def silu(n, k):
                    j = n * G + k
                    act.wait_ge(e_b_ps, j + 1)
                    act.wait_ge(e_in, held(j - 1))
                    act.activation(sg[:, k % 2, :], psB[:, k % 2, 0:INNER], ACT.Silu).then_inc(e_sg, 1)

                def y_copy(n, k):
                    j = n * G + k
                    act.wait_ge(e_d_ps, j + 1)
                    act.wait_ge(e_out[k], 16 * n)
                    act.copy(y[:, k, :], psD[:, k % 2, 0:D]).then_inc(e_d, 1)

                rounds(act, (0, xT_copy), (1, silu), (3, y_copy))

            @block.tensor
            def _(pe):
                pe.wait_ge(e_neg, 1)
                pe.matmul(psA[:, 0, 0:BLOCKS], pidx_neg[:], taken[:], start=True, stop=True).then_inc(e_own_ps, 1)
                pe.wait_ge(e_words, 3)
                pe.wait_ge(e_w, 16 * 2 * TILES)

                offsets = {}

                def load_offsets(n, k):
                    if k == 0:
                        first = -1 if not isinstance(n, int) or n > 0 else 0
                        count = (0 if isinstance(n, int) and n == ROUNDS else G // 4) - first
                        _, values = nc.values_load_multi_w_load_instructions(
                            words[0:1, bass.ds(n * (G // R) + first, count)], engines=(mybir.EngineType.PE,),
                            min_val=0, max_val=EXPERTS ** 4 - 1)
                        for w in range(count):
                            for r in range(4):
                                at = 6 * r - 8
                                offsets[4 * (first + w) + r] = (
                                    (values[w] >> at) & ((EXPERTS - 1) * D) if at > 0 else
                                    (values[w] & ((EXPERTS - 1) << 6 * r)) * (1 << -at))

                def turn_x(n, k):
                    j = n * G + k
                    pe.wait_ge(e_x[k], 16 * (n + 1))
                    pe.wait_ge(e_a, held(j - 1))
                    for c in range(KC):
                        last = pe.transpose(psA[:, k % 2, c * P:(c + 1) * P], xg[:, k, c * P:(c + 1) * P], ident)
                    last.then_inc(e_a_ps, 1)

                def gate_up(n, k):
                    j = n * G + k
                    off = offsets[k - G if k >= G - 1 else k]
                    pe.wait_ge(e_a, j + 1)
                    pe.wait_ge(e_in, held(j - 1))
                    for c in range(KC):
                        last = pe.matmul(psB[:, k % 2, 0:GU], xT[:, k % 2, c, :], wgu_s[:, bass.ds(off + c * GU, GU)],
                                         start=(c == 0), stop=(c == KC - 1))
                    last.then_inc(e_b_ps, 1)

                def turn_inner(n, k):
                    j = n * G + k
                    pe.wait_ge(e_in, j + 1)
                    pe.wait_ge(e_c, held(j - 1))
                    pe.transpose(psC[:, k % 2, 0:P], inner[:, k % 2, :], ident).then_inc(e_c_ps, 1)

                def down(n, k):
                    j = n * G + k
                    off = offsets[k - G if k >= G - 3 else k]
                    if isinstance(n, int) and j == 0:
                        pe.wait_ge(e_wdp, 16)
                        pe.wait_ge(e_zero, 2)
                        pe.wait_ge(e_zero_dve, 1)
                    pe.wait_ge(e_c, j + 1)
                    pe.wait_ge(e_d, held(j - 1))
                    pe.matmul(psD[:, k % 2, 0:D], innerT[:, k % 2, :], wdp_s[:, bass.ds(off, D)],
                              start=True, stop=True).then_inc(e_d_ps, 1)

                rounds(pe, (0, load_offsets), (0, turn_x), (1, gate_up), (2, turn_inner), (3, down))

            @block.gpsimd
            def _(pool):
                pool.memset(inner[:], 0.0).then_inc(e_zero, 1)
                pool.wait_ge(e_zero, 1)
                pool.memset(wdp_s[INNER:P, 0:EXPERTS * D // 2], 0.0).then_inc(e_zero, 1)

                def scatter(n, k):
                    j = n * G + k
                    pool.wait_ge(e_dst, n * (G // R) + k // R + 1)
                    pool.wait_ge(e_d, j + 1)
                    pool.sem_inc(waits_met)
                    pool.indirect_dma_start(
                        res_d, bass.IndirectOffsetOnAxis(ap=dst_i[:, k:k + 1], axis=0), y[:, k, :], None,
                        bounds_check=ROUTED - 1, oob_is_err=False).then_inc(e_out[k], 16)

                rounds(pool, (0, scatter))
                for k in range(G):
                    pool.wait_ge(e_out[k], 16 * ROUNDS)

        with ExitStack() as ctx:
            sb = lambda n, s, d: ctx.enter_context(nc.sbuf_tensor(n, s, d))
            ps = lambda n, s: ctx.enter_context(nc.psum_tensor(n, s, F32))
            R = 4
            yk = sb("yk", [P, R, TOP, D], F32)
            xs = sb("xs", [P, R, D + SHARED], F32)
            sig = sb("sig", [P, 2, INNER + 1], F32)
            prod = sb("prod", [P, 2, INNER], F32)
            sh = sb("sh", [P, 2, P], F32)
            shT = sb("shT", [P, 2, P], F32)
            acc = sb("acc", [P, 2, D], F32)
            fin = sb("fin", [P, 2, D], F32)
            psS = ps("psS", [P, 2, SEQ])
            psY = ps("psY", [P, 2, SEQ])
            ON_PE = 2
            (c_zero, c_sig, c_prod, c_sh, c_t_ps, c_t, c_y_ps, c_acc, c_fin) = [sem(n) for n in (
                "zero_padding sigmoid_ready product_ready sh_ready shT_psum shT_ready added_psum sum_ready "
                "fin_ready").split()]
            c_in = [sem(f"yk_in{k}") for k in range(R)]
            c_out = [sem(f"fin_out{k}") for k in range(2)]
            block = ctx.enter_context(nc.Block())

            def tiles(eng, *stages):
                def some(n, ks):
                    for k in ks:
                        for behind, stage in stages:
                            if not isinstance(n, int) or 0 <= n * R + k - behind < ALL_TILES:
                                stage(n - 1 if k < behind else n, (k - behind) % R)

                some(0, range(R))
                with eng.Fori(1, ALL_TILES // R) as n:
                    some(n, range(R))
                some(ALL_TILES // R, range(max(behind for behind, _ in stages)))

            @block.sync
            def _(sp):
                res_v = res_d.rearrange("(t p k) h -> t p k h", p=P, k=TOP)

                def load(n, k):
                    j = n * R + k
                    sp.wait_ge(c_acc, held(j - R + 1))
                    sp.wait_ge(c_y_ps, held(j - R + 1))
                    sp.dma_start(yk[:, k], res_v[bass.ds(j, 1)].rearrange("a p k h -> p (a k) h")
                                 ).then_inc(c_in[k], 16)
                    sp.dma_start(xs[:, k], x2_v[bass.ds(j, 1)].rearrange("a p h -> p (a h)")
                                 ).then_inc(c_in[k], 16)

                tiles(sp, (0, load))

            @block.gpsimd
            def _(pool):
                pool.memset(sh[:], 0.0).then_inc(c_zero, 1)
                pool.wait_ge(c_zero, 1)
                pool.memset(shT[:], 0.0).then_inc(c_zero, 1)

            @block.scalar
            def _(act):
                out_v = out.rearrange("b (t p) h -> (b t) p h", p=P)

                def sigmoid(n, k):
                    j = n * R + k
                    act.wait_ge(c_in[k], 32 * (n + 1))
                    act.wait_ge(c_sh, held(j - 1))
                    act.activation(sig[:, k % 2, :], xs[:, k, D:D + INNER + 1], ACT.Sigmoid).then_inc(c_sig, 1)

                def shT_copy(n, k):
                    j = n * R + k
                    act.wait_ge(c_t_ps, j + 1)
                    act.wait_ge(c_y_ps, held(j - 1))
                    act.copy(shT[:, k % 2, :], psS[:, k % 2, 0:P]).then_inc(c_t, 1)

                def store(n, k):
                    j = n * R + k
                    act.wait_ge(c_fin, j + 1)
                    act.dma_start(out_v[bass.ds(j, 1)].rearrange("a p h -> p (a h)"), fin[:, k % 2, :]
                                  ).then_inc(c_out[k % 2], 16)

                tiles(act, (0, sigmoid), (1, shT_copy), (3, store))
                for k in range(2):
                    act.wait_ge(c_out[k], 16 * ALL_TILES // 2)

            @block.tensor
            def _(pe):
                pe.wait_ge(c_zero, 2)

                def turn(n, k):
                    j = n * R + k
                    pe.wait_ge(c_sh, j + 1)
                    pe.wait_ge(c_t, held(j - 1))
                    pe.transpose(psS[:, k % 2, 0:P], sh[:, k % 2, :], ident).then_inc(c_t_ps, 1)

                def add(n, k):
                    j = n * R + k
                    pe.wait_ge(c_in[k], 32 * (n + 1))
                    pe.wait_ge(c_fin, held(j - 1))
                    at = psY[:, k % 2, 0:D]
                    pe.matmul(at, ident, xs[:, k, 0:D], start=True, stop=False)
                    for c in range(ON_PE):
                        pe.matmul(at, ident, yk[:, k, c, :], start=False, stop=False)
                    pe.wait_ge(c_t, j + 1)
                    pe.matmul(at, shT[:, k % 2, :], shd_w[:], start=False, stop=True).then_inc(c_y_ps, 1)

                tiles(pe, (1, turn), (2, add))

            @block.vector
            def _(dve):
                dve.wait_ge(c_zero, 2)

                def gated(n, k):
                    j = n * R + k
                    dve.wait_ge(c_in[k], 32 * (n + 1))
                    dve.tensor_tensor(prod[:, k % 2, :], xs[:, k, D:D + INNER], xs[:, k, D + INNER + 1:D + SHARED],
                                      ALU.mult).then_inc(c_prod, 1)
                    dve.wait_ge(c_prod, j + 1)
                    dve.wait_ge(c_sig, j + 1)
                    dve.wait_ge(c_t_ps, held(j - 1))
                    dve.scalar_tensor_tensor(out=sh[:, k % 2, 0:INNER], in0=sig[:, k % 2, 0:INNER],
                                             scalar=sig[:, k % 2, INNER:INNER + 1], in1=prod[:, k % 2, :],
                                             op0=ALU.mult, op1=ALU.mult).then_inc(c_sh, 1)

                def total(n, k):
                    dve.wait_ge(c_in[k], 32 * (n + 1))
                    dve.tensor_reduce(acc[:, k % 2, :], yk[:, k, ON_PE:TOP].rearrange("p k h -> p h k"), AX.X,
                                      ALU.add).then_inc(c_acc, 1)

                def finish(n, k):
                    j = n * R + k
                    dve.wait_ge(c_acc, j + 1)
                    dve.wait_ge(c_y_ps, j + 1)
                    dve.wait_ge(c_out[k % 2], held(16 * (n * 2 + k // 2)))
                    dve.tensor_tensor(fin[:, k % 2, :], psY[:, k % 2, 0:D], acc[:, k % 2, :], ALU.add
                                      ).then_inc(c_fin, 1)

                tiles(dve, (0, gated), (2, finish), (1, total))


def constants():
    c = np.zeros((P, C_END), np.float32)
    p = np.arange(P)
    c[:, C_IDENT:C_IDENT + P] = np.eye(P)
    c[:, C_MASK1:C_MASK1 + P] = np.where(p[None, :] > p[:, None], MASKED, 0.0)
    c[:, C_MASK2:C_MASK2 + P] = np.where(p[:, None] > p[None, :], MASKED, 0.0)
    c[:, C_TRI:C_TRI + P] = p[:, None] < p[None, :]
    c[:, C_PIDX:C_PIDX + P] = p[:, None]
    i = np.arange(1, HEAD_D // 2 + 1, dtype=np.float32)
    thetas = np.float32(10000.0) ** (np.float32(-2.0) * (i - np.float32(1.0)) / np.float32(HEAD_D))
    ang = np.arange(1, SEQ + 1, dtype=np.float32)[:, None] * thetas.astype(np.float32)
    for at, table in ((C_COS, np.cos(ang)), (C_SIN, np.sin(ang)), (C_NSIN, -np.sin(ang))):
        c[:, at:at + TILES * 8] = table.astype(np.float32).reshape(TILES, P, 8).transpose(1, 0, 2).reshape(P, -1)
    c[:, C_BLK:C_BLK + BLOCKS] = P * np.arange(BLOCKS)
    token = np.arange(ALL_TILES)[None, :, None] * P + p[:, None, None]
    c[:, C_DIGIT:C_END] = float(EXPERTS) ** np.arange(4)
    c[:, C_DSTC:C_DIGIT] = (token * TOP + np.arange(TOP) - SKIP).reshape(P, -1)
    return c


def kernel(**inputs):
    import concourse.bacc as _bacc
    from concourse.bass_utils import run_bass_kernel_spmd as _run

    a = {k.replace("L0_", ""): np.asarray(v) for k, v in inputs.items()}

    def rows(w):
        return np.ascontiguousarray(w.T.reshape(KC, P, -1).transpose(1, 0, 2))

    const = constants()
    const[:, C_BQKV:C_BQKV + QKV_D] = np.concatenate([a["attn_bq"], a["attn_bk"], a["attn_bv"]])[None, :]
    const[:, C_BO:C_BO + D] = a["attn_bo"][None, :]
    arrays = {
        "x_in": a["attn_x"],
        "const_in_d": const,
        "wqkv_in": rows(np.concatenate([a["attn_Wq"], a["attn_Wk"], a["attn_Wv"]])),
        "wo_in": rows(a["attn_Wo"]),
        "wroute_in": rows(np.concatenate([a["ffn_gate_w"], a["ffn_sh_gate_w"], a["ffn_sh_gate1_w"],
                                          a["ffn_sh_up_w"]])),
        "wgu_in": np.ascontiguousarray(
            a["ffn_gu_w"].reshape(EXPERTS, GU, KC, P).transpose(3, 0, 2, 1).reshape(P, -1)),
        "wdp_in": np.ascontiguousarray(a["ffn_dp_w"].transpose(2, 0, 1).reshape(INNER, -1)),
        "wshd_in": np.ascontiguousarray(a["ffn_sh_down_w"].T),
    }
    nc = _bacc.Bacc("TRN2", target_bir_lowering=False, num_devices=1)
    args = []
    for name, v in arrays.items():
        arrays[name] = np.ascontiguousarray(v)
        args.append(nc.dram_tensor(name, v.shape, mybir.dt.from_np(v.dtype), kind="ExternalInput").ap())
    args.append(nc.dram_tensor("out_d", (BATCH, SEQ, D), F32, kind="ExternalOutput").ap())
    build(nc, *args)
    r = _run(nc, [arrays], core_ids=[0])
    return r.results[0]["out_d"]
```
